# Optimizing a Trainium2 kernel written in Bass

```python
import numpy as np
import jax
import jax.numpy as jnp

def _softmax(x, axis=-1):
    return jax.nn.softmax(x, axis=axis)

def _gelu(x):
    return jax.nn.gelu(x, approximate=True)

def _silu(x):
    return jax.nn.silu(x)

def _sigmoid(x):
    return jax.nn.sigmoid(x)

def _layernorm(x, axis=-1, eps=1e-05):
    m = jnp.mean(x, axis=axis, keepdims=True)
    v = jnp.var(x, axis=axis, keepdims=True)
    return (x - m) / jnp.sqrt(v + eps)

def _scatter_add(tgt, idx, src, axis=0):
    return tgt.at[idx].add(src)

def _segment_sum(src, seg, n):
    return jax.ops.segment_sum(src, seg, n)
kernel_name = 'mk_gps_d1_gnn_r8_47212f'

def setup_inputs(seed: int=0):
    np.random.seed(seed)
    _w = jnp.asarray

    def _rec_inputs():
        import jax
        import jax.numpy as jnp
        _gk = jax.random.key(seed)
        x = -0.0002117 + 1 * jax.random.normal(jax.random.fold_in(_gk, 1), (1250, 1024), jnp.float32)
        src = jax.random.randint(jax.random.fold_in(_gk, 2), (20000,), 0, 1250, jnp.int32)
        dst = jnp.minimum((1250 * jax.random.uniform(jax.random.fold_in(_gk, 3), (20000,)) ** 2.0).astype(jnp.int32), 9999)
        _o = jnp.argsort(dst, stable=True)
        src = src[_o]
        dst = dst[_o]
        return (x, src, dst)
    x, src, dst = _rec_inputs()

    def _L0_gnn_setup():
        import jax, jax.numpy as jnp
        import numpy as np
        N_NODES = 3125
        N_EDGES = 50000
        D = 1024

        def _sage_layer(h, edge_src, edge_dst, deg_inv, W_self, W_neigh, b):
            msg = h[edge_src]
            agg = jax.ops.segment_sum(msg, edge_dst, num_segments=h.shape[0])
            mean = agg * deg_inv[:, None]
            return h @ W_self + mean @ W_neigh + b
        key = jax.random.key(seed)
        ks = jax.random.split(key, 8)
        s = 1.0 / np.sqrt(D)
        return {'x': jax.random.normal(ks[0], (N_NODES, D), dtype=jnp.float32), 'edge_src': jax.random.randint(ks[1], (N_EDGES,), 0, N_NODES, dtype=jnp.int32), 'edge_dst': jax.random.randint(ks[2], (N_EDGES,), 0, N_NODES, dtype=jnp.int32), 'W_self0': jax.random.normal(ks[3], (D, D), dtype=jnp.float32) * s, 'W_neigh0': jax.random.normal(ks[4], (D, D), dtype=jnp.float32) * s, 'b0': jnp.zeros((D,), dtype=jnp.float32), 'W_self1': jax.random.normal(ks[5], (D, D), dtype=jnp.float32) * s, 'W_neigh1': jax.random.normal(ks[6], (D, D), dtype=jnp.float32) * s, 'b1': jnp.zeros((D,), dtype=jnp.float32)}
    _L0_gnn_all = _L0_gnn_setup()
    _L0_gnn_in = {k: v for k, v in _L0_gnn_all.items() if k in ('W_self0', 'W_neigh0', 'b0', 'W_self1', 'W_neigh1', 'b1')}
    del _L0_gnn_all

    def _L0_mix_setup():
        import jax, jax.numpy as jnp
        import numpy as np
        B, N, C, H, K = (4, 512, 1024, 16, 2)
        D = C // H

        def _kernel(x):
            return jax.nn.silu(x) + 0.5
        key = jax.random.key(seed)
        ks = jax.random.split(key, 8)
        s = 0.02
        x = jax.random.normal(ks[0], (B, N, C), jnp.float32)
        Wq = jax.random.normal(ks[1], (C, C), jnp.float32) * s
        bq = jnp.zeros((C,), jnp.float32)
        Wk = jax.random.normal(ks[2], (K, C, C), jnp.float32) * s
        bk = jnp.zeros((K, C), jnp.float32)
        Wv = jax.random.normal(ks[3], (K, C, C), jnp.float32) * s
        bv = jnp.zeros((K, C), jnp.float32)
        Wo = jax.random.normal(ks[4], (C, C), jnp.float32) * s
        bo = jnp.zeros((C,), jnp.float32)
        ln_g = jnp.ones((C,), jnp.float32)
        ln_b = jnp.zeros((C,), jnp.float32)
        return dict(x=x, Wq=Wq, bq=bq, Wk=Wk, bk=bk, Wv=Wv, bv=bv, Wo=Wo, bo=bo, ln_g=ln_g, ln_b=ln_b)
    _L0_mix_all = _L0_mix_setup()
    _L0_mix_in = {k: v for k, v in _L0_mix_all.items() if k in ('Wq', 'bq', 'Wk', 'bk', 'Wv', 'bv', 'Wo', 'bo', 'ln_g', 'ln_b')}
    del _L0_mix_all

    def _L0_ffn_setup():
        import jax, jax.numpy as jnp
        import numpy as np
        B, S, H = (8, 1024, 1024)
        FF = 512
        E = 8
        TOP_K = 2
        LN_EPS = 1e-12

        def _layernorm(x, w, b):
            mu = jnp.mean(x, axis=-1, keepdims=True)
            var = jnp.mean(jnp.square(x - mu), axis=-1, keepdims=True)
            return (x - mu) * jax.lax.rsqrt(var + LN_EPS) * w + b
        key = jax.random.key(seed)
        ks = jax.random.split(key, 8)
        sc_h = 1.0 / np.sqrt(H)
        sc_ff = 1.0 / np.sqrt(FF)
        return {'hidden_states': jax.random.normal(ks[0], (B, S, H), jnp.float32), 'router_w': jax.random.normal(ks[1], (E, H), jnp.float32) * sc_h, 'router_b': jnp.zeros((E,), jnp.float32), 'w1': jax.random.normal(ks[2], (E, FF, H), jnp.float32) * sc_h, 'b1': jax.random.normal(ks[3], (E, FF), jnp.float32) * 0.01, 'w2': jax.random.normal(ks[4], (E, H, FF), jnp.float32) * sc_ff, 'b2': jax.random.normal(ks[5], (E, H), jnp.float32) * 0.01, 'ln_w': jnp.ones((H,), jnp.float32), 'ln_b': jnp.zeros((H,), jnp.float32)}
    _L0_ffn_all = _L0_ffn_setup()
    _L0_ffn_in = {k: v for k, v in _L0_ffn_all.items() if k in ('router_w', 'router_b', 'w1', 'b1', 'w2', 'b2', 'ln_w', 'ln_b')}
    del _L0_ffn_all
    return {'x': x, 'src': src, 'dst': dst, 'L0_gnn_W_self0': _L0_gnn_in['W_self0'], 'L0_gnn_W_neigh0': _L0_gnn_in['W_neigh0'], 'L0_gnn_b0': _L0_gnn_in['b0'], 'L0_gnn_W_self1': _L0_gnn_in['W_self1'], 'L0_gnn_W_neigh1': _L0_gnn_in['W_neigh1'], 'L0_gnn_b1': _L0_gnn_in['b1'], 'L0_mix_Wq': _L0_mix_in['Wq'], 'L0_mix_bq': _L0_mix_in['bq'], 'L0_mix_Wk': _L0_mix_in['Wk'], 'L0_mix_bk': _L0_mix_in['bk'], 'L0_mix_Wv': _L0_mix_in['Wv'], 'L0_mix_bv': _L0_mix_in['bv'], 'L0_mix_Wo': _L0_mix_in['Wo'], 'L0_mix_bo': _L0_mix_in['bo'], 'L0_mix_ln_g': _L0_mix_in['ln_g'], 'L0_mix_ln_b': _L0_mix_in['ln_b'], 'L0_ffn_router_w': _L0_ffn_in['router_w'], 'L0_ffn_router_b': _L0_ffn_in['router_b'], 'L0_ffn_w1': _L0_ffn_in['w1'], 'L0_ffn_b1': _L0_ffn_in['b1'], 'L0_ffn_w2': _L0_ffn_in['w2'], 'L0_ffn_b2': _L0_ffn_in['b2'], 'L0_ffn_ln_w': _L0_ffn_in['ln_w'], 'L0_ffn_ln_b': _L0_ffn_in['ln_b']}

def reference(x, src, dst, L0_gnn_W_self0, L0_gnn_W_neigh0, L0_gnn_b0, L0_gnn_W_self1, L0_gnn_W_neigh1, L0_gnn_b1, L0_mix_Wq, L0_mix_bq, L0_mix_Wk, L0_mix_bk, L0_mix_Wv, L0_mix_bv, L0_mix_Wo, L0_mix_bo, L0_mix_ln_g, L0_mix_ln_b, L0_ffn_router_w, L0_ffn_router_b, L0_ffn_w1, L0_ffn_b1, L0_ffn_w2, L0_ffn_b2, L0_ffn_ln_w, L0_ffn_ln_b):
    import jax
    import jax.numpy as jnp

    def _L0_gnn_ref(x, edge_src, edge_dst, W_self0, W_neigh0, b0, W_self1, W_neigh1, b1):
        import jax, jax.numpy as jnp
        import numpy as np
        N_NODES = 3125
        N_EDGES = 50000
        D = 1024

        def _sage_layer(h, edge_src, edge_dst, deg_inv, W_self, W_neigh, b):
            msg = h[edge_src]
            agg = jax.ops.segment_sum(msg, edge_dst, num_segments=h.shape[0])
            mean = agg * deg_inv[:, None]
            return h @ W_self + mean @ W_neigh + b
        N = x.shape[0]
        deg = jax.ops.segment_sum(jnp.ones_like(edge_dst, dtype=x.dtype), edge_dst, num_segments=N)
        deg_inv = 1.0 / jnp.maximum(deg, 1.0)
        h = jax.nn.relu(_sage_layer(x, edge_src, edge_dst, deg_inv, W_self0, W_neigh0, b0))
        out = _sage_layer(h, edge_src, edge_dst, deg_inv, W_self1, W_neigh1, b1)
        return out

    def _L0_mix_ref(x, Wq, bq, Wk, bk, Wv, bv, Wo, bo, ln_g, ln_b):
        import jax, jax.numpy as jnp
        import numpy as np
        B, N, C, H, K = (4, 512, 1024, 16, 2)
        D = C // H

        def _kernel(x):
            return jax.nn.silu(x) + 0.5
        dtype = x.dtype
        Bn, Nn, Cn = x.shape
        q = x + x @ Wq.T + bq
        ks = x[None] + jnp.einsum('bnc,kdc->kbnd', x, Wk) + bk[:, None, None, :]
        vs = x[None] + jnp.einsum('bnc,kdc->kbnd', x, Wv) + bv[:, None, None, :]
        q = q.reshape(Bn, Nn, H, D).transpose(0, 2, 1, 3)
        ks = ks.reshape(K, Bn, Nn, H, D).transpose(0, 1, 3, 2, 4)
        vs = vs.reshape(K, Bn, Nn, H, D).transpose(0, 1, 3, 2, 4)
        q = _kernel(q)
        ks = _kernel(ks)
        q = q / (jnp.linalg.norm(q, axis=-1, keepdims=True) + 1e-06)
        ks = ks / (jnp.linalg.norm(ks, axis=-1, keepdims=True) + 1e-06)
        scale = Nn ** (-0.5)
        ks = ks.astype(jnp.float32) * scale
        vs = vs.astype(jnp.float32) * scale
        states = jnp.einsum('kbhnd,kbhne->kbhde', ks, vs)
        state = jnp.prod(states, axis=0)
        out = jnp.einsum('bhnd,bhde->bhne', q.astype(jnp.float32), state)
        out = out.astype(dtype)
        out = out.transpose(0, 2, 1, 3).reshape(Bn, Nn, Cn)
        mu = out.mean(axis=-1, keepdims=True)
        var = out.var(axis=-1, keepdims=True)
        out = (out - mu) * jax.lax.rsqrt(var + 1e-05) * ln_g + ln_b
        out = out @ Wo.T + bo
        return out

    def _L0_ffn_ref(hidden_states, router_w, router_b, w1, b1, w2, b2, ln_w, ln_b):
        import jax, jax.numpy as jnp
        import numpy as np
        B, S, H = (8, 1024, 1024)
        FF = 512
        E = 8
        TOP_K = 2
        LN_EPS = 1e-12

        def _layernorm(x, w, b):
            mu = jnp.mean(x, axis=-1, keepdims=True)
            var = jnp.mean(jnp.square(x - mu), axis=-1, keepdims=True)
            return (x - mu) * jax.lax.rsqrt(var + LN_EPS) * w + b
        b, s, h = hidden_states.shape
        flat = hidden_states.reshape(-1, h)
        logits = flat @ router_w.T + router_b
        topk_vals, topk_idx = jax.lax.top_k(logits, TOP_K)
        topk_w = jax.nn.softmax(topk_vals, axis=-1)
        out = jnp.zeros_like(flat)
        n_exp = w1.shape[0]
        for e in range(n_exp):
            cw = jnp.sum(jnp.where(topk_idx == e, topk_w, 0.0), axis=-1)
            y = jax.nn.gelu(flat @ w1[e].T + b1[e], approximate=False)
            y = y @ w2[e].T + b2[e]
            out = out + y * cw[:, None]
        out = out.reshape(b, s, h) + hidden_states
        return _layernorm(out, ln_w, ln_b)
    xn = _layernorm(x, axis=-1)
    x = x + _L0_gnn_ref(xn, src, dst, L0_gnn_W_self0, L0_gnn_W_neigh0, L0_gnn_b0, L0_gnn_W_self1, L0_gnn_W_neigh1, L0_gnn_b1) + _L0_mix_ref(xn[None], L0_mix_Wq, L0_mix_bq, L0_mix_Wk, L0_mix_bk, L0_mix_Wv, L0_mix_bv, L0_mix_Wo, L0_mix_bo, L0_mix_ln_g, L0_mix_ln_b)[0]
    x = x + _L0_ffn_ref(_layernorm(x, axis=-1)[None], L0_ffn_router_w, L0_ffn_router_b, L0_ffn_w1, L0_ffn_b1, L0_ffn_w2, L0_ffn_b2, L0_ffn_ln_w, L0_ffn_ln_b)[0]
    return x

_drawn_inputs = setup_inputs


def setup_inputs(seed=0):
    import zlib

    import numpy as np

    out = dict(_drawn_inputs(seed))
    spreads = {'L0_gnn_b0': (0.0, 0.1),
     'L0_gnn_b1': (0.0, 0.1),
     'L0_mix_bq': (0.0, 2.0),
     'L0_mix_bk': (0.0, 2.0),
     'L0_mix_bv': (0.0, 0.1),
     'L0_mix_bo': (0.0, 0.1),
     'L0_mix_ln_g': (1.0, 0.6),
     'L0_mix_ln_b': (0.0, 0.1),
     'L0_ffn_router_b': (0.0, 0.1),
     'L0_ffn_ln_w': (1.0, 0.2),
     'L0_ffn_ln_b': (0.0, 0.1)}
    factors = {'L0_mix_Wk': 69.744,
     'L0_ffn_b1': 27.96,
     'L0_ffn_b2': 8.0,
     'L0_mix_Wq': 15.381,
     'L0_mix_Wv': 2.776}
    for name, (base, spread) in spreads.items():
        noise = np.random.default_rng([zlib.crc32(name.encode()), seed]).standard_normal(out[name].shape)
        drawn = base * np.exp(spread * noise) if base else spread * noise
        out[name] = jnp.asarray(drawn.astype(out[name].dtype))
    for name, factor in factors.items():
        out[name] = (out[name] * factor).astype(out[name].dtype)
    return out
```

```python
from contextlib import ExitStack

import concourse.bass as bass
from concourse import mybir

ALU = mybir.AluOpType
ACT = mybir.ActivationFunctionType
F32 = mybir.dt.float32
F16 = mybir.dt.float16
I32 = mybir.dt.int32
U32 = mybir.dt.uint32
AX = mybir.AxisListType

P = 128
N = 1250
T = -(-N // P)
NP = T * P
LAST = N - (T - 1) * P
D = 1024
KC = D // P
HD = 64
HEADS = D // HD
E = 20000
EJ = 160
TG = 4
GROUPS = 50
SPP = GROUPS * TG
ROWS = P * SPP
EXPERTS = 8
FF = 512
BATCHES = 18
SW = 256.0
SX = 16.0
SS = 4096.0
COLS = [(0, 512), (512, 512), (1024, N - 1024)]
assert GROUPS >= E // (TG * P) + T and GROUPS == 5 * T

PLAIN = list(range(KC))
DIAG = [[4 * h + q + d * (4 if h == 0 else -4) for q in range(4) for d in (0, 1)] for h in (0, 1)]


def program(nc, x, edge_src, edge_dst, weights, rows, cols, b1col, router, router_b, b2, out):
    x_t = x.rearrange("(t p) d -> p t d", p=P)
    out_t = out.rearrange("(t p) d -> p t d", p=P)
    with ExitStack() as ctx:
        dram = lambda name, shape: nc.dram_tensor(name, shape, F32, kind="Internal").ap()
        bucket_rows = dram("bucket_rows", [ROWS + P * (EJ - E // P), 2])
        mixed = dram("mixed", [NP, D]).rearrange("(t p) d -> p t d", p=P)
        selfT = dram("selfT", [D, N]).rearrange("(o p) n -> p o n", p=P)
        x1_d = dram("x1", [NP, D]).rearrange("(t p) d -> p t d", p=P)
        y_d = dram("y", [NP, D]).rearrange("(t p) d -> p t d", p=P)

        top = [-(-nc.sbuf_base // 64) * 64]

        def region(nbytes):
            at = top[0]
            top[0] += -(-nbytes // 64) * 64
            return at

        def put(name, shape, dt, at):
            return nc.alloc_sbuf_tensor_at(name, shape, dt, offset=at)

        r1, r2 = region(4 * KC * NP), region(4 * KC * NP)
        r_adj = region(2 * T * NP)
        r_slot, r_stage = region(4 * 4 * 4096), region(2 * 4 * D)

        def small(name, shape, dt=F32):
            n = 1
            for s in shape[1:]:
                n *= s
            at = region(n * (2 if dt == F16 else 4))
            return put(name, shape, dt, at)

        act_hi = put("act_hi", [P, KC, NP], F16, r1)
        act_lo = put("act_lo", [P, KC, NP], F16, r1 + 2 * KC * NP)
        ln_hi = put("ln_hi", [P, KC, NP], F16, r2)
        ln_lo = put("ln_lo", [P, KC, NP], F16, r2 + 2 * KC * NP)
        z_hi = put("z_hi", [P, T, D], F16, r2)
        z_lo = put("z_lo", [P, T, D], F16, r2 + 2 * T * D)
        acc = put("acc", [P, T, D], F32, r2)
        adj = put("adj", [P, T, NP], F16, r_adj)
        gelu_hi = put("gelu_hi", [P, 4, NP], F16, r_adj)
        gelu_lo = put("gelu_lo", [P, 4, NP], F16, r_adj + 8 * NP)
        g32 = put("g32", [P, 2, 512], F32, r_adj + 16 * NP)
        b2_sb = put("b2_sb", [EXPERTS, D], F32, r_adj)
        cwT = put("cwT", [EXPERTS, NP], F32, r_adj + 4 * D)
        lg = put("lg", [P, 6, T, EXPERTS], F32, r_adj + 4 * D + 4 * NP)
        wslot = put("wslot", [P, 16, 2, D], F16, r_slot)
        stage = put("stage", [P, 2, D], F32, r_stage)

        ident = small("ident", [P, P])
        ones16 = small("ones16", [P, P], F16)
        block_f = small("block_f", [P, GROUPS])
        block_i = small("block_i", [P, GROUPS], I32)
        colv = small("colv", [P, 4, KC])
        colraw = small("colraw", [P, 3, KC])
        b1c = small("b1c", [P, EXPERTS * 4])
        rw32 = small("rw32", [P, KC, EXPERTS])
        rw16 = small("rw16", [P, KC, 2, EXPERTS], F16)
        rb = small("rb", [P, EXPERTS])
        dinv_col = small("dinv_col", [P, T])
        stats = small("stats", [P, 2, 12])
        mv = small("mv", [P, 2, 2])
        rstd = small("rstd", [P, 2])
        ssq = small("ssq", [P, 2, HEADS])
        nrm = small("nrm", [P, 2, HEADS])
        half_pow = small("half_pow", [P, HEADS])
        mhalf_pow = small("mhalf_pow", [P, 2])
        halfc = small("halfc", [P, 1])
        sel = small("sel", [P, 6, T])
        cws = small("cws", [P, T, EXPERTS])
        r_late = top[0]
        iota_d = small("iota_d", [P, N], F16)
        iota_s = small("iota_s", [P, P], F16)
        edges = small("edges", [P, SPP, 2])
        r_work = top[0]

        class Work:
            def __init__(self, at, end):
                self.at, self.end = at, end

            def __call__(self, name, shape, dt=F32):
                n = 1
                for s in shape[1:]:
                    n *= s
                t = put(name, shape, dt, self.at)
                self.at += -(-n * (2 if dt == F16 else 4) // 64) * 64
                assert self.at <= self.end, (name, self.at, self.end)
                return t

        end = nc.sbuf_usable_end
        w = Work(r2, r_adj)
        xin0 = w("xin0", [P, 2, D])
        xn0 = w("xn0", [P, 2, D])
        w = Work(r_slot + 2 * 4 * 4096, r_stage)
        ge = w("ge", [P, T + 1, EJ])
        member = w("member", [P, T, EJ])
        cum = w("cum", [P, T, EJ])
        posb = w("posb", [P, T, EJ])
        e_i = w("e_i", [P, 2, EJ], I32)
        w = Work(r2, r_adj)
        kb = w("kb", [P, 2, 512])
        ks = w("ks", [P, 2, 512])
        ksq = w("ksq", [P, 2, 512])
        v16 = w("v16", [P, 2, 512])
        k_hi_t, k_lo_t, v_hi_t, v_lo_t = (w(n, [P, 2, 512], F16) for n in ("k_hi", "k_lo", "v_hi", "v_lo"))
        bk_bc = w("bk_bc", [P, 2, D])
        bv_bc = w("bv_bc", [P, 2, D])
        w = Work(r_work, end)
        st0 = w("st0", [P, 2, 512])
        stp = w("stp", [P, 512])
        zeros16 = w("zeros16", [P, 512], F16)
        idx = w("idx", [P, EJ], I32)
        pay = w("pay", [P, EJ, 2])
        idx_b = w("idx_b", [P, 4, 1], I32)
        pay_b = w("pay_b", [P, 4, 2])
        st_hi = w("st_hi", [P, 2, 512], F16)
        st_lo = w("st_lo", [P, 2, 512], F16)
        mask = w("mask", [P, 4, P])
        bq_bc = w("bq_bc", [P, D])
        w = Work(r_adj, r_slot)
        es = w("es", [P, 5, EJ])
        e_small = w("e_small", [P, 5, 16])
        ei_small = w("ei_small", [P, 16], I32)
        upper = w("upper", [P, P])
        ones32 = w("ones32", [P, P])
        minus1 = w("minus1", [P, 2 * SPP])
        iota_i = w("iota_i", [P, N], I32)
        giota_i = w("giota_i", [P, GROUPS], I32)
        giota = w("giota", [P, GROUPS])
        pid_i = w("pid_i", [P, EJ], I32)
        lnx = put("lnx", [P, D], F32, r_work)
        lnf = put("lnf", [P, D], F32, r_work + 4 * D)
        w = Work(r_adj, r_slot)
        qn = w("qn", [P, 2, D])
        qT_hi_t = w("qT_hi", [P, 2, D], F16)
        qT_lo_t = w("qT_lo", [P, 2, D], F16)
        qb = w("qb", [P, D])
        qs = w("qs", [P, D])
        w = Work(r_work, end)
        bsum = w("bsum", [P, D])
        xin = w("xin", [P, 2, D])
        mo = w("mo", [P, 2, D])
        w = Work(r_work, end)
        dst_1h = w("dst_1h", [P, 2, TG, N], F16)
        src_1h = w("src_1h", [P, 2, TG, P], F16)
        w = Work(r_work, end)
        dinv = w("dinv", [P, NP])
        s0 = w("s0", [P, 2, N])
        tg = w("tg", [P, N])
        w = Work(r_late, end)
        xm = w("xm", [P, 2, D])
        x1 = w("x1b", [P, 2, D])
        yb = w("yb", [P, 2, D])
        w = Work(r_late, end)
        lnw_bc = w("lnw_bc", [P, D])
        lnb_bc = w("lnb_bc", [P, D])
        x1in = w("x1in", [P, 2, D])
        fin = w("fin", [P, 2, D])

        ps = ctx.enter_context(nc.psum_tensor("ps", [P, 8, 512], F32))

        def banks(b, n, width=None):
            v = ps[:, b:b + n, :].rearrange("p b n -> p (b n)")
            return v if width is None else v[:, 0:width]

        names = """x_in0 x_in1 consts_in cols_in const_made edge_in rank_step
            minus_made minus_out edge_tot edge_placed totals_made
            ln0_var ln0_rstd ln0_done ln0_T ln0_hi ln0_lo
            stage_in0 stage_in1 diag_added w_hi w_lo
            k_biased v_scaled kv_ready k_silu k_sq v_hi v_lo k_ssq k_nrm k_inv k_normed k_hi k_lo
            state_zero state_mm state_first state_step state_lo zeros_made
            edge_copied scat0 scat1 scat2 scat3 table_in
            q_ready0 q_ready1 q_biased0 q_biased1 q_silu q_sq q_ssq q_nrm q_inv q_normed
            qT_ready qT_hi qT_lo o_ready o_stat o_var o_rstd o_normed lnT_ready lnT_f lnT_hi lnT_lo
            bsum_made wo_ready wo_biased wo_x mixed_out0 mixed_out1 xin_in0 xin_in1
            adj_zero zp_ready z_hi z_lo onehot grp_ready grp_added deg_ready dinv_max dinv_made dcol_ready dcol_made
            s_ready s_biased s_out0 s_out1 s_in0 s_in1 a_ready a_scaled a_sum h_hi h_lo
            z1_ready z1_hi z1_lo
            f_s f_g f_x1a f_x1 f_stat f_var f_rstd f_y f_T f_yhi f_ylo f_lg xm_in0 xm_in1 x1_out0 x1_out1 y_out0 y_out1
            rw_lo r_step r_exp acc_in b2_in cwT_ready cwT_made b2_ready b2_added
            g_ready g_gelu g_hi g_lo gpad y_ready y_added
            x1_in0 x1_in1 lnwb_in e_stat e_var e_rstd e_n e_affine e_x out0 out1 prep_step ln0_stat bv_scaled bsum_in r_done passed""".split()
        S = {n: ctx.enter_context(nc.semaphore(n)) for n in names}
        block = ctx.enter_context(nc.Block())
        ds = bass.ds

        def chunk_loop(eng, body):
            body(0, 0, None)
            body(1, 1, None)
            with eng.Fori(1, T // 2) as i:
                body(2 * i, 0, i - 1)
                body(2 * i + 1, 1, i - 1)

        def settle(eng):
            eng.sem_inc(S["passed"], 1)

        def q_loop(eng, body):
            for c in range(4):
                body(c, c % 2, None if c < 2 else 0)
            with eng.Fori(2, T // 2) as i:
                body(2 * i, 0, i - 1)
                body(2 * i + 1, 1, i - 1)
            body(T, 0, None)
            body(T + 1, 1, None)

        def expert_loop(eng, body):
            body(0, 0, True, False)
            body(1, 1, False, False)
            with eng.Fori(1, EXPERTS // 2 - 1) as i:
                body(2 * i, 0, False, False)
                body(2 * i + 1, 1, False, False)
            body(EXPERTS - 2, 0, False, False)
            body(EXPERTS - 1, 1, False, True)

        @block.sync
        def _(sp):
            def stage_load(batch, i, j):
                if batch == 0 and isinstance(i, int) and i == 0:
                    pass
                else:
                    sp.wait_ge(S["w_lo"], 8 * batch + 2 * i + j - 1)
                sp.dma_start(stage[:, j, :], weights[ds(8 * batch + 4 * j + i, 1)].rearrange("a p d -> p (a d)")).then_inc(S[f"stage_in{j}"], 16)

            def batch_load(batch):
                if batch == 0:
                    for j in range(2):
                        stage_load(0, 0, j)
                    with sp.Fori(1, 4) as i:
                        for j in range(2):
                            stage_load(0, i, j)
                else:
                    with sp.Fori(0, 4) as i:
                        for j in range(2):
                            stage_load(batch, i, j)

            sp.dma_start(e_i[:, 0, :], edge_src).then_inc(S["edge_in"], 16)
            sp.dma_start(e_i[:, 1, :], edge_dst).then_inc(S["edge_in"], 16)
            for c in range(2):
                sp.dma_start(xin0[:, c, :], x_t[:, c, :]).then_inc(S[f"x_in{c}"], 16)
            sp.dma_start(colraw[:], cols).then_inc(S["cols_in"], 16)
            sp.dma_start(b1c[:], b1col).then_inc(S["cols_in"], 16)
            sp.dma_start(rw32[:], router).then_inc(S["cols_in"], 16)
            sp.dma_start(rb[:], router_b.partition_broadcast(P)).then_inc(S["cols_in"], 16)
            sp.dma_start(bq_bc[:], rows[0].partition_broadcast(P)).then_inc(S["consts_in"], 16)
            with sp.Fori(1, T // 2) as i:
                for j in range(2):
                    sp.wait_ge(S["ln0_done"], 2 * i + j - 1)
                    sp.dma_start(xin0[:, j, :], x_t[:, ds(2 * i + j, 1), :].rearrange("p a d -> p (a d)"))\
                      .then_inc(S[f"x_in{j}"], 16)
            batch_load(0)
            sp.wait_ge(S["ln0_lo"], T)
            for k in range(2):
                sp.dma_start(bk_bc[:, k, :], rows[1 + k].partition_broadcast(P)).then_inc(S["consts_in"], 16)
                sp.dma_start(bv_bc[:, k, :], rows[3 + k].partition_broadcast(P)).then_inc(S["consts_in"], 16)
            for batch in range(1, BATCHES):
                batch_load(batch)

        @block.gpsimd
        def _(pool):
            pool.memset(minus1[:], -1.0).then_inc(S["minus_made"], 1)
            pool.memset(ident[:], 0.0).then_inc(S["zeros_made"], 1)
            pool.memset(ones32[:], 1.0).then_inc(S["zeros_made"], 1)
            pool.memset(upper[:], 0.0).then_inc(S["zeros_made"], 1)
            pool.wait_ge(S["zeros_made"], 3)
            pool.affine_select(out=ident[:], in_=ident[:], compare_op=ALU.not_equal, fill=1.0, base=0,
                               pattern=[[-1, P]], channel_multiplier=1).then_inc(S["const_made"], 1)
            pool.affine_select(out=upper[:], in_=ones32[:], compare_op=ALU.is_gt, fill=0.0, base=0,
                               pattern=[[1, P]], channel_multiplier=-1).then_inc(S["const_made"], 1)
            pool.memset(ones16[:], 1.0).then_inc(S["const_made"], 1)
            pool.memset(half_pow[:], 0.5).then_inc(S["const_made"], 1)
            pool.memset(mhalf_pow[:], -0.5).then_inc(S["const_made"], 1)
            pool.memset(halfc[:], 0.5).then_inc(S["const_made"], 1)
            pool.iota(iota_i[:], pattern=[[1, N]], base=0, channel_multiplier=0).then_inc(S["const_made"], 1)
            pool.iota(giota_i[:], pattern=[[TG * P, GROUPS]], base=0, channel_multiplier=0)\
                .then_inc(S["const_made"], 1)
            pool.iota(pid_i[:], pattern=[[P, EJ]], base=ROWS - P * (E // P), channel_multiplier=1).then_inc(S["const_made"], 1)
            pool.wait_ge(S["minus_made"], 1)
            pool.dma_start(bucket_rows[0:ROWS, :].rearrange("(p s) c -> p (s c)", p=P), minus1[:])\
                .then_inc(S["minus_out"], 16)
            pool.wait_ge(S["const_made"], 9)
            with pool.Fori(0, T) as c:
                pool.wait_ge(S["ln0_var"], c + 1)
                pool.tensor_tensor(rstd[:, 0:1], mv[:, 0, 1:2], mhalf_pow[:, 0:1], ALU.pow).then_inc(S["ln0_rstd"], 1)

            pool.wait_ge(S["edge_placed"], 2)
            pool.wait_ge(S["minus_out"], 16)

            def kv(g):
                pool.wait_ge(S["k_ssq"], g + 1)
                pool.tensor_tensor(nrm[:, 0, 0:8], ssq[:, 0, 0:8], half_pow[:, 0:8], ALU.pow).then_inc(S["k_nrm"], 1)

            def place(g, first):
                for q in range(4):
                    if not first:
                        pool.wait_ge(S[f"scat{q}"], 16 * g)
                    pool.tensor_copy(idx_b[:, q, :], idx[:, ds(4 * g + q, 1)]).then_inc(S["edge_copied"], 1)
                    pool.tensor_copy(pay_b[:, q, :], pay[:, ds(4 * g + q, 1), :].rearrange("p a c -> p (a c)"))\
                        .then_inc(S["edge_copied"], 1)
                    pool.wait_ge(S["edge_copied"], 8 * g + 2 * q + 2)
                    settle(pool)
                    pool.indirect_dma_start(
                        out=bucket_rows, out_offset=bass.IndirectOffsetOnAxis(ap=idx_b[:, q, :].bitcast(U32), axis=0),
                        in_=pay_b[:, q, :], in_offset=None).then_inc(S[f"scat{q}"], 16)

            kv(0)
            place(0, True)
            with pool.Fori(1, 4 * T) as g:
                kv(g)
                place(g, False)
            for q in range(4):
                pool.wait_ge(S[f"scat{q}"], 16 * 4 * T)
            pool.dma_start(edges[:].rearrange("p s c -> p (s c)"),
                           bucket_rows[0:ROWS, :].rearrange("(p s) c -> p (s c)", p=P)).then_inc(S["table_in"], 16)

            def q_body(c, j, conv):
                if not (isinstance(c, int) and c < 2):
                    pool.wait_ge(S["o_var"], c - 1)
                    pool.tensor_tensor(rstd[:, 0:1], mv[:, 0, 1:2], mhalf_pow[:, 0:1], ALU.pow).then_inc(S["o_rstd"], 1)
                if not (isinstance(c, int) and c >= T):
                    pool.wait_ge(S["q_ssq"], c + 1)
                    pool.tensor_tensor(nrm[:, 1, :], ssq[:, 1, :], half_pow[:], ALU.pow).then_inc(S["q_nrm"], 1)

            q_loop(pool, q_body)

            pool.wait_ge(S["lnT_lo"], T)
            pool.dma_start(bsum[:], rows[5].partition_broadcast(P)).then_inc(S["bsum_in"], 16)
            pool.dma_start(mo[:, 1, :], rows[6].partition_broadcast(P)).then_inc(S["bsum_in"], 16)
            pool.memset(adj[:], 0.0).then_inc(S["adj_zero"], 1)
            for j in range(2):
                pool.dma_start(xin[:, j, :], x_t[:, j, :]).then_inc(S[f"xin_in{j}"], 16)

            def wo_body(c, j, conv):
                pool.wait_ge(S["wo_x"], c + 1)
                pool.dma_start(mixed[:, ds(c, 1), :].rearrange("p a d -> p (a d)"), mo[:, j, :])\
                    .then_inc(S[f"mixed_out{j}"], 16)

            def wo_load(c, j):
                pool.dma_start(xin[:, j, :], x_t[:, ds(c, 1), :].rearrange("p a d -> p (a d)"))\
                    .then_inc(S[f"xin_in{j}"], 16)

            with pool.Fori(0, T // 2 - 1) as i:
                for j in range(2):
                    wo_body(2 * i + j, j, None)
                    wo_load(2 * i + j + 2, j)
            wo_body(T - 2, 0, None)
            wo_body(T - 1, 1, None)

            with pool.Fori(0, KC // 2) as i:
                for j in range(2):
                    pool.wait_ge(S["s_biased"], 2 * i + j + 1)
                    pool.dma_start(selfT[:, ds(2 * i + j, 1), :].rearrange("p a d -> p (a d)"), s0[:, j, :])\
                        .then_inc(S[f"s_out{j}"], 16)
            for j in range(2):
                pool.wait_ge(S[f"s_out{j}"], 16 * KC // 2)
            for j in range(2):
                pool.dma_start(s0[:, j, :], selfT[:, j, :]).then_inc(S[f"s_in{j}"], 16)
            with pool.Fori(1, KC // 2) as i:
                for j in range(2):
                    pool.wait_ge(S["h_lo"], 2 * i + j - 1)
                    pool.dma_start(s0[:, j, :], selfT[:, ds(2 * i + j, 1), :].rearrange("p a d -> p (a d)"))\
                        .then_inc(S[f"s_in{j}"], 16)

            pool.wait_ge(S["h_lo"], KC)
            for j in range(2):
                pool.wait_ge(S[f"mixed_out{j}"], 16 * T // 2)
            for j in range(2):
                pool.dma_start(xm[:, j, :], mixed[:, j, :]).then_inc(S[f"xm_in{j}"], 16)

            def f_body(c, j, last):
                pool.wait_ge(S["f_var"], c + 1)
                pool.tensor_tensor(rstd[:, 0:1], mv[:, 0, 1:2], mhalf_pow[:, 0:1], ALU.pow).then_inc(S["f_rstd"], 1)
                pool.wait_ge(S["f_x1"], c + 1)
                pool.dma_start(x1_d[:, ds(c, 1), :].rearrange("p a d -> p (a d)"), x1[:, j, :])\
                    .then_inc(S[f"x1_out{j}"], 16)
                if not last:
                    pool.dma_start(xm[:, j, :], mixed[:, ds(c + 2, 1), :].rearrange("p a d -> p (a d)"))\
                        .then_inc(S[f"xm_in{j}"], 16)
                pool.wait_ge(S["f_y"], c + 1)
                settle(pool)
                pool.dma_start(y_d[:, ds(c, 1), :].rearrange("p a d -> p (a d)"), yb[:, j, :])\
                    .then_inc(S[f"y_out{j}"], 16)

            with pool.Fori(0, T // 2 - 1) as i:
                for j in range(2):
                    f_body(2 * i + j, j, False)
            f_body(T - 2, 0, True)
            f_body(T - 1, 1, True)
            for j in range(2):
                pool.wait_ge(S[f"y_out{j}"], 16 * T // 2)
            for j in range(2):
                pool.wait_ge(S[f"x1_out{j}"], 16 * T // 2)
            pool.wait_ge(S["f_g"], T)
            pool.dma_start(acc[:], y_d).then_inc(S["acc_in"], 16)
            pool.dma_start(b2_sb[:], b2).then_inc(S["b2_in"], 16)
            pool.wait_ge(S["f_ylo"], T)
            pool.dma_start(lnw_bc[:], rows[7].partition_broadcast(P)).then_inc(S["lnwb_in"], 16)
            pool.dma_start(lnb_bc[:], rows[8].partition_broadcast(P)).then_inc(S["lnwb_in"], 16)
            for j in range(2):
                pool.dma_start(x1in[:, j, :], x1_d[:, j, :]).then_inc(S[f"x1_in{j}"], 16)

            def end_body(c, j, last):
                pool.wait_ge(S["e_var"], c + 1)
                pool.tensor_tensor(rstd[:, 0:1], mv[:, 0, 1:2], mhalf_pow[:, 0:1], ALU.pow).then_inc(S["e_rstd"], 1)
                pool.wait_ge(S["e_x"], c + 1)
                pool.dma_start(out_t[:, ds(c, 1), :].rearrange("p a d -> p (a d)"), fin[:, j, :])\
                    .then_inc(S[f"out{j}"], 16)
                if not last:
                    pool.dma_start(x1in[:, j, :], x1_d[:, ds(c + 2, 1), :].rearrange("p a d -> p (a d)"))\
                        .then_inc(S[f"x1_in{j}"], 16)

            with pool.Fori(0, T // 2 - 1) as i:
                for j in range(2):
                    end_body(2 * i + j, j, False)
            end_body(T - 2, 0, True)
            end_body(T - 1, 1, True)
            for j in range(2):
                pool.wait_ge(S[f"out{j}"], 16 * T // 2)

        @block.tensor
        def _(pe):
            def w_at(slot, pos, part, c0, n):
                o = (pos % 2) * 512 + c0
                return wslot[:, 4 * slot + pos // 2, part, o:o + n]

            def nodes_unit(bank, hi, lo, slots, order, last=None):
                for pos in range(KC):
                    for s, b in zip(slots, bank):
                        lh, ll = hi(order[pos]), lo(order[pos])
                        pe.matmul(ps[:, b, :], lh, w_at(s, pos, 0, 0, 512), start=(pos == 0), stop=False)
                        pe.matmul(ps[:, b, :], lh, w_at(s, pos, 1, 0, 512), start=False, stop=False)
                        m = pe.matmul(ps[:, b, :], ll, w_at(s, pos, 0, 0, 512), start=False, stop=(pos == KC - 1))
                return m

            def tile_of(t, c):
                return lambda k: t[:, k, ds(c * P, P)] if not isinstance(c, int) else t[:, k, c * P:(c + 1) * P]

            def transposes(bank, src):
                for k in range(KC):
                    m = pe.matmul(ps[:, bank + k // 4, (k % 4) * P:(k % 4 + 1) * P], src[:, k * P:(k + 1) * P],
                                  ident[:], start=True, stop=True, is_transpose=True)
                return m

            pe.wait_ge(S["const_made"], 9)

            pe.wait_ge(S["edge_tot"], 1)
            pe.matmul(ps[:, 7, 0:T], upper[:], e_small[:, 0, 0:T], start=True, stop=True)
            pe.matmul(ps[:, 7, 16:16 + T], ones32[:], e_small[:, 0, 0:T], start=True, stop=True)\
              .then_inc(S["totals_made"], 1)

            def ln0(c, j, conv):
                pe.wait_ge(S["ln0_done"], c + 1)
                if not (isinstance(c, int) and c < 2):
                    pe.wait_ge(S["ln0_lo"], c - 1)
                transposes(2 * j, xn0[:, j, :]).then_inc(S["ln0_T"], 1)

            chunk_loop(pe, ln0)

            for ph in range(4):
                h = ph % 2
                slot = 2 * (ph % 2)
                sbank = 4 + ph % 2
                pe.wait_ge(S["w_lo"], 8 * (ph + 1))
                if ph == 0:
                    pe.wait_ge(S["ln0_lo"], T)
                    pe.wait_ge(S["state_zero"], 1)
                if ph >= 2:
                    pe.wait_ge(S["state_first"], ph - 1)
                pe.matmul(ps[:, sbank, :], zeros16[:, 0:P], zeros16[:], start=True, stop=False,
                          skip_group_check=True)

                def kv(c, j, conv, ph=ph, h=h, slot=slot, sbank=sbank):
                    g = T * ph + c
                    if not (isinstance(c, int) and g < 2):
                        pe.wait_ge(S["v_scaled"], g - 1)
                    nodes_unit([2 * j, 2 * j + 1], tile_of(act_hi, c), tile_of(act_lo, c),
                               [slot, slot + 1], DIAG[h]).then_inc(S["kv_ready"], 1)
                    if not (isinstance(c, int) and c == 0):
                        states(g - 1, 1 - j, P)

                def states(g, j, rows_, sbank=sbank):
                    pe.wait_ge(S["v_lo"], g + 1)
                    pe.wait_ge(S["k_lo"], g + 1)
                    for p in range(4):
                        o = ps[:, sbank, p * P:(p + 1) * P]
                        for a, b in ((k_hi_t, v_hi_t), (k_hi_t, v_lo_t), (k_lo_t, v_hi_t)):
                            m = pe.matmul(o, a[0:rows_, j, p * P:(p + 1) * P], b[0:rows_, j, p * P:(p + 1) * P],
                                          start=False, stop=False, skip_group_check=True)
                    m.then_inc(S["state_mm"], 1)

                kv(0, 0, None)
                kv(1, 1, None)
                with pe.Fori(1, T // 2) as i:
                    kv(2 * i, 0, None)
                    kv(2 * i + 1, 1, None)
                states(T * ph + T - 1, 1, LAST)

            pe.wait_ge(S["w_lo"], 8 * 5)
            pe.wait_ge(S["v_scaled"], 4 * T)
            pe.wait_ge(S["state_lo"], 2)

            def q_body(c, j, conv):
                early = isinstance(c, int) and c < 2
                done = isinstance(c, int) and c >= T
                hi, lo = tile_of(act_hi, c), tile_of(act_lo, c)
                if not done:
                    if not (isinstance(c, int) and c == 0):
                        pe.wait_ge(S["q_biased0"], c)
                    nodes_unit([0], hi, lo, [0], DIAG[0]).then_inc(S["q_ready0"], 1)
                if not early:
                    pe.wait_ge(S["qT_lo"], c - 1)
                    if not (isinstance(c, int) and c == 2):
                        pe.wait_ge(S["o_normed"], c - 2)
                    for p in range(KC):
                        o = ps[:, 4 + p // 4, (p % 4) * P:(p % 4 + 1) * P]
                        s = lambda t: t[:, p // 4, (p % 4) * P:(p % 4 + 1) * P]
                        q = lambda t: t[:, j, p * P:(p + 1) * P]
                        pe.matmul(o, q(qT_hi_t), s(st_hi), start=True, stop=False)
                        pe.matmul(o, q(qT_hi_t), s(st_lo), start=False, stop=False)
                        m = pe.matmul(o, q(qT_lo_t), s(st_hi), start=False, stop=True)
                    m.then_inc(S["o_ready"], 1)
                if not done:
                    if not (isinstance(c, int) and c == 0):
                        pe.wait_ge(S["q_biased1"], c)
                    nodes_unit([1], hi, lo, [1], DIAG[1]).then_inc(S["q_ready1"], 1)
                if not early:
                    pe.wait_ge(S["o_normed"], c - 1)
                    if not (isinstance(c, int) and c == 2):
                        pe.wait_ge(S["lnT_f"], c - 2)
                    transposes(6, lnx).then_inc(S["lnT_ready"], 1)
                if not (isinstance(c, int) and (c == 0 or c > T)):
                    pe.wait_ge(S["q_normed"], c)
                    if not (isinstance(c, int) and c == 1):
                        pe.wait_ge(S["qT_lo"], c - 1)
                    transposes(2, qn[:, 1 - j, :]).then_inc(S["qT_ready"], 1)

            q_loop(pe, q_body)

            pe.wait_ge(S["w_lo"], 8 * 6)
            pe.wait_ge(S["q_biased1"], T)
            pe.wait_ge(S["qT_lo"], T)
            pe.wait_ge(S["lnT_lo"], T)

            def wo_body(c, j, conv):
                if not (isinstance(c, int) and c < 2):
                    pe.wait_ge(S["wo_biased"], c - 1)
                nodes_unit([2 * j, 2 * j + 1], tile_of(ln_hi, c), tile_of(ln_lo, c), [2, 3], PLAIN)\
                    .then_inc(S["wo_ready"], 1)

            chunk_loop(pe, wo_body)

            pe.wait_ge(S["w_lo"], 8 * 7)
            pe.wait_ge(S["wo_biased"], T)
            pe.wait_ge(S["lnT_f"], T)

            def group(g, par, first):
                pe.wait_ge(S["onehot"], g + 1)
                if not first:
                    pe.wait_ge(S["grp_added"], g - 1)
                for t in range(TG):
                    for n, (c0, w_) in enumerate(COLS):
                        m = pe.matmul(ps[:, 3 * par + n, 0:w_], src_1h[:, par, t, :], dst_1h[:, par, t, c0:c0 + w_],
                                      start=(t == 0), stop=(t == TG - 1))
                m.then_inc(S["grp_ready"], 1)

            def z_body(c, j, conv):
                if not (isinstance(c, int) and c == 0):
                    pe.wait_ge(S["z_lo"], c)
                nodes_unit([6, 7], tile_of(act_hi, c), tile_of(act_lo, c), [0, 1], PLAIN)\
                    .then_inc(S["zp_ready"], 1)
                for q in range(5):
                    group(5 * c + q, (5 * j + q) % 2, isinstance(c, int) and 5 * c + q < 2)

            chunk_loop(pe, z_body)
            pe.wait_ge(S["grp_added"], GROUPS)
            for n, w_ in enumerate((512, 512, NP - 1024)):
                for s in range(T):
                    m = pe.matmul(ps[:, n, 0:w_], ones16[:], adj[:, s, n * 512:n * 512 + w_],
                                  start=(s == 0), stop=(s == T - 1))
            m.then_inc(S["deg_ready"], 1)
            pe.wait_ge(S["dinv_made"], 1)
            for t in range(T):
                m = pe.matmul(ps[:, 3, t:t + 1], dinv[0:1, t * P:(t + 1) * P], ident[0:1, 0:1], start=True, stop=True)
            m.then_inc(S["dcol_ready"], 1)

            pe.wait_ge(S["w_lo"], 8 * 8)
            pe.wait_ge(S["dcol_made"], 1)

            def feature_unit(bank, lhs, last_k, rhs_hi, rhs_lo):
                for k in range(last_k):
                    lh, ll = lhs(k)
                    for n, (c0, w_) in enumerate(COLS):
                        pe.matmul(ps[:, bank + n, 0:w_], lh, rhs_hi(k, c0, w_), start=(k == 0), stop=False)
                    if rhs_lo is not None:
                        for n, (c0, w_) in enumerate(COLS):
                            pe.matmul(ps[:, bank + n, 0:w_], lh, rhs_lo(k, c0, w_), start=False, stop=False)
                    for n, (c0, w_) in enumerate(COLS):
                        m = pe.matmul(ps[:, bank + n, 0:w_], ll, rhs_hi(k, c0, w_), start=False, stop=(k == last_k - 1))
                return m

            def s_chunk(u, i, j):
                o = 4 * u + 2 * i + j
                if not (u == 0 and isinstance(i, int) and i == 0):
                    pe.wait_ge(S["s_biased"], o - 1)

                def lhs(k):
                    at = lambda part: wslot[:, 4 * (2 + u) + k // 2, part, ds((k % 2) * 512 + (2 * i + j) * P, P)]
                    return at(0), at(1)
                feature_unit(3 * j, lhs, KC, lambda k, c0, w_: act_hi[:, k, c0:c0 + w_],
                             lambda k, c0, w_: act_lo[:, k, c0:c0 + w_]).then_inc(S["s_ready"], 1)

            for u in range(2):
                if u == 0:
                    s_chunk(0, 0, 0)
                    s_chunk(0, 0, 1)
                with pe.Fori(1 - u, 2) as i:
                    s_chunk(u, i, 0)
                    s_chunk(u, i, 1)

            pe.wait_ge(S["s_biased"], KC)
            pe.wait_ge(S["z_lo"], T)

            def a_chunk(o, j, first):
                if not first:
                    pe.wait_ge(S["a_scaled"], o - 1)
                feature_unit(3 * j, lambda s: (z_hi[:, s, ds(o * P, P)], z_lo[:, s, ds(o * P, P)]), T,
                             lambda s, c0, w_: adj[:, s, c0:c0 + w_], None).then_inc(S["a_ready"], 1)

            a_chunk(0, 0, True)
            a_chunk(1, 1, True)
            with pe.Fori(1, KC // 2) as i:
                a_chunk(2 * i, 0, False)
                a_chunk(2 * i + 1, 1, False)

            pe.wait_ge(S["w_lo"], 8 * 9)
            pe.wait_ge(S["h_lo"], KC)

            def z1_body(c, j, conv):
                if not (isinstance(c, int) and c < 2):
                    pe.wait_ge(S["z1_lo"], c - 1)
                nodes_unit([2 * j, 2 * j + 1], tile_of(act_hi, c), tile_of(act_lo, c), [0, 1], PLAIN)\
                    .then_inc(S["z1_ready"], 1)

            chunk_loop(pe, z1_body)

            pe.wait_ge(S["w_lo"], 8 * 10)
            pe.wait_ge(S["z1_lo"], T)
            pe.wait_ge(S["rw_lo"], 1)

            def f_body(c, j, conv):
                done = isinstance(c, int) and c >= T
                zero = isinstance(c, int) and c == 0
                if not done:
                    if not zero:
                        pe.wait_ge(S["f_x1a"], c)
                    nodes_unit([0, 1], tile_of(act_hi, c), tile_of(act_lo, c), [2, 3], PLAIN)\
                        .then_inc(S["f_s"], 1)
                if not zero:
                    pe.wait_ge(S["f_y"], c)
                    if not (isinstance(c, int) and c == 1):
                        pe.wait_ge(S["f_ylo"], c - 1)
                    transposes(4, yb[:, 1 - j, :]).then_inc(S["f_T"], 1)
                if not done:
                    if not zero:
                        pe.wait_ge(S["f_x1"], c)
                    for s in range(T):
                        a = adj[:, s, ds(c * P, P)]
                        for hh in range(2):
                            pe.matmul(ps[:, 2 + hh, :], a, z_hi[:, s, hh * 512:(hh + 1) * 512], start=(s == 0), stop=False)
                            m = pe.matmul(ps[:, 2 + hh, :], a, z_lo[:, s, hh * 512:(hh + 1) * 512],
                                          start=False, stop=(s == T - 1))
                    m.then_inc(S["f_g"], 1)
                if not zero:
                    pe.wait_ge(S["f_ylo"], c)
                    for k in range(KC):
                        col = ds(c * P - P, P)
                        o = ps[:, 6, ds(c * EXPERTS - EXPERTS, EXPERTS)]
                        pe.matmul(o, act_hi[:, k, col], rw16[:, k, 0, :], start=(k == 0), stop=False)
                        pe.matmul(o, act_hi[:, k, col], rw16[:, k, 1, :], start=False, stop=False)
                        m = pe.matmul(o, act_lo[:, k, col], rw16[:, k, 0, :], start=False, stop=(k == KC - 1))
                    m.then_inc(S["f_lg"], 1)

            chunk_loop(pe, f_body)
            f_body(T, 0, None)

            pe.wait_ge(S["r_done"], 1)
            pe.wait_ge(S["b2_in"], 16)
            for t in range(T):
                m = pe.matmul(ps[0:EXPERTS, t // 4, (t % 4) * P:(t % 4 + 1) * P], lg[:, 5, t, :], ident[:],
                              start=True, stop=True, is_transpose=True)
            m.then_inc(S["cwT_ready"], 1)
            pe.wait_ge(S["cwT_made"], 1)
            for t in range(T):
                if t >= 2:
                    pe.wait_ge(S["b2_added"], t - 1)
                for hh in range(2):
                    m = pe.matmul(ps[:, 4 + 2 * (t % 2) + hh, :], cwT[:, t * P:(t + 1) * P],
                                  b2_sb[:, hh * 512:(hh + 1) * 512], start=True, stop=True)
                m.then_inc(S["b2_ready"], 1)
            pe.wait_ge(S["b2_added"], T)
            pe.wait_ge(S["gpad"], 1)

            def expert(e, par, first, last):
                slot = 2 * par

                def first_product(tile, c0, w_, initial):
                    for f in range(4):
                        if not initial:
                            pe.wait_ge(S["g_gelu"], 12 * e + 4 * tile + f - 3)
                        for k in range(KC):
                            rh, rl = ((act_hi[:, k, c0:c0 + w_], act_lo[:, k, c0:c0 + w_]) if isinstance(c0, int)
                                      else (act_hi[:, k, ds(c0, w_)], act_lo[:, k, ds(c0, w_)]))
                            pe.matmul(ps[:, f, 0:w_], w_at(slot, k, 0, f * P, P), rh, start=(k == 0), stop=False)
                            pe.matmul(ps[:, f, 0:w_], w_at(slot, k, 0, f * P, P), rl, start=False, stop=False)
                            m = pe.matmul(ps[:, f, 0:w_], w_at(slot, k, 1, f * P, P), rh, start=False, stop=(k == KC - 1))
                        m.then_inc(S["g_ready"], 1)

                pe.wait_ge(S["w_lo"], 8 * e + 8 * 11)
                for n, (c0, w_) in enumerate(COLS):
                    first_product(n, c0, w_, first and n == 0)

                def second_product(c, j, conv):
                    for hh in range(2):
                        b = 4 + 2 * j + hh
                        if not (first and isinstance(c, int) and c < 2):
                            pe.wait_ge(S["y_added"], 20 * e + 2 * c + hh - 3)
                        if hh == 0:
                            if isinstance(c, int):
                                pe.wait_ge(S["g_lo"], 12 * e + 4)
                        for k in range(4):
                            gh, gl = gelu_hi[:, k, ds(c * P, P)], gelu_lo[:, k, ds(c * P, P)]
                            wh, wl = (wslot[:, 4 * (slot + 1) + k, part, hh * 512:(hh + 1) * 512] for part in (0, 1))
                            pe.matmul(ps[:, b, :], gh, wh, start=(k == 0), stop=False)
                            pe.matmul(ps[:, b, :], gh, wl, start=False, stop=False)
                            m = pe.matmul(ps[:, b, :], gl, wh, start=False, stop=(k == 3))
                        m.then_inc(S["y_ready"], 1)

                second_product(0, 0, None)
                second_product(1, 1, None)
                second_product(2, 0, None)
                second_product(3, 1, None)
                pe.wait_ge(S["g_lo"], 12 * e + 12)
                settle(pe)
                with pe.Fori(2, T // 2) as i:
                    second_product(2 * i, 0, None)
                    second_product(2 * i + 1, 1, None)

            expert_loop(pe, expert)

        @block.scalar
        def _(act):
            act.preload_act_table(ACT.Silu)

            def convert(batch, i, diag):
                for j in range(2):
                    if diag:
                        act.wait_ge(S["diag_added"], 8 * batch + 2 * i + j + 1)
                    else:
                        act.wait_ge(S[f"stage_in{j}"], 16 * (4 * batch + i + 1))
                    settle(act)
                    slot = 8 * (batch % 2) + 4 * j
                    act.activation(wslot[:, ds(slot + i, 1), 0, :].rearrange("p a d -> p (a d)"), stage[:, j, :],
                                   ACT.Copy, scale=SW).then_inc(S["w_hi"], 1)

            act.wait_ge(S["cols_in"], 64)
            act.activation(colv[:, 0, :], colraw[:, 0, :], ACT.Copy).then_inc(S["prep_step"], 1)
            act.activation(colv[:, 2:4, :], colraw[:, 1:3, :], ACT.Copy, scale=SX).then_inc(S["prep_step"], 1)
            act.activation(colv[:, 1, :], colraw[:, 0, :], ACT.Copy, scale=SX).then_inc(S["prep_step"], 1)
            act.wait_ge(S["prep_step"], 3)
            act.activation(rw16[:, :, 0, :], rw32[:], ACT.Copy, scale=SW).then_inc(S["prep_step"], 1)

            def ln0(c, j, conv):
                act.wait_ge(S["ln0_T"], c + 1)
                settle(act)
                act.activation(act_hi[:, :, ds(c * P, P)],
                               banks(2 * j, 2).rearrange("p (k n) -> p k n", n=P), ACT.Copy, scale=SX)\
                    .then_inc(S["ln0_hi"], 1)

            chunk_loop(act, ln0)
            with act.Fori(0, 4) as i:
                convert(0, i, True)
            act.wait_ge(S["consts_in"], 16 * 5)
            act.activation(bv_bc[:], bv_bc[:], ACT.Copy, scale=SX).then_inc(S["bv_scaled"], 1)

            for ph in range(4):
                def kv(c, j, conv, ph=ph):
                    g = T * ph + c
                    act.wait_ge(S["k_biased"], g + 1)
                    act.activation(ks[:, j, :], kb[:, j, :], ACT.Silu).then_inc(S["k_silu"], 1)
                    act.wait_ge(S["k_silu"], g + 1)
                    act.activation(ksq[:, j, :], ks[:, j, :], ACT.Square, bias=halfc[:]).then_inc(S["k_sq"], 1)
                    act.wait_ge(S["v_scaled"], g + 1)
                    if not (isinstance(c, int) and g < 2):
                        act.wait_ge(S["state_mm"], g - 1)
                    act.activation(v_hi_t[:, j, :], v16[:, j, :], ACT.Copy).then_inc(S["v_hi"], 1)
                    act.wait_ge(S["k_normed"], g + 1)
                    act.activation(k_hi_t[:, j, :], kb[:, j, :], ACT.Copy, scale=SX).then_inc(S["k_hi"], 1)
                    if conv is not None and j == 1:
                        convert(ph + 1, conv, True)

                chunk_loop(act, kv)

            def q_body(c, j, conv):
                if not (isinstance(c, int) and c >= T):
                    act.wait_ge(S["q_biased1"], c + 1)
                    act.activation(qs[:], qb[:], ACT.Silu).then_inc(S["q_silu"], 1)
                    act.wait_ge(S["q_silu"], c + 1)
                    act.activation(qb[:], qs[:], ACT.Square, bias=halfc[:]).then_inc(S["q_sq"], 1)
                if not (isinstance(c, int) and c < 2):
                    act.wait_ge(S["lnT_ready"], c - 1)
                    if not (isinstance(c, int) and c == 2):
                        act.wait_ge(S["lnT_lo"], c - 2)
                    for k in range(KC):
                        m = act.activation(lnf[:, k * P:(k + 1) * P], banks(6, 2)[:, k * P:(k + 1) * P], ACT.Identity,
                                           scale=colv[:, 2, k:k + 1], bias=colv[:, 3, k:k + 1])
                    m.then_inc(S["lnT_f"], 1)
                    act.wait_ge(S["lnT_f"], c - 1)
                    settle(act)
                    act.activation(ln_hi[:, :, ds(c * P - 2 * P, P)], lnf[:].rearrange("p (k n) -> p k n", n=P),
                                   ACT.Copy).then_inc(S["lnT_hi"], 1)
                if not (isinstance(c, int) and (c == 0 or c > T)):
                    act.wait_ge(S["qT_ready"], c)
                    if not (isinstance(c, int) and c < 3):
                        act.wait_ge(S["o_ready"], c - 2)
                    act.activation(qT_hi_t[:, 1 - j, :], banks(2, 2), ACT.Copy, scale=SX).then_inc(S["qT_hi"], 1)
                if conv is not None and j == 1:
                    convert(5, conv, False)

            q_loop(act, q_body)

            def wo_body(c, j, conv):
                if conv is not None and j == 1:
                    act.wait_ge(S["wo_ready"], c)
                    convert(6, conv, False)

            chunk_loop(act, wo_body)
            act.wait_ge(S["wo_ready"], T)

            def z_body(c, j, conv):
                act.wait_ge(S["zp_ready"], c + 1)
                settle(act)
                act.activation(z_hi[:, ds(c, 1), :].rearrange("p a d -> p (a d)"), banks(6, 2), ACT.Copy,
                               scale=1.0 / SW).then_inc(S["z_hi"], 1)
                if conv is not None and j == 1:
                    convert(7, conv, False)

            chunk_loop(act, z_body)

            act.wait_ge(S["dcol_made"], 1)

            def s_chunk(u, i, j):
                o = 4 * u + 2 * i + j
                act.wait_ge(S["s_ready"], o + 1)
                if not (u == 0 and isinstance(i, int) and i == 0):
                    act.wait_ge(S[f"s_out{j}"], 16 * (2 * u + i))
                settle(act)
                act.activation(s0[:, j, :], banks(3 * j, 3, N), ACT.Identity, scale=1.0 / (SW * SX),
                               bias=colv[:, 0, ds(o, 1)]).then_inc(S["s_biased"], 1)
                if j == 1:
                    convert_at(2 * u + i)

            def convert_at(i):
                convert(8, i, False)

            for u in range(2):
                if u == 0:
                    s_chunk(0, 0, 0)
                    s_chunk(0, 0, 1)
                with act.Fori(1 - u, 2) as i:
                    s_chunk(u, i, 0)
                    s_chunk(u, i, 1)

            def h_chunk(o, j):
                act.wait_ge(S["a_sum"], o + 1)
                settle(act)
                act.activation(act_hi[:, ds(o, 1), 0:N].rearrange("p a n -> p (a n)"), s0[:, j, :], ACT.Relu)\
                    .then_inc(S["h_hi"], 1)

            with act.Fori(0, KC // 2) as i:
                h_chunk(2 * i, 0)
                h_chunk(2 * i + 1, 1)

            def z1_body(c, j, conv):
                act.wait_ge(S["z1_ready"], c + 1)
                settle(act)
                act.activation(z_hi[:, ds(c, 1), :].rearrange("p a d -> p (a d)"), banks(2 * j, 2), ACT.Copy,
                               scale=1.0 / SW).then_inc(S["z1_hi"], 1)
                if conv is not None and j == 1:
                    convert(9, conv, False)

            chunk_loop(act, z1_body)

            def f_body(c, j, conv):
                if not (isinstance(c, int) and c == 0):
                    act.wait_ge(S["f_T"], c)
                    settle(act)
                    act.activation(act_hi[:, :, ds(c * P - P, P)],
                                   banks(4, 2).rearrange("p (k n) -> p k n", n=P), ACT.Copy, scale=SX)\
                        .then_inc(S["f_yhi"], 1)
                if conv is not None and j == 1:
                    convert(10, conv, False)

            chunk_loop(act, f_body)
            f_body(T, 0, None)

            act.wait_ge(S["r_step"], 1)
            act.activation(sel[:, 2, :], sel[:, 1, :], ACT.Exp).then_inc(S["r_exp"], 1)
            act.preload_act_table(ACT.Gelu)

            def expert(e, par, first, last):
                def gelu(tile, c0, w_):
                    for f in range(4):
                        n = 12 * e + 4 * tile + f
                        act.wait_ge(S["g_ready"], n + 1)
                        if not (first and tile == 0 and f < 2):
                            act.wait_ge(S["g_lo"], n - 1)
                        settle(act)
                        act.activation(g32[:, f % 2, 0:w_], ps[:, f, 0:w_], ACT.Gelu, scale=1.0 / (SW * SX),
                                       bias=b1c[:, ds(e * 4 + f, 1)]).then_inc(S["g_gelu"], 1)
                        act.wait_ge(S["g_gelu"], n + 1)
                        settle(act)
                        act.activation(gelu_hi[:, f, c0:c0 + w_], g32[:, f % 2, 0:w_], ACT.Copy, scale=SX)\
                            .then_inc(S["g_hi"], 1)

                for n, (c0, w_) in enumerate(COLS):
                    gelu(n, c0, w_)
                if not last:
                    with act.Fori(0, 4) as i:
                        for j in range(2):
                            act.wait_ge(S[f"stage_in{j}"], 16 * (4 * (e + 11) + i + 1))
                            settle(act)
                            slot = 8 * (1 - par) + 4 * j
                            act.activation(wslot[:, ds(slot + i, 1), 0, :].rearrange("p a d -> p (a d)"),
                                           stage[:, j, :], ACT.Copy, scale=SW).then_inc(S["w_hi"], 1)

            expert_loop(act, expert)

        @block.vector
        def _(dve):
            steps = [0]

            def then(ins):
                steps[0] += 1
                ins.then_inc(S["rank_step"], 1)
                dve.wait_ge(S["rank_step"], steps[0])

            def diag_add(batch, i):
                for j in range(2):
                    dve.wait_ge(S[f"stage_in{j}"], 16 * (4 * batch + i + 1))
                    d = stage[:, j, ds(i * P, P)]
                    dve.tensor_tensor(d, d, ident[:], ALU.add).then_inc(S["diag_added"], 1)

            def convert(batch, i):
                for j in range(2):
                    dve.wait_ge(S["w_hi"], 8 * batch + 2 * i + j + 1)
                    slot = 8 * (batch % 2) + 4 * j
                    at = lambda part: wslot[:, ds(slot + i, 1), part, :].rearrange("p a d -> p (a d)")
                    dve.scalar_tensor_tensor(at(1), stage[:, j, :], SW, at(0), ALU.mult, ALU.subtract)\
                        .then_inc(S["w_lo"], 1)

            then(dve.memset(mask[:], 0.0))
            dve.memset(mask[0:HD, :, 0:HD], SS)
            then(dve.memset(mask[HD:P, :, HD:P], SS))
            dve.wait_ge(S["edge_in"], 32)
            src_f, dst_f, rowf, tmp, loc = (es[:, n, :] for n in range(5))
            then(dve.tensor_copy(es[:, 0:2, :], e_i[:]))
            for b in range(T + 1):
                m = dve.tensor_scalar(ge[:, b, :], src_f, float(P * b), None, ALU.is_ge)
            then(m)
            dve.memset(tmp, 1.0)
            then(dve.tensor_tensor(member[:], ge[:, 0:T, :], ge[:, 1:T + 1, :], ALU.subtract))
            for b in range(T):
                m = dve.tensor_tensor_scan(cum[:, b, :], tmp, member[:, b, :], 0.0, ALU.mult, ALU.add)
            then(m)
            dve.tensor_copy(e_small[:, 0, 0:T], cum[:, :, EJ - 1]).then_inc(S["edge_tot"], 1)
            dve.wait_ge(S["const_made"], 9)
            dve.tensor_copy(iota_d[:], iota_i[:])
            dve.tensor_copy(iota_s[:], iota_i[:, 0:P])
            dve.tensor_copy(giota[:], giota_i[:])
            dve.wait_ge(S["totals_made"], 1)
            before, size, ends, offs = (e_small[:, n, 0:T] for n in (1, 2, 3, 4))
            then(dve.tensor_scalar(size, ps[:, 7, 16:16 + T], float(TG * P - 1), None, ALU.add))
            then(dve.tensor_copy(ei_small[:, 0:T], size))
            then(dve.tensor_scalar(ei_small[:, 0:T], ei_small[:, 0:T], 9, 9, ALU.arith_shift_right,
                                   ALU.logical_shift_left))
            then(dve.tensor_copy(size, ei_small[:, 0:T]))
            then(dve.tensor_tensor_scan(ends, tmp[:, 0:T], size, 0.0, ALU.mult, ALU.add))
            then(dve.tensor_tensor(offs, ends, size, ALU.subtract))
            then(dve.scalar_tensor_tensor(offs, ps[:, 7, 0:T], -1.0, offs, ALU.add, ALU.add))
            for b in range(T):
                m = dve.scalar_tensor_tensor(posb[:, b, :], cum[:, b, :], offs[:, b:b + 1], member[:, b, :],
                                             ALU.add, ALU.mult)
            then(m)
            then(dve.tensor_reduce(rowf, posb[:].rearrange("p b j -> p j b"), AX.X, ALU.add))
            pi = e_i[:, 0, :]
            part = e_i[:, 1, :]
            then(dve.tensor_copy(pi, rowf))
            then(dve.tensor_scalar(part, pi, TG * P - 1, 2, ALU.bitwise_and, ALU.arith_shift_right))
            then(dve.tensor_copy(tmp, part))
            then(dve.tensor_scalar(part, pi, 9, 2, ALU.arith_shift_right, ALU.logical_shift_left))
            then(dve.tensor_copy(loc, part))
            then(dve.scalar_tensor_tensor(rowf, tmp, float(SPP), loc, ALU.mult, ALU.add))
            then(dve.tensor_scalar(part, pi, TG - 1, None, ALU.bitwise_and))
            then(dve.tensor_copy(tmp, part))
            then(dve.tensor_tensor(rowf, rowf, tmp, ALU.add))
            then(dve.tensor_copy(tmp, pid_i[:]))
            then(dve.tensor_tensor(rowf, rowf, tmp, ALU.subtract))
            then(dve.tensor_tensor(rowf, rowf, ge[:, 0, :], ALU.mult))
            then(dve.tensor_tensor(rowf, rowf, tmp, ALU.add))
            dve.tensor_copy(idx[:], rowf).then_inc(S["edge_placed"], 1)
            then(dve.tensor_reduce(loc, ge[:, 1:T, :].rearrange("p b j -> p j b"), AX.X, ALU.add))
            dve.tensor_copy(pay[:, :, 1], dst_f)
            dve.scalar_tensor_tensor(pay[:, :, 0], loc, -float(P), src_f, ALU.mult, ALU.add)\
                .then_inc(S["edge_placed"], 1)
            then(dve.memset(block_f[:], 0.0))
            for b in range(T - 1):
                then(dve.scalar_tensor_tensor(block_f[:], giota[:], ends[:, b:b + 1], block_f[:], ALU.is_ge, ALU.add))
            then(dve.tensor_copy(block_i[:], block_f[:]))

            dve.wait_ge(S["prep_step"], 4)
            dve.scalar_tensor_tensor(rw16[:, :, 1, :], rw32[:], SW, rw16[:, :, 0, :], ALU.mult, ALU.subtract)\
                .then_inc(S["rw_lo"], 1)

            def norm_tile(src, dst, count, stat, var, rstd_sem, eps, done):
                settle(dve)
                for hh in range(2):
                    m = dve.bn_stats(stats[:, 0, 6 * hh:6 * hh + 6], src[:, hh * 512:(hh + 1) * 512])
                m.then_inc(S[stat], 1)
                dve.wait_ge(S[stat], 2 * count + 1)
                settle(dve)
                dve.bn_aggr(mv[:, 0, :], stats[:, 0, :]).then_inc(S[stat], 1)
                dve.wait_ge(S[stat], 2 * count + 2)
                dve.tensor_scalar(mv[:, 0, 1:2], mv[:, 0, 1:2], eps, None, ALU.add).then_inc(S[var], 1)
                dve.wait_ge(S[rstd_sem], count + 1)
                return dve.tensor_scalar(dst, src, mv[:, 0, 0:1], rstd[:, 0:1], ALU.subtract, ALU.mult)\
                    .then_inc(S[done], 1)

            def ln0_lo(c, j):
                dve.wait_ge(S["ln0_hi"], c + 1)
                dve.scalar_tensor_tensor(act_lo[:, :, ds(c * P, P)], banks(2 * j, 2).rearrange("p (k n) -> p k n", n=P),
                                         SX, act_hi[:, :, ds(c * P, P)], ALU.mult, ALU.subtract)\
                    .then_inc(S["ln0_lo"], 1)

            def ln0(c, j, conv):
                i = c // 2 if isinstance(c, int) else conv + 1
                dve.wait_ge(S[f"x_in{j}"], 16 * (i + 1))
                if not (isinstance(c, int) and c < 2):
                    dve.wait_ge(S["ln0_T"], c - 1)
                norm_tile(xin0[:, j, :], xn0[:, j, :], c, "ln0_stat", "ln0_var", "ln0_rstd", 1e-5, "ln0_done")
                if not (isinstance(c, int) and c == 0):
                    ln0_lo(c - 1, 1 - j)

            chunk_loop(dve, ln0)
            ln0_lo(T - 1, 1)

            with dve.Fori(0, 4) as i:
                diag_add(0, i)
                convert(0, i)
            dve.memset(zeros16[:], 0.0).then_inc(S["state_zero"], 1)
            dve.wait_ge(S["bv_scaled"], 1)

            for ph in range(4):
                kk, h = ph // 2, ph % 2

                def kv(c, j, conv, ph=ph, kk=kk, h=h):
                    g = T * ph + c
                    dve.wait_ge(S["kv_ready"], g + 1)
                    dve.scalar_tensor_tensor(kb[:, j, :], ps[:, 2 * j, :], 1.0 / (SW * SX),
                                             bk_bc[:, kk, h * 512:(h + 1) * 512], ALU.mult, ALU.add)\
                        .then_inc(S["k_biased"], 1)
                    dve.scalar_tensor_tensor(v16[:, j, :], ps[:, 2 * j + 1, :], 1.0 / SW,
                                             bv_bc[:, kk, h * 512:(h + 1) * 512], ALU.mult, ALU.add)\
                        .then_inc(S["v_scaled"], 1)
                    if conv is not None and j == 1:
                        diag_add(ph + 1, conv)
                    dve.wait_ge(S["k_sq"], g + 1)
                    dve.tensor_reduce(ssq[:, 0, 0:8], ksq[:, j, :].rearrange("p (a b) -> p a b", b=HD), AX.X, ALU.add)\
                        .then_inc(S["k_ssq"], 1)
                    dve.wait_ge(S["v_hi"], g + 1)
                    dve.tensor_tensor(v_lo_t[:, j, :], v16[:, j, :], v_hi_t[:, j, :], ALU.subtract)\
                        .then_inc(S["v_lo"], 1)
                    dve.wait_ge(S["k_nrm"], g + 1)
                    dve.tensor_scalar(nrm[:, 0, 0:8], nrm[:, 0, 0:8], 1e-6, None, ALU.add).then_inc(S["k_inv"], 1)
                    dve.wait_ge(S["k_inv"], 2 * (g) + 1)
                    dve.reciprocal(nrm[:, 0, 0:8], nrm[:, 0, 0:8]).then_inc(S["k_inv"], 1)
                    dve.wait_ge(S["k_inv"], 2 * g + 2)
                    dve.scalar_tensor_tensor(kb[:, j, :].rearrange("p (a b) -> p a b", b=HD),
                                             ks[:, j, :].rearrange("p (a b) -> p a b", b=HD), 0.5,
                                             nrm[:, 0, 0:8].unsqueeze(2).broadcast_to([P, 8, HD]),
                                             ALU.add, ALU.mult).then_inc(S["k_normed"], 1)
                    dve.wait_ge(S["k_hi"], g + 1)
                    dve.scalar_tensor_tensor(k_lo_t[:, j, :], kb[:, j, :], SX, k_hi_t[:, j, :], ALU.mult,
                                             ALU.subtract).then_inc(S["k_lo"], 1)
                    if conv is not None and j == 1:
                        convert(ph + 1, conv)

                chunk_loop(dve, kv)
                dve.wait_ge(S["state_mm"], T * (ph + 1))
                sb = ps[:, 4 + ph % 2, :]
                sc = 1.0 / (SX * SX * N)
                if kk == 0:
                    dve.tensor_scalar(st0[:, h, :], sb, sc, None, ALU.mult).then_inc(S["state_first"], 1)
                else:
                    dve.scalar_tensor_tensor(stp[:], sb, sc, st0[:, h, :], ALU.mult, ALU.mult)\
                        .then_inc(S["state_step"], 1)
                    dve.wait_ge(S["state_step"], 3 * h + 1)
                    dve.tensor_tensor(stp[:], stp[:], mask[:].rearrange("p a b -> p (a b)"), ALU.mult)\
                        .then_inc(S["state_step"], 1)
                    dve.wait_ge(S["state_step"], 3 * h + 2)
                    dve.tensor_copy(st_hi[:, h, :], stp[:]).then_inc(S["state_step"], 1)
                    dve.wait_ge(S["state_step"], 3 * h + 3)
                    dve.tensor_tensor(st_lo[:, h, :], stp[:], st_hi[:, h, :], ALU.subtract)\
                        .then_inc(S["state_lo"], 1)

            def q_body(c, j, conv):
                early = isinstance(c, int) and c < 2
                done = isinstance(c, int) and c >= T

                def evac(hh):
                    dve.wait_ge(S[f"q_ready{hh}"], c + 1)
                    dve.scalar_tensor_tensor(qb[:, hh * 512:(hh + 1) * 512], ps[:, hh, :], 1.0 / (SW * SX),
                                             bq_bc[:, hh * 512:(hh + 1) * 512], ALU.mult, ALU.add)\
                        .then_inc(S[f"q_biased{hh}"], 1)
                if not done:
                    evac(0)
                if not early:
                    dve.wait_ge(S["o_ready"], c - 1)
                    if not (isinstance(c, int) and c == 2):
                        dve.wait_ge(S["lnT_ready"], c - 2)
                    norm_tile(banks(4, 2), lnx[:], c - 2, "o_stat", "o_var", "o_rstd", 1e-5 * (SX * SS) ** 2, "o_normed")
                if not done:
                    evac(1)
                if not early:
                    dve.wait_ge(S["lnT_hi"], c - 1)
                    dve.tensor_tensor(ln_lo[:, :, ds(c * P - 2 * P, P)], lnf[:].rearrange("p (k n) -> p k n", n=P),
                                      ln_hi[:, :, ds(c * P - 2 * P, P)], ALU.subtract).then_inc(S["lnT_lo"], 1)
                if not (isinstance(c, int) and (c == 0 or c > T)):
                    dve.wait_ge(S["qT_hi"], c)
                    dve.scalar_tensor_tensor(qT_lo_t[:, 1 - j, :], banks(2, 2), SX, qT_hi_t[:, 1 - j, :], ALU.mult,
                                             ALU.subtract).then_inc(S["qT_lo"], 1)
                if not done:
                    dve.wait_ge(S["q_sq"], c + 1)
                    dve.tensor_reduce(ssq[:, 1, :], qb[:].rearrange("p (a b) -> p a b", b=HD), AX.X, ALU.add)\
                        .then_inc(S["q_ssq"], 1)
                    dve.wait_ge(S["q_nrm"], c + 1)
                    dve.tensor_scalar(nrm[:, 1, :], nrm[:, 1, :], 1e-6, None, ALU.add).then_inc(S["q_inv"], 1)
                    dve.wait_ge(S["q_inv"], 2 * c + 1)
                    dve.reciprocal(nrm[:, 1, :], nrm[:, 1, :]).then_inc(S["q_inv"], 1)
                    dve.wait_ge(S["q_inv"], 2 * c + 2)
                    dve.scalar_tensor_tensor(qn[:, j, :].rearrange("p (a b) -> p a b", b=HD),
                                             qs[:].rearrange("p (a b) -> p a b", b=HD), 0.5,
                                             nrm[:, 1, :].unsqueeze(2).broadcast_to([P, HEADS, HD]),
                                             ALU.add, ALU.mult).then_inc(S["q_normed"], 1)
                if conv is not None and j == 1:
                    convert(5, conv)

            q_loop(dve, q_body)

            dve.wait_ge(S["bsum_in"], 32)
            dve.tensor_tensor(bsum[:], bsum[:], mo[:, 1, :], ALU.add).then_inc(S["bsum_made"], 1)
            dve.wait_ge(S["bsum_made"], 1)

            def wo_body(c, j, conv):
                i = c // 2 if isinstance(c, int) else conv + 1
                dve.wait_ge(S["wo_ready"], c + 1)
                if not (isinstance(c, int) and c < 2):
                    dve.wait_ge(S[f"mixed_out{j}"], 16 * i)
                dve.scalar_tensor_tensor(mo[:, j, :], banks(2 * j, 2), 1.0 / (SW * SX), bsum[:], ALU.mult,
                                         ALU.add).then_inc(S["wo_biased"], 1)
                dve.wait_ge(S["wo_biased"], c + 1)
                dve.wait_ge(S[f"xin_in{j}"], 16 * (i + 1))
                dve.tensor_tensor(mo[:, j, :], mo[:, j, :], xin[:, j, :], ALU.add).then_inc(S["wo_x"], 1)
                if conv is not None and j == 1:
                    convert(6, conv)

            chunk_loop(dve, wo_body)

            dve.wait_ge(S["table_in"], 16)
            dve.wait_ge(S["adj_zero"], 1)
            for j in range(2):
                dve.wait_ge(S[f"mixed_out{j}"], 16 * T // 2)

            def one_hots(g, par, first):
                if not first:
                    dve.wait_ge(S["grp_ready"], g - 1)
                for t in range(TG):
                    col = TG * g + t
                    dve.tensor_scalar(src_1h[:, par, t, :], iota_s[:],
                                      edges[:, ds(col, 1), 0], None, ALU.is_equal)
                    m = dve.tensor_scalar(dst_1h[:, par, t, :], iota_d[:],
                                          edges[:, ds(col, 1), 1], None, ALU.is_equal)
                m.then_inc(S["onehot"], 1)

            def add_group(g, par):
                dve.wait_ge(S["grp_ready"], g + 1)
                if not (isinstance(g, int) and g == 0):
                    dve.wait_ge(S["grp_added"], g)
                blk = dve.value_load(block_i[0:1, ds(g, 1)], min_val=0, max_val=T - 1)
                row = adj[:, ds(blk, 1), 0:N].rearrange("p a n -> p (a n)")
                dve.tensor_tensor(row, banks(3 * par, 3, N), row, ALU.add).then_inc(S["grp_added"], 1)

            def z_low(c):
                dve.wait_ge(S["z_hi"], c + 1)
                at = lambda t: t[:, ds(c, 1), :].rearrange("p a d -> p (a d)")
                dve.scalar_tensor_tensor(at(z_lo), banks(6, 2), 1.0 / SW, at(z_hi), ALU.mult, ALU.subtract)\
                    .then_inc(S["z_lo"], 1)

            def z_body(c, j, conv):
                for q in range(5):
                    g = 5 * c + q
                    par = (5 * j + q) % 2
                    one_hots(g, par, isinstance(c, int) and g < 2)
                    if q == 0:
                        z_low(c)
                    if not (isinstance(c, int) and g == 0):
                        add_group(g - 1, 1 - par)
                if conv is not None and j == 1:
                    convert(7, conv)

            chunk_loop(dve, z_body)
            add_group(GROUPS - 1, 1)
            dve.wait_ge(S["deg_ready"], 1)
            dve.tensor_scalar(dinv[:], banks(0, 3, NP), 1.0, None, ALU.max).then_inc(S["dinv_max"], 1)
            dve.wait_ge(S["dinv_max"], 1)
            dve.reciprocal(dinv[:], dinv[:]).then_inc(S["dinv_made"], 1)
            dve.wait_ge(S["dcol_ready"], 1)
            dve.tensor_scalar(dinv_col[:], ps[:, 3, 0:T], 1.0 / SX, None, ALU.mult).then_inc(S["dcol_made"], 1)

            with dve.Fori(0, 4) as i:
                convert(8, i)
            dve.wait_ge(S["dinv_made"], 1)

            def h_chunk(o, i, j):
                dve.wait_ge(S["a_ready"], o + 1)
                dve.tensor_tensor(tg[:], banks(3 * j, 3, N), dinv[:, 0:N], ALU.mult).then_inc(S["a_scaled"], 1)
                dve.wait_ge(S["a_scaled"], o + 1)
                dve.wait_ge(S[f"s_in{j}"], 16 * (i + 1))
                dve.scalar_tensor_tensor(s0[:, j, :], s0[:, j, :], SX, tg[:], ALU.mult, ALU.add)\
                    .then_inc(S["a_sum"], 1)
                dve.wait_ge(S["h_hi"], o + 1)
                at = lambda t: t[:, ds(o, 1), 0:N].rearrange("p a n -> p (a n)")
                dve.scalar_tensor_tensor(at(act_lo), s0[:, j, :], 0.0, at(act_hi), ALU.max, ALU.subtract)\
                    .then_inc(S["h_lo"], 1)

            with dve.Fori(0, KC // 2) as i:
                h_chunk(2 * i, i, 0)
                h_chunk(2 * i + 1, i, 1)

            def z1_body(c, j, conv):
                dve.wait_ge(S["z1_hi"], c + 1)
                at = lambda t: t[:, ds(c, 1), :].rearrange("p a d -> p (a d)")
                dve.scalar_tensor_tensor(at(z_lo), banks(2 * j, 2), 1.0 / SW, at(z_hi), ALU.mult, ALU.subtract)\
                    .then_inc(S["z1_lo"], 1)
                if conv is not None and j == 1:
                    convert(9, conv)

            chunk_loop(dve, z1_body)

            def f_body(c, j, conv):
                i = c // 2 if isinstance(c, int) else conv + 1
                done = isinstance(c, int) and c >= T
                if not done:
                    dve.wait_ge(S["f_s"], c + 1)
                    dve.wait_ge(S[f"xm_in{j}"], 16 * (i + 1))
                    if not (isinstance(c, int) and c < 2):
                        dve.wait_ge(S[f"x1_out{j}"], 16 * i)
                    dve.scalar_tensor_tensor(x1[:, j, :], banks(0, 2), 1.0 / (SW * SX), xm[:, j, :], ALU.mult,
                                             ALU.add).then_inc(S["f_x1a"], 1)
                if not (isinstance(c, int) and c == 0):
                    dve.wait_ge(S["f_yhi"], c)
                    dve.scalar_tensor_tensor(act_lo[:, :, ds(c * P - P, P)],
                                             banks(4, 2).rearrange("p (k n) -> p k n", n=P), SX,
                                             act_hi[:, :, ds(c * P - P, P)], ALU.mult, ALU.subtract)\
                        .then_inc(S["f_ylo"], 1)
                if not done:
                    dve.wait_ge(S["f_g"], c + 1)
                    dve.wait_ge(S["f_x1a"], c + 1)
                    dve.scalar_tensor_tensor(x1[:, j, :], banks(2, 2), dinv_col[:, ds(c, 1)], x1[:, j, :], ALU.mult,
                                             ALU.add).then_inc(S["f_x1"], 1)
                    dve.wait_ge(S["f_x1"], c + 1)
                    if not (isinstance(c, int) and c < 2):
                        dve.wait_ge(S[f"y_out{j}"], 16 * i)
                    norm_tile(x1[:, j, :], yb[:, j, :], c, "f_stat", "f_var", "f_rstd", 1e-5, "f_y")
                if conv is not None and j == 1:
                    convert(10, conv)

            chunk_loop(dve, f_body)
            f_body(T, 0, None)

            dve.wait_ge(S["f_lg"], T)
            L, one1, rest, one2, tmp8, cwv = (lg[:, n] for n in range(6))
            v1, dv, ex, v2, w1v, w2v = (sel[:, n, :] for n in range(6))
            bc = lambda a: a.unsqueeze(2).broadcast_to([P, T, EXPERTS])

            def first_largest(src, best, onehot):
                then(dve.tensor_reduce(best, src, AX.X, ALU.max))
                then(dve.tensor_tensor(tmp8, src, bc(best), ALU.is_equal))
                for e in range(EXPERTS):
                    m = dve.tensor_scalar(tmp8[:, :, e], tmp8[:, :, e], float(EXPERTS - e), None, ALU.mult)
                then(m)
                then(dve.tensor_reduce(w1v, tmp8, AX.X, ALU.max))
                then(dve.tensor_tensor(onehot, tmp8, bc(w1v), ALU.is_equal))

            then(dve.scalar_tensor_tensor(L, ps[:, 6, 0:T * EXPERTS].rearrange("p (t e) -> p t e", e=EXPERTS),
                                          1.0 / (SW * SX), rb[:].unsqueeze(1).broadcast_to([P, T, EXPERTS]),
                                          ALU.mult, ALU.add))
            first_largest(L, v1, one1)
            then(dve.scalar_tensor_tensor(rest, one1, -1e30, L, ALU.mult, ALU.add))
            first_largest(rest, v2, one2)
            dve.tensor_tensor(dv, v2, v1, ALU.subtract).then_inc(S["r_step"], 1)
            dve.wait_ge(S["r_exp"], 1)
            then(dve.tensor_scalar(w2v, ex, 1.0, None, ALU.add))
            then(dve.reciprocal(w1v, w2v))
            then(dve.tensor_tensor(w2v, ex, w1v, ALU.mult))
            dve.tensor_tensor(one1, one1, bc(w1v), ALU.mult)
            then(dve.tensor_tensor(one2, one2, bc(w2v), ALU.mult))
            then(dve.tensor_tensor(cwv, one1, one2, ALU.add))
            dve.tensor_scalar(cws[:], cwv, 1.0 / (SW * SX), None, ALU.mult).then_inc(S["r_done"], 1)

            dve.wait_ge(S["cwT_ready"], 1)
            dve.tensor_copy(cwT[:], ps[0:EXPERTS, 0:3, :].rearrange("p b n -> p (b n)")[:, 0:NP])\
                .then_inc(S["cwT_made"], 1)
            dve.wait_ge(S["acc_in"], 16)
            for t in range(T):
                dve.wait_ge(S["b2_ready"], t + 1)
                dve.tensor_tensor(acc[:, t, :], banks(4 + 2 * (t % 2), 2), acc[:, t, :], ALU.add)\
                    .then_inc(S["b2_added"], 1)
            dve.wait_ge(S["b2_ready"], T)
            dve.memset(gelu_hi[:, :, N:NP], 0.0)
            dve.memset(gelu_lo[:, :, N:NP], 0.0).then_inc(S["gpad"], 1)

            def finish(c, j, conv):
                i = c // 2 if isinstance(c, int) else conv
                if not (isinstance(c, int) and c < 2):
                    dve.wait_ge(S[f"out{j}"], 16 * i)
                dve.wait_ge(S["y_added"], 2 * T * 7 + 2 * c + 2)
                norm_tile(acc[:, ds(c, 1), :].rearrange("p a d -> p (a d)"), fin[:, j, :], c, "e_stat", "e_var",
                          "e_rstd", 1e-12, "e_n")
                dve.wait_ge(S["e_n"], c + 1)
                dve.tensor_tensor(fin[:, j, :], fin[:, j, :], lnw_bc[:], ALU.mult).then_inc(S["e_affine"], 1)
                dve.wait_ge(S["e_affine"], 2 * c + 1)
                dve.tensor_tensor(fin[:, j, :], fin[:, j, :], lnb_bc[:], ALU.add).then_inc(S["e_affine"], 1)
                dve.wait_ge(S["e_affine"], 2 * c + 2)
                dve.wait_ge(S[f"x1_in{j}"], 16 * (i + 1))
                dve.tensor_tensor(fin[:, j, :], fin[:, j, :], x1in[:, j, :], ALU.add).then_inc(S["e_x"], 1)

            def expert(e, par, first, last):
                for tile, (c0, w_) in enumerate(COLS):
                    for f in range(4):
                        n = 12 * e + 4 * tile + f
                        dve.wait_ge(S["g_hi"], n + 1)
                        dve.scalar_tensor_tensor(gelu_lo[:, f, c0:c0 + w_], g32[:, f % 2, 0:w_], SX,
                                                 gelu_hi[:, f, c0:c0 + w_], ALU.mult, ALU.subtract)\
                            .then_inc(S["g_lo"], 1)

                def add_expert(c, j):
                    for hh in range(2):
                        n = 20 * e + 2 * c + hh
                        dve.wait_ge(S["y_ready"], n + 1)
                        a = acc[:, ds(c, 1), hh * 512:(hh + 1) * 512].rearrange("p a d -> p (a d)")
                        dve.scalar_tensor_tensor(a, ps[:, 4 + 2 * j + hh, :],
                                                 cws[:, ds(c, 1), ds(e, 1)].rearrange("p a b -> p (a b)"), a,
                                                 ALU.mult, ALU.add).then_inc(S["y_added"], 1)

                if last:
                    dve.wait_ge(S["lnwb_in"], 32)
                    for j in range(2):
                        add_expert(j, j)
                        finish(j, j, 0)
                    with dve.Fori(1, T // 2) as i:
                        for j in range(2):
                            add_expert(2 * i + j, j)
                            finish(2 * i + j, j, i)
                    return
                with dve.Fori(0, 4) as i:
                    for j in range(2):
                        add_expert(2 * i + j, j)
                    for j in range(2):
                        dve.wait_ge(S["w_hi"], 8 * (e + 11) + 2 * i + j + 1)
                        slot = 8 * (1 - par) + 4 * j
                        at = lambda part: wslot[:, ds(slot + i, 1), part, :].rearrange("p a d -> p (a d)")
                        dve.scalar_tensor_tensor(at(1), stage[:, j, :], SW, at(0), ALU.mult, ALU.subtract)\
                            .then_inc(S["w_lo"], 1)
                for j in range(2):
                    add_expert(8 + j, j)

            expert_loop(dve, expert)


def unit(w, order):
    import numpy as np
    v = w.reshape(KC, P, 512)[order].reshape(4, 2, P, 512)
    return np.ascontiguousarray(v.transpose(0, 2, 1, 3)).reshape(4, P, D)


def kernel(**inputs):
    import numpy as np
    import concourse.bacc as bacc
    from concourse import mybir as mb
    from concourse.bass_utils import run_bass_kernel_spmd

    g = {k.replace("L0_", ""): np.asarray(v) for k, v in inputs.items()}
    x = np.zeros((NP, D), np.float32)
    x[:N] = g["x"]

    def edge_grid(e):
        v = np.full(EJ * P, -1, np.int32)
        v[:E] = e
        return np.ascontiguousarray(v.reshape(EJ, P).T)

    units = []
    for kk in range(2):
        for h in range(2):
            for name in ("mix_Wk", "mix_Wv"):
                units.append(unit(g[name][kk].T[:, h * 512:(h + 1) * 512], DIAG[h]))
    for w, orders in ((g["mix_Wq"].T, DIAG), (g["mix_Wo"].T, (PLAIN, PLAIN)), (g["gnn_W_neigh0"], (PLAIN, PLAIN)),
                      (g["gnn_W_self0"], (PLAIN, PLAIN)), (g["gnn_W_neigh1"], (PLAIN, PLAIN)),
                      (g["gnn_W_self1"], (PLAIN, PLAIN))):
        for h in range(2):
            units.append(unit(w[:, h * 512:(h + 1) * 512], orders[h]))
    for e in range(EXPERTS):
        units.append(unit(g["ffn_w1"][e].T, PLAIN))
        units.append(np.ascontiguousarray(g["ffn_w2"][e].T).reshape(4, P, D))

    def columns(v):
        return v.reshape(-1, P).T

    arrays = {
        "x": x, "edge_src": edge_grid(g["src"]), "edge_dst": edge_grid(g["dst"]),
        "weights": np.concatenate(units),
        "rows": np.stack([g["mix_bq"], g["mix_bk"][0], g["mix_bk"][1], g["mix_bv"][0], g["mix_bv"][1], g["gnn_b1"],
                          g["mix_bo"], g["ffn_ln_w"], g["ffn_ln_b"]]),
        "cols": np.stack([columns(g["gnn_b0"]), columns(g["mix_ln_g"]), columns(g["mix_ln_b"])], axis=1),
        "b1col": columns(g["ffn_b1"]),
        "router": g["ffn_router_w"].T.reshape(KC, P, EXPERTS).transpose(1, 0, 2),
        "router_b": g["ffn_router_b"], "b2": g["ffn_b2"],
    }
    arrays = {k: np.ascontiguousarray(v) for k, v in arrays.items()}
    nc = bacc.Bacc("TRN2", target_bir_lowering=False, num_devices=1)
    aps = [nc.dram_tensor("in_" + k, v.shape, mb.dt.from_np(v.dtype), kind="ExternalInput").ap()
           for k, v in arrays.items()]
    aps.append(nc.dram_tensor("out_y", (NP, D), mb.dt.float32, kind="ExternalOutput").ap())
    program(nc, *aps)
    r = run_bass_kernel_spmd(nc, [{"in_" + k: v for k, v in arrays.items()}], core_ids=[0])
    return r.results[0]["out_y"][:N]
```

```python
from contextlib import ExitStack

import concourse.bass as bass
from concourse import mybir

ALU = mybir.AluOpType
ACT = mybir.ActivationFunctionType
F32 = mybir.dt.float32
F16 = mybir.dt.float16
I32 = mybir.dt.int32
U32 = mybir.dt.uint32
AX = mybir.AxisListType

P = 128
N = 1250
T = -(-N // P)
NP = T * P
LAST = N - (T - 1) * P
D = 1024
KC = D // P
HD = 64
HEADS = D // HD
E = 20000
EJ = 160
TG = 4
GROUPS = 50
SPP = GROUPS * TG
ROWS = P * SPP
EXPERTS = 8
FF = 512
DENSE = 10
TOP = 2
MOE_GROUPS = TOP * N // (2 * P) + EXPERTS
MOE_TILES = 2 * MOE_GROUPS
EDGE_COPIES = 2 * EJ
SW = 256.0
SX = 16.0
SS = 4096.0
COLS = [(0, 512), (512, 512), (1024, N - 1024)]
assert GROUPS >= E // (TG * P) + T and GROUPS == 5 * T

PLAIN = list(range(KC))
DIAG = [[4 * h + q + d * (4 if h == 0 else -4) for q in range(4) for d in (0, 1)] for h in (0, 1)]


def program(nc, x, edge_src, edge_dst, weights, rows, cols, b1col, router, router_b, b2, out):
    x_t = x.rearrange("(t p) d -> p t d", p=P)
    out_t = out.rearrange("(t p) d -> p t d", p=P)
    with ExitStack() as ctx:
        dram = lambda name, shape: nc.dram_tensor(name, shape, F32, kind="Internal").ap()
        bucket_rows = dram("bucket_rows", [ROWS + P * (EJ - E // P), 2])
        mixed = dram("mixed", [NP, D]).rearrange("(t p) d -> p t d", p=P)
        selfT = dram("selfT", [D, N]).rearrange("(o p) n -> p o n", p=P)
        x1_d = dram("x1", [NP, D]).rearrange("(t p) d -> p t d", p=P)
        y_rows = dram("y", [NP, D])
        y_d = y_rows.rearrange("(t p) d -> p t d", p=P)
        moe_rows = dram("moe_rows", [MOE_TILES * P, D])

        top = [-(-nc.sbuf_base // 64) * 64]

        def region(nbytes):
            at = top[0]
            top[0] += -(-nbytes // 64) * 64
            return at

        def put(name, shape, dt, at):
            return nc.alloc_sbuf_tensor_at(name, shape, dt, offset=at)

        r1, r2 = region(4 * KC * NP), region(4 * KC * NP)
        r_adj = region(2 * T * NP)
        r_slot, r_stage = region(4 * 4 * 4096), region(2 * 4 * D)

        def small(name, shape, dt=F32):
            n = 1
            for s in shape[1:]:
                n *= s
            at = region(n * (2 if dt == F16 else 4))
            return put(name, shape, dt, at)

        act_hi = put("act_hi", [P, KC, NP], F16, r1)
        act_lo = put("act_lo", [P, KC, NP], F16, r1 + 2 * KC * NP)
        ln_hi = put("ln_hi", [P, KC, NP], F16, r2)
        ln_lo = put("ln_lo", [P, KC, NP], F16, r2 + 2 * KC * NP)
        z_hi = put("z_hi", [P, T, D], F16, r2)
        z_lo = put("z_lo", [P, T, D], F16, r2 + 2 * T * D)
        acc = put("acc", [P, T, D], F32, r2)
        adj = put("adj", [P, T, NP], F16, r_adj)
        wslot = put("wslot", [P, 16, 2, D], F16, r_slot)
        stage = put("stage", [P, 2, D], F32, r_stage)

        ident = small("ident", [P, P])
        colv = small("colv", [P, 4, KC])
        b1c = small("b1c", [P, EXPERTS * 4])
        rw16 = small("rw16", [P, KC, 2, EXPERTS], F16)
        rb = small("rb", [P, EXPERTS])
        dinv_col = small("dinv_col", [P, T])
        stats = small("stats", [P, 2, 12])
        mv = small("mv", [P, 2, 2])
        rstd = small("rstd", [P, 2])
        ssq = put("ssq", [P, 2, HEADS], F32, r_adj + 4 * 6 * D)
        nrm = put("nrm", [P, 2, HEADS], F32, r_adj + 4 * 6 * D + 4 * 2 * HEADS)
        half_pow = small("half_pow", [P, HEADS])
        mhalf_pow = small("mhalf_pow", [P, 2])
        halfc = small("halfc", [P, 1])
        r_late = top[0]
        ones16 = small("ones16", [P, P], F16)
        block_f = small("block_f", [P, GROUPS])
        block_i = small("block_i", [P, GROUPS], I32)
        colraw = small("colraw", [P, 3, KC])
        rw32 = small("rw32", [P, KC, EXPERTS])
        iota_d = small("iota_d", [P, N], F16)
        edges = small("edges", [P, SPP, 2])
        r_work = top[0]

        class Work:
            def __init__(self, at, end):
                self.at, self.end = at, end

            def __call__(self, name, shape, dt=F32):
                n = 1
                for s in shape[1:]:
                    n *= s
                t = put(name, shape, dt, self.at)
                self.at += -(-n * (2 if dt == F16 else 4) // 64) * 64
                assert self.at <= self.end, (name, self.at, self.end)
                return t

        end = nc.sbuf_usable_end
        w = Work(r2, r_adj)
        xin0 = w("xin0", [P, 2, D])
        xn0 = w("xn0", [P, 2, D])
        w = Work(r_slot + 2 * 4 * 4096, r_stage)
        ge = w("ge", [P, T + 1, EJ])
        member = w("member", [P, T, EJ])
        cum = w("cum", [P, T, EJ])
        posb = w("posb", [P, T, EJ])
        e_i = w("e_i", [P, 2, EJ], I32)
        w = Work(r2, r_adj)
        kb = w("kb", [P, 2, 512])
        ks = w("ks", [P, 2, 512])
        ksq = w("ksq", [P, 2, 512])
        v16 = w("v16", [P, 2, 512])
        k_hi_t, k_lo_t, v_hi_t, v_lo_t = (w(n, [P, 2, 512], F16) for n in ("k_hi", "k_lo", "v_hi", "v_lo"))
        bk_bc = w("bk_bc", [P, 2, D])
        bv_bc = w("bv_bc", [P, 2, D])
        w = Work(r_work, end)
        st0 = w("st0", [P, 2, 512])
        stp = w("stp", [P, 512])
        zeros16 = w("zeros16", [P, 512], F16)
        idx = w("idx", [P, EJ], I32)
        pay = w("pay", [P, EJ, 2])
        idx_b = w("idx_b", [P, 4, 1], I32)
        pay_b = w("pay_b", [P, 4, 2])
        st_hi = w("st_hi", [P, 2, 512], F16)
        st_lo = w("st_lo", [P, 2, 512], F16)
        mask = w("mask", [P, 4, P])
        bq_bc = w("bq_bc", [P, D])
        w = Work(r_adj, r_slot)
        es = w("es", [P, 5, EJ])
        e_small = w("e_small", [P, 5, 16])
        ei_small = w("ei_small", [P, 16], I32)
        upper = w("upper", [P, P])
        ones32 = w("ones32", [P, P])
        minus1 = w("minus1", [P, 2 * SPP])
        iota_i = w("iota_i", [P, N], I32)
        giota_i = w("giota_i", [P, GROUPS], I32)
        giota = w("giota", [P, GROUPS])
        pid_i = w("pid_i", [P, EJ], I32)
        lnx = put("lnx", [P, D], F32, r_work)
        lnf = put("lnf", [P, D], F32, r_work + 4 * D)
        w = Work(r_adj, r_slot)
        qn = w("qn", [P, 2, D])
        qT_hi_t = w("qT_hi", [P, 2, D], F16)
        qT_lo_t = w("qT_lo", [P, 2, D], F16)
        qb = w("qb", [P, D])
        qs = w("qs", [P, D])
        w = Work(r_work, end)
        bsum = w("bsum", [P, D])
        xin = w("xin", [P, 2, D])
        mo = w("mo", [P, 2, D])
        w = Work(r_work, end)
        dst_1h = w("dst_1h", [P, 2, TG, N], F16)
        src_1h = w("src_1h", [P, 2, TG, P], F16)
        counts = w("counts", [P, N], F16)
        w = Work(r_work, end)
        dinv = w("dinv", [P, NP])
        s0 = w("s0", [P, 2, N])
        tg = w("tg", [P, N])
        w = Work(r_late, end)
        xm = w("xm", [P, 2, D])
        x1 = w("x1b", [P, 2, D])
        yb = w("yb", [P, 2, D])
        lnb_bc = w("lnb_bc", [P, D])
        w = Work(r_adj, r_slot)
        lg = w("lg", [P, 6, T, EXPERTS])
        sel = w("sel", [P, 6, T])
        mrank = w("mrank", [P, 4, EXPERTS, T])
        msmall = w("msmall", [P, 6, EXPERTS])
        msmall_i = w("msmall_i", [P, EXPERTS], I32)
        mgroup = w("mgroup", [P, 2, MOE_GROUPS])
        mpos = w("mpos", [P, 3, TOP, T])
        mpos_i = w("mpos_i", [P, 2, TOP, T], I32)
        node_f = w("node_f", [P, T])
        reset = w("reset", [P, EXPERTS, T])
        count_down = w("count_down", [P, EXPERTS])
        upper2 = w("upper2", [P, P])
        ones2 = w("ones2", [P, P])
        iota_m = w("iota_m", [P, P])
        row_1h = w("row_1h", [P, TOP, T, P], F16)
        tile_1h = w("tile_1h", [P, TOP, T, MOE_TILES], F16)
        assert w.at <= r_adj + 4 * 6 * D
        w = Work(r1, r2)
        xg = w("xg", [P, 2, 2, D])
        xT_hi_t = w("xT_hi", [P, 2, KC, 2 * P], F16)
        xT_lo_t = w("xT_lo", [P, 2, KC, 2 * P], F16)
        gelu_hi = w("gelu_hi", [P, 4, 2 * P], F16)
        gelu_lo = w("gelu_lo", [P, 4, 2 * P], F16)
        g32 = w("g32", [P, 2, 2 * P])
        w = Work(r_adj, r_slot)
        yo = w("yo", [P, 2, 2, D])
        b2_bc = w("b2_bc", [P, 2, D])
        cw = w("cw", [P, TOP, T])
        slot_i = w("slot_i", [P, TOP, T], I32)
        expert_i = w("expert_i", [P, MOE_GROUPS], I32)
        node_i = w("node_i", [P, MOE_TILES], I32)
        gidx = w("gidx", [P, 4, 1], I32)
        nmr = w("nmr", [P, 2])
        w = Work(r_late, end)
        lnw_bc = w("lnw_bc", [P, D])
        stage2 = w("stage2", [P, 2, D])
        x1in = w("x1in", [P, 2, D])
        w = Work(r1, r2)
        yg = w("yg", [P, 2, TOP, D])
        fin = w("fin", [P, 2, D])

        ps = ctx.enter_context(nc.psum_tensor("ps", [P, 8, 512], F32))

        def banks(b, n, width=None):
            v = ps[:, b:b + n, :].rearrange("p b n -> p (b n)")
            return v if width is None else v[:, 0:width]

        names = """x_in0 x_in1 consts_in cols_in const_made edge_in rank_step minus_out edge_tot edge_placed
            totals_made ln0_var ln0_rstd ln0_done ln0_T ln0_hi ln0_lo stage_in0 stage_in1 diag_added w_hi
            w_lo k_biased v_scaled kv_ready k_silu k_sq v_hi v_lo k_ssq k_nrm k_inv k_normed k_hi k_lo
            state_mm state_first state_step state_lo zeros_made scat0 scat1 scat2 scat3 table_in q_ready0
            q_ready1 q_biased0 q_biased1 q_silu q_sq q_ssq q_nrm q_inv q_normed qT_ready qT_hi qT_lo
            o_ready o_stat o_var o_rstd o_normed lnT_ready lnT_f lnT_hi lnT_lo wo_ready wo_biased wo_x
            zp_ready z_hi z_lo onehot grp_ready grp_copied grp_added deg_ready dinv_made dcol_ready dcol_made s_ready
            s_biased s_out0 s_out1 s_in0 s_in1 a_ready a_scaled a_sum h_hi h_lo f_s f_g f_x1a f_x1 f_stat
            f_var f_rstd f_y f_T f_yhi f_ylo f_lg rw_lo r_step r_exp acc_in r_const r_tot r_before
            experts_made r_1h nodes_ready nodes_made stage_in2 stage_in3 xg_in00 xg_in01 xg_in10 xg_in11
            x_T xT_hi xT_lo g_ready g_gelu g_hi g_lo y_ready y_evac b2_in0 b2_in1 yo_out0 yo_out1 x1_plus
            e_nmr e_n e_w e_x prep_step ln0_stat passed res_in0 res_in1 res_out0 res_out1 rows_out0
            rows_out1 e_sum idx_copied bias_in xin_in0 xin_in1 out0 out1 x1_in0 x1_in1""".split()
        S = {n: ctx.enter_context(nc.semaphore(n)) for n in names}
        block = ctx.enter_context(nc.Block())
        ds = bass.ds

        def chunk_loop(eng, body):
            body(0, 0, None)
            body(1, 1, None)
            with eng.Fori(1, T // 2) as i:
                body(2 * i, 0, i - 1)
                body(2 * i + 1, 1, i - 1)

        def settle(eng):
            eng.sem_inc(S["passed"], 1)

        def q_loop(eng, body):
            for c in range(4):
                body(c, c % 2, None if c < 2 else 0)
            with eng.Fori(2, T // 2) as i:
                body(2 * i, 0, i - 1)
                body(2 * i + 1, 1, i - 1)
            body(T, 0, None)
            body(T + 1, 1, None)

        def group_loop(eng, body):
            body(0, 0, False)
            body(1, 1, False)
            with eng.Fori(1, MOE_GROUPS // 2) as i:
                body(2 * i, 0, False)
                body(2 * i + 1, 1, False)
            body(MOE_GROUPS - 1, 0, True)

        @block.sync
        def _(sp):
            def stage_load(batch, i, j):
                if batch == 0 and isinstance(i, int) and i == 0:
                    pass
                else:
                    sp.wait_ge(S["w_lo"], 8 * batch + 2 * i + j - 1)
                sp.dma_start(stage[:, j, :], weights[ds(8 * batch + 4 * j + i, 1)].rearrange("a p d -> p (a d)")).then_inc(S[f"stage_in{j}"], 16)

            def batch_load(batch):
                if batch == 0:
                    for j in range(2):
                        stage_load(0, 0, j)
                    with sp.Fori(1, 4) as i:
                        for j in range(2):
                            stage_load(0, i, j)
                else:
                    with sp.Fori(0, 4) as i:
                        for j in range(2):
                            stage_load(batch, i, j)

            sp.dma_start(e_i[:, 0, :], edge_src).then_inc(S["edge_in"], 16)
            sp.dma_start(e_i[:, 1, :], edge_dst).then_inc(S["edge_in"], 16)
            for c in range(2):
                sp.dma_start(xin0[:, c, :], x_t[:, c, :]).then_inc(S[f"x_in{c}"], 16)
            sp.dma_start(colraw[:], cols).then_inc(S["cols_in"], 16)
            sp.dma_start(b1c[:], b1col).then_inc(S["cols_in"], 16)
            sp.dma_start(rw32[:], router).then_inc(S["cols_in"], 16)
            sp.dma_start(rb[:], router_b.partition_broadcast(P)).then_inc(S["cols_in"], 16)
            sp.dma_start(bq_bc[:], rows[0].partition_broadcast(P)).then_inc(S["consts_in"], 16)
            with sp.Fori(1, T // 2) as i:
                for j in range(2):
                    sp.wait_ge(S["ln0_done"], 2 * i + j - 1)
                    sp.dma_start(xin0[:, j, :], x_t[:, ds(2 * i + j, 1), :].rearrange("p a d -> p (a d)"))\
                      .then_inc(S[f"x_in{j}"], 16)
            batch_load(0)
            sp.wait_ge(S["ln0_lo"], T)
            for k in range(2):
                sp.dma_start(bk_bc[:, k, :], rows[1 + k].partition_broadcast(P)).then_inc(S["consts_in"], 16)
                sp.dma_start(bv_bc[:, k, :], rows[3 + k].partition_broadcast(P)).then_inc(S["consts_in"], 16)
            for batch in range(1, DENSE + 1):
                batch_load(batch)
            sp.wait_ge(S["experts_made"], 1)
            sp.wait_ge(S["w_lo"], 8 * (DENSE + 1))
            sp.wait_ge(S["nodes_made"], 1)
            for j in range(2):
                sp.wait_ge(S[f"res_out{j}"], 16 * T)
            for j in range(2):
                sp.dma_start(x1in[:, j, :], x1_d[:, j, :]).then_inc(S[f"x1_in{j}"], 16)
            sp.dma_start(b2_bc[:, 0, :], b2[0].partition_broadcast(P)).then_inc(S["b2_in0"], 16)

            def group_load(g, par, last):
                if last:
                    return
                e = sp.value_load(expert_i[0:1, ds(g + 1, 1)], min_val=0, max_val=EXPERTS - 1)
                for i in range(4):
                    for j in range(2):
                        buf = (2 * i + j) % 4
                        if not (isinstance(g, int) and g == 0 and i < 2):
                            sp.wait_ge(S["w_lo"], 8 * g + 8 * (DENSE + 1) + 2 * i + j - 3)
                        t = stage[:, buf, :] if buf < 2 else stage2[:, buf - 2, :]
                        sp.dma_start(t, weights[ds(8 * e + (8 * DENSE + 4 * j + i), 1)].rearrange("a p d -> p (a d)"))\
                            .then_inc(S[f"stage_in{buf}"], 16)
                if not (isinstance(g, int) and g < 1):
                    sp.wait_ge(S["y_evac"], 4 * g)
                sp.dma_start(b2_bc[:, 1 - par, :], b2[ds(e, 1), :].rearrange("a d -> (a d)").partition_broadcast(P))\
                    .then_inc(S[f"b2_in{1 - par}"], 16)

            group_loop(sp, group_load)

            def end_move(c, i, j, last):
                sp.wait_ge(S["e_x"], c + 1)
                sp.dma_start(out_t[:, ds(c, 1), :].rearrange("p a d -> p (a d)"), fin[:, j, :])\
                    .then_inc(S[f"out{j}"], 16)
                if not last:
                    sp.dma_start(x1in[:, j, :], x1_d[:, ds(c + 2, 1), :].rearrange("p a d -> p (a d)"))\
                        .then_inc(S[f"x1_in{j}"], 16)

            with sp.Fori(0, T // 2 - 1) as i:
                for j in range(2):
                    end_move(2 * i + j, i, j, False)
            for j in range(2):
                end_move(T - 2 + j, None, j, True)
            for j in range(2):
                sp.wait_ge(S[f"out{j}"], 16 * T // 2)

        @block.gpsimd
        def _(pool):
            pool.memset(minus1[:], -1.0).then_inc(S["zeros_made"], 1)
            pool.memset(ident[:], 0.0).then_inc(S["zeros_made"], 1)
            pool.memset(ones32[:], 1.0).then_inc(S["zeros_made"], 1)
            pool.memset(upper[:], 0.0).then_inc(S["zeros_made"], 1)
            pool.wait_ge(S["zeros_made"], 4)
            pool.affine_select(out=ident[:], in_=ident[:], compare_op=ALU.not_equal, fill=1.0, base=0,
                               pattern=[[-1, P]], channel_multiplier=1).then_inc(S["const_made"], 1)
            pool.affine_select(out=upper[:], in_=ones32[:], compare_op=ALU.is_gt, fill=0.0, base=0,
                               pattern=[[1, P]], channel_multiplier=-1).then_inc(S["const_made"], 1)
            pool.memset(ones16[:], 1.0).then_inc(S["const_made"], 1)
            pool.memset(half_pow[:], 0.5).then_inc(S["const_made"], 1)
            pool.memset(mhalf_pow[:], -0.5).then_inc(S["const_made"], 1)
            pool.memset(halfc[:], 0.5).then_inc(S["const_made"], 1)
            pool.iota(iota_i[:], pattern=[[1, N]], base=0, channel_multiplier=0).then_inc(S["const_made"], 1)
            pool.iota(giota_i[:], pattern=[[TG * P, GROUPS]], base=0, channel_multiplier=0)\
                .then_inc(S["const_made"], 1)
            pool.iota(pid_i[:], pattern=[[P, EJ]], base=ROWS - P * (E // P), channel_multiplier=1).then_inc(S["const_made"], 1)
            pool.wait_ge(S["zeros_made"], 1)
            pool.dma_start(bucket_rows[0:ROWS, :].rearrange("(p s) c -> p (s c)", p=P), minus1[:])\
                .then_inc(S["minus_out"], 16)
            pool.wait_ge(S["const_made"], 9)
            with pool.Fori(0, T) as c:
                pool.wait_ge(S["ln0_var"], c + 1)
                pool.tensor_tensor(rstd[:, 0:1], mv[:, 0, 1:2], mhalf_pow[:, 0:1], ALU.pow).then_inc(S["ln0_rstd"], 1)

            pool.wait_ge(S["edge_placed"], 2)
            pool.wait_ge(S["minus_out"], 16)

            def kv(g):
                pool.wait_ge(S["k_ssq"], g + 1)
                pool.tensor_tensor(nrm[:, 0, 0:8], ssq[:, 0, 0:8], half_pow[:, 0:8], ALU.pow).then_inc(S["k_nrm"], 1)

            def place(g, first):
                for q in range(4):
                    if not first:
                        pool.wait_ge(S[f"scat{q}"], 16 * g)
                    pool.tensor_copy(idx_b[:, q, :], idx[:, ds(4 * g + q, 1)]).then_inc(S["idx_copied"], 1)
                    pool.tensor_copy(pay_b[:, q, :], pay[:, ds(4 * g + q, 1), :].rearrange("p a c -> p (a c)"))\
                        .then_inc(S["idx_copied"], 1)
                    pool.wait_ge(S["idx_copied"], 8 * g + 2 * q + 2)
                    settle(pool)
                    pool.indirect_dma_start(
                        out=bucket_rows, out_offset=bass.IndirectOffsetOnAxis(ap=idx_b[:, q, :].bitcast(U32), axis=0),
                        in_=pay_b[:, q, :], in_offset=None).then_inc(S[f"scat{q}"], 16)

            kv(0)
            place(0, True)
            with pool.Fori(1, 4 * T) as g:
                kv(g)
                place(g, False)
            for q in range(4):
                pool.wait_ge(S[f"scat{q}"], 16 * 4 * T)
            pool.dma_start(edges[:].rearrange("p s c -> p (s c)"),
                           bucket_rows[0:ROWS, :].rearrange("(p s) c -> p (s c)", p=P)).then_inc(S["table_in"], 16)

            def q_body(c, j, conv):
                if not (isinstance(c, int) and c < 2):
                    pool.wait_ge(S["o_var"], c - 1)
                    pool.tensor_tensor(rstd[:, 0:1], mv[:, 0, 1:2], mhalf_pow[:, 0:1], ALU.pow).then_inc(S["o_rstd"], 1)
                if not (isinstance(c, int) and c >= T):
                    pool.wait_ge(S["q_ssq"], c + 1)
                    pool.tensor_tensor(nrm[:, 1, :], ssq[:, 1, :], half_pow[:], ALU.pow).then_inc(S["q_nrm"], 1)

            q_loop(pool, q_body)

            pool.wait_ge(S["lnT_lo"], T)
            pool.dma_start(bsum[:], rows[5].partition_broadcast(P)).then_inc(S["bias_in"], 16)
            pool.dma_start(mo[:, 1, :], rows[6].partition_broadcast(P)).then_inc(S["bias_in"], 16)
            pool.memset(adj[:], 0.0).then_inc(S["zeros_made"], 1)
            for j in range(2):
                pool.dma_start(xin[:, j, :], x_t[:, j, :]).then_inc(S[f"xin_in{j}"], 16)

            def wo_body(c, j, conv):
                pool.wait_ge(S["wo_x"], c + 1)
                pool.dma_start(mixed[:, ds(c, 1), :].rearrange("p a d -> p (a d)"), mo[:, j, :])\
                    .then_inc(S[f"res_out{j}"], 16)

            def wo_load(c, j):
                pool.dma_start(xin[:, j, :], x_t[:, ds(c, 1), :].rearrange("p a d -> p (a d)"))\
                    .then_inc(S[f"xin_in{j}"], 16)

            with pool.Fori(0, T // 2 - 1) as i:
                for j in range(2):
                    wo_body(2 * i + j, j, None)
                    wo_load(2 * i + j + 2, j)
            wo_body(T - 2, 0, None)
            wo_body(T - 1, 1, None)

            with pool.Fori(0, KC // 2) as i:
                for j in range(2):
                    pool.wait_ge(S["s_biased"], 2 * i + j + 1)
                    pool.dma_start(selfT[:, ds(2 * i + j, 1), :].rearrange("p a d -> p (a d)"), s0[:, j, :])\
                        .then_inc(S[f"s_out{j}"], 16)
            for j in range(2):
                pool.wait_ge(S[f"s_out{j}"], 16 * KC // 2)
            for j in range(2):
                pool.dma_start(s0[:, j, :], selfT[:, j, :]).then_inc(S[f"s_in{j}"], 16)
            with pool.Fori(1, KC // 2) as i:
                for j in range(2):
                    pool.wait_ge(S["h_lo"], 2 * i + j - 1)
                    pool.dma_start(s0[:, j, :], selfT[:, ds(2 * i + j, 1), :].rearrange("p a d -> p (a d)"))\
                        .then_inc(S[f"s_in{j}"], 16)

            pool.wait_ge(S["h_lo"], KC)
            for j in range(2):
                pool.wait_ge(S[f"res_out{j}"], 16 * T // 2)
            for j in range(2):
                pool.dma_start(xm[:, j, :], mixed[:, j, :]).then_inc(S[f"res_in{j}"], 16)
            pool.dma_start(lnb_bc[:], rows[8].partition_broadcast(P)).then_inc(S["bias_in"], 16)
            pool.wait_ge(S["bias_in"], 16 * 3)

            def f_body(c, j, last):
                pool.wait_ge(S["f_var"], c + 1)
                pool.tensor_tensor(rstd[:, 0:1], mv[:, 0, 1:2], mhalf_pow[:, 0:1], ALU.pow).then_inc(S["f_rstd"], 1)
                if not last:
                    pool.wait_ge(S["f_x1a"], c + 1)
                    pool.dma_start(xm[:, j, :], mixed[:, ds(c + 2, 1), :].rearrange("p a d -> p (a d)"))\
                        .then_inc(S[f"res_in{j}"], 16)
                pool.wait_ge(S["f_y"], c + 1)
                settle(pool)
                pool.dma_start(y_d[:, ds(c, 1), :].rearrange("p a d -> p (a d)"), yb[:, j, :])\
                    .then_inc(S[f"rows_out{j}"], 16)
                pool.tensor_tensor(x1[:, j, :], x1[:, j, :], lnb_bc[:], ALU.add).then_inc(S["x1_plus"], 1)
                pool.wait_ge(S["x1_plus"], c + 1)
                settle(pool)
                pool.dma_start(x1_d[:, ds(c, 1), :].rearrange("p a d -> p (a d)"), x1[:, j, :])\
                    .then_inc(S[f"res_out{j}"], 16)

            with pool.Fori(0, T // 2 - 1) as i:
                for j in range(2):
                    f_body(2 * i + j, j, False)
            f_body(T - 2, 0, True)
            f_body(T - 1, 1, True)
            for j in range(2):
                pool.wait_ge(S[f"rows_out{j}"], 16 * T // 2)
            for j in range(2):
                pool.wait_ge(S[f"res_out{j}"], 16 * T)
            pool.wait_ge(S["f_g"], T)
            pool.memset(ones2[:], 1.0).then_inc(S["r_const"], 1)
            pool.wait_ge(S["r_const"], 1)
            pool.affine_select(out=upper2[:], in_=ones2[:], compare_op=ALU.is_gt, fill=0.0, base=0,
                               pattern=[[1, P]], channel_multiplier=-1).then_inc(S["r_const"], 1)
            pool.iota(iota_m[:].bitcast(I32), pattern=[[1, P]], base=0, channel_multiplier=0).then_inc(S["r_const"], 1)
            pool.iota(node_f[:].bitcast(I32), pattern=[[P, T]], base=0, channel_multiplier=1).then_inc(S["r_const"], 1)
            pool.iota(count_down[:].bitcast(I32), pattern=[[-1, EXPERTS]], base=EXPERTS, channel_multiplier=0)\
                .then_inc(S["r_const"], 1)
            pool.iota(mgroup[:, 0, :].bitcast(I32), pattern=[[2 * P, MOE_GROUPS]], base=0, channel_multiplier=0)\
                .then_inc(S["r_const"], 1)
            pool.dma_start(acc[:], y_d).then_inc(S["acc_in"], 16)
            pool.wait_ge(S["f_ylo"], T)
            pool.dma_start(lnw_bc[:], rows[7].partition_broadcast(P)).then_inc(S["bias_in"], 16)
            pool.wait_ge(S["f_lg"], T)
            pool.wait_ge(S["nodes_made"], 1)

            def gather(g, par):
                for h in range(2):
                    n = 2 * g + h
                    b = 2 * par + h
                    if not (isinstance(g, int) and g < 2):
                        pool.wait_ge(S["x_T"], n - 3)
                    pool.tensor_copy(gidx[:, b, :], node_i[:, ds(n, 1)]).then_inc(S["idx_copied"], 1)
                    pool.wait_ge(S["idx_copied"], EDGE_COPIES + n + 1)
                    settle(pool)
                    pool.indirect_dma_start(
                        out=xg[:, par, h, :], out_offset=None, in_=y_rows,
                        in_offset=bass.IndirectOffsetOnAxis(ap=gidx[:, b, :].bitcast(U32), axis=0))\
                        .then_inc(S[f"xg_in{par}{h}"], 16)

            gather(0, 0)
            gather(1, 1)

            def group_move(g, par, ahead=True):
                if ahead:
                    gather(g + 2, par)
                for h in range(2):
                    pool.wait_ge(S["y_evac"], 4 * g + 2 * h + 2)
                    settle(pool)
                    pool.dma_start(moe_rows[ds(256 * g + P * h, P), :], yo[:, par, h, :]).then_inc(S[f"yo_out{par}"], 16)

            with pool.Fori(0, MOE_GROUPS // 2 - 1) as i:
                group_move(2 * i, 0)
                group_move(2 * i + 1, 1)
            group_move(MOE_GROUPS - 3, 0)
            group_move(MOE_GROUPS - 2, 1, False)
            group_move(MOE_GROUPS - 1, 0, False)
            pool.wait_ge(S["bias_in"], 16 * 4)
            pool.wait_ge(S["yo_out0"], 16 * 2 * (MOE_GROUPS // 2 + 1))
            pool.wait_ge(S["yo_out1"], 16 * 2 * (MOE_GROUPS // 2))

            def take(c, j):
                for k in range(TOP):
                    n = TOP * c + k
                    pool.tensor_copy(gidx[:, 2 * j + k, :], slot_i[:, k, ds(c, 1)]).then_inc(S["idx_copied"], 1)
                    pool.wait_ge(S["idx_copied"], EDGE_COPIES + MOE_TILES + n + 1)
                    settle(pool)
                    pool.indirect_dma_start(
                        out=yg[:, j, k, :], out_offset=None, in_=moe_rows,
                        in_offset=bass.IndirectOffsetOnAxis(ap=gidx[:, 2 * j + k, :].bitcast(U32), axis=0))\
                        .then_inc(S[f"xg_in{j}{k}"], 16)

            def end_body(c, j, last):
                pool.wait_ge(S["f_var"], T + c + 1)
                pool.tensor_tensor(rstd[:, j:j + 1], mv[:, j, 1:2], mhalf_pow[:, 0:1], ALU.pow).then_inc(S["f_rstd"], 1)
                if not last:
                    take(c + 2, j)
                pool.wait_ge(S["e_n"], c + 1)
                pool.tensor_tensor(fin[:, j, :], fin[:, j, :], lnw_bc[:], ALU.mult).then_inc(S["e_w"], 1)

            take(0, 0)
            take(1, 1)
            with pool.Fori(0, T // 2 - 1) as i:
                for j in range(2):
                    end_body(2 * i + j, j, False)
            end_body(T - 2, 0, True)
            end_body(T - 1, 1, True)

        @block.tensor
        def _(pe):
            def w_at(slot, pos, part, c0, n):
                o = (pos % 2) * 512 + c0
                return wslot[:, 4 * slot + pos // 2, part, o:o + n]

            def nodes_unit(bank, hi, lo, slots, order, part=range(KC)):
                for pos in part:
                    for s, b in zip(slots, bank):
                        lh, ll = hi(order[pos]), lo(order[pos])
                        pe.matmul(ps[:, b, :], lh, w_at(s, pos, 0, 0, 512), start=(pos == 0), stop=False)
                        pe.matmul(ps[:, b, :], lh, w_at(s, pos, 1, 0, 512), start=False, stop=False)
                        m = pe.matmul(ps[:, b, :], ll, w_at(s, pos, 0, 0, 512), start=False, stop=(pos == KC - 1))
                return m

            def tile_of(t, c):
                return lambda k: t[:, k, ds(c * P, P)] if not isinstance(c, int) else t[:, k, c * P:(c + 1) * P]

            def transposes(bank, src):
                for k in range(KC):
                    m = pe.matmul(ps[:, bank + k // 4, (k % 4) * P:(k % 4 + 1) * P], src[:, k * P:(k + 1) * P],
                                  ident[:], start=True, stop=True, is_transpose=True)
                return m

            pe.wait_ge(S["const_made"], 9)

            pe.wait_ge(S["edge_tot"], 1)
            pe.matmul(ps[:, 7, 0:T], upper[:], e_small[:, 0, 0:T], start=True, stop=True)
            pe.matmul(ps[:, 7, 16:16 + T], ones32[:], e_small[:, 0, 0:T], start=True, stop=True)\
              .then_inc(S["totals_made"], 1)

            def ln0(c, j, conv):
                pe.wait_ge(S["ln0_done"], c + 1)
                if not (isinstance(c, int) and c < 2):
                    pe.wait_ge(S["ln0_lo"], c - 1)
                transposes(2 * j, xn0[:, j, :]).then_inc(S["ln0_T"], 1)

            chunk_loop(pe, ln0)

            for ph in range(4):
                h = ph % 2
                slot = 2 * (ph % 2)
                sbank = 4 + ph % 2
                pe.wait_ge(S["w_lo"], 8 * (ph + 1))
                if ph == 0:
                    pe.wait_ge(S["ln0_lo"], T)
                    pe.wait_ge(S["edge_placed"], 3)
                if ph >= 2:
                    pe.wait_ge(S["state_first"], ph - 1)
                pe.matmul(ps[:, sbank, :], zeros16[:, 0:P], zeros16[:], start=True, stop=False,
                          skip_group_check=True)

                def kv(c, j, conv, ph=ph, h=h, slot=slot, sbank=sbank):
                    g = T * ph + c
                    if not (isinstance(c, int) and g < 2):
                        pe.wait_ge(S["v_scaled"], g - 1)
                    nodes_unit([2 * j, 2 * j + 1], tile_of(act_hi, c), tile_of(act_lo, c),
                               [slot, slot + 1], DIAG[h]).then_inc(S["kv_ready"], 1)
                    if not (isinstance(c, int) and c == 0):
                        states(g - 1, 1 - j, P)

                def states(g, j, rows_, sbank=sbank):
                    pe.wait_ge(S["v_lo"], g + 1)
                    pe.wait_ge(S["k_lo"], g + 1)
                    for p in range(4):
                        o = ps[:, sbank, p * P:(p + 1) * P]
                        for a, b in ((k_hi_t, v_hi_t), (k_hi_t, v_lo_t), (k_lo_t, v_hi_t)):
                            m = pe.matmul(o, a[0:rows_, j, p * P:(p + 1) * P], b[0:rows_, j, p * P:(p + 1) * P],
                                          start=False, stop=False, skip_group_check=True)
                    m.then_inc(S["state_mm"], 1)

                kv(0, 0, None)
                kv(1, 1, None)
                with pe.Fori(1, T // 2) as i:
                    kv(2 * i, 0, None)
                    kv(2 * i + 1, 1, None)
                states(T * ph + T - 1, 1, LAST)

            pe.wait_ge(S["w_lo"], 8 * 5)
            pe.wait_ge(S["v_scaled"], 4 * T)
            pe.wait_ge(S["state_lo"], 2)

            def q_body(c, j, conv):
                early = isinstance(c, int) and c < 2
                done = isinstance(c, int) and c >= T
                hi, lo = tile_of(act_hi, c), tile_of(act_lo, c)
                if not done:
                    if not (isinstance(c, int) and c == 0):
                        pe.wait_ge(S["q_biased0"], c)
                    nodes_unit([0], hi, lo, [0], DIAG[0]).then_inc(S["q_ready0"], 1)
                if not early:
                    pe.wait_ge(S["qT_lo"], c - 1)
                    if not (isinstance(c, int) and c == 2):
                        pe.wait_ge(S["o_normed"], c - 2)
                    for p in range(KC):
                        o = ps[:, 4 + p // 4, (p % 4) * P:(p % 4 + 1) * P]
                        s = lambda t: t[:, p // 4, (p % 4) * P:(p % 4 + 1) * P]
                        q = lambda t: t[:, j, p * P:(p + 1) * P]
                        pe.matmul(o, q(qT_hi_t), s(st_hi), start=True, stop=False)
                        pe.matmul(o, q(qT_hi_t), s(st_lo), start=False, stop=False)
                        m = pe.matmul(o, q(qT_lo_t), s(st_hi), start=False, stop=True)
                    m.then_inc(S["o_ready"], 1)
                if not done:
                    if not (isinstance(c, int) and c == 0):
                        pe.wait_ge(S["q_biased1"], c)
                    nodes_unit([1], hi, lo, [1], DIAG[1]).then_inc(S["q_ready1"], 1)
                if not early:
                    pe.wait_ge(S["o_normed"], c - 1)
                    if not (isinstance(c, int) and c == 2):
                        pe.wait_ge(S["lnT_f"], c - 2)
                    transposes(6, lnx).then_inc(S["lnT_ready"], 1)
                if not (isinstance(c, int) and (c == 0 or c > T)):
                    pe.wait_ge(S["q_normed"], c)
                    if not (isinstance(c, int) and c == 1):
                        pe.wait_ge(S["qT_lo"], c - 1)
                    transposes(2, qn[:, 1 - j, :]).then_inc(S["qT_ready"], 1)

            q_loop(pe, q_body)

            pe.wait_ge(S["w_lo"], 8 * 6)
            pe.wait_ge(S["q_biased1"], T)
            pe.wait_ge(S["qT_lo"], T)
            pe.wait_ge(S["lnT_lo"], T)

            def wo_body(c, j, conv):
                if not (isinstance(c, int) and c < 2):
                    pe.wait_ge(S["wo_biased"], c - 1)
                nodes_unit([2 * j, 2 * j + 1], tile_of(ln_hi, c), tile_of(ln_lo, c), [2, 3], PLAIN)\
                    .then_inc(S["wo_ready"], 1)

            chunk_loop(pe, wo_body)

            pe.wait_ge(S["w_lo"], 8 * 7)
            pe.wait_ge(S["wo_biased"], T)
            pe.wait_ge(S["lnT_f"], T)

            def group(g, par, first):
                pe.wait_ge(S["onehot"], g + 1)
                if not first:
                    pe.wait_ge(S["grp_copied"], g - 1)
                for t in range(TG):
                    for n, (c0, w_) in enumerate(COLS):
                        m = pe.matmul(ps[:, 3 * par + n, 0:w_], src_1h[:, par, t, :], dst_1h[:, par, t, c0:c0 + w_],
                                      start=(t == 0), stop=(t == TG - 1))
                m.then_inc(S["grp_ready"], 1)

            def z_body(c, j, conv):
                if not (isinstance(c, int) and c == 0):
                    pe.wait_ge(S["z_lo"], c)
                for q in range(5):
                    if q < 4:
                        m = nodes_unit([6, 7], tile_of(act_hi, c), tile_of(act_lo, c), [0, 1], PLAIN,
                                       range(2 * q, 2 * q + 2))
                    if q == 3:
                        m.then_inc(S["zp_ready"], 1)
                    group(5 * c + q, (5 * j + q) % 2, isinstance(c, int) and 5 * c + q < 2)

            chunk_loop(pe, z_body)
            pe.wait_ge(S["grp_added"], GROUPS)
            for n, w_ in enumerate((512, 512, NP - 1024)):
                for s in range(T):
                    m = pe.matmul(ps[:, 5 + n, 0:w_], ones16[:], adj[:, s, n * 512:n * 512 + w_],
                                  start=(s == 0), stop=(s == T - 1))
            m.then_inc(S["deg_ready"], 1)
            pe.wait_ge(S["w_lo"], 8 * 8)

            def feature_unit(bank, lhs, last_k, rhs_hi, rhs_lo):
                for k in range(last_k):
                    lh, ll = lhs(k)
                    for n, (c0, w_) in enumerate(COLS):
                        pe.matmul(ps[:, bank + n, 0:w_], lh, rhs_hi(k, c0, w_), start=(k == 0), stop=False)
                    if rhs_lo is not None:
                        for n, (c0, w_) in enumerate(COLS):
                            pe.matmul(ps[:, bank + n, 0:w_], lh, rhs_lo(k, c0, w_), start=False, stop=False)
                    for n, (c0, w_) in enumerate(COLS):
                        m = pe.matmul(ps[:, bank + n, 0:w_], ll, rhs_hi(k, c0, w_), start=False, stop=(k == last_k - 1))
                return m

            def s_chunk(u, i, j):
                o = 4 * u + 2 * i + j
                if not (u == 0 and isinstance(i, int) and i == 0):
                    pe.wait_ge(S["s_biased"], o - 1)

                def lhs(k):
                    at = lambda part: wslot[:, 4 * (2 + u) + k // 2, part, ds((k % 2) * 512 + (2 * i + j) * P, P)]
                    return at(0), at(1)
                feature_unit(3 * j, lhs, KC, lambda k, c0, w_: act_hi[:, k, c0:c0 + w_],
                             lambda k, c0, w_: act_lo[:, k, c0:c0 + w_]).then_inc(S["s_ready"], 1)

            for u in range(2):
                if u == 0:
                    s_chunk(0, 0, 0)
                    pe.wait_ge(S["dinv_made"], 2)
                    for t in range(T):
                        m = pe.matmul(ps[:, 7, t:t + 1], dinv[0:1, t * P:(t + 1) * P], ident[0:1, 0:1],
                                      start=True, stop=True)
                    m.then_inc(S["dcol_ready"], 1)
                    s_chunk(0, 0, 1)
                with pe.Fori(1 - u, 2) as i:
                    s_chunk(u, i, 0)
                    s_chunk(u, i, 1)

            pe.wait_ge(S["s_biased"], KC)
            pe.wait_ge(S["z_lo"], T)

            def a_chunk(o, j, first):
                if not first:
                    pe.wait_ge(S["a_scaled"], o - 1)
                feature_unit(3 * j, lambda s: (z_hi[:, s, ds(o * P, P)], z_lo[:, s, ds(o * P, P)]), T,
                             lambda s, c0, w_: adj[:, s, c0:c0 + w_], None).then_inc(S["a_ready"], 1)

            a_chunk(0, 0, True)
            a_chunk(1, 1, True)
            with pe.Fori(1, KC // 2) as i:
                a_chunk(2 * i, 0, False)
                a_chunk(2 * i + 1, 1, False)

            pe.wait_ge(S["w_lo"], 8 * 9)
            pe.wait_ge(S["h_lo"], KC)

            def z1_body(c, j, conv):
                if not (isinstance(c, int) and c < 2):
                    pe.wait_ge(S["z_lo"], T + c - 1)
                nodes_unit([2 * j, 2 * j + 1], tile_of(act_hi, c), tile_of(act_lo, c), [0, 1], PLAIN)\
                    .then_inc(S["zp_ready"], 1)

            chunk_loop(pe, z1_body)

            pe.wait_ge(S["w_lo"], 8 * 10)
            pe.wait_ge(S["z_lo"], 2 * T)
            pe.wait_ge(S["rw_lo"], 1)

            def f_body(c, j, conv):
                done = isinstance(c, int) and c >= T
                zero = isinstance(c, int) and c == 0
                if not done:
                    if not zero:
                        pe.wait_ge(S["f_x1a"], c)
                    nodes_unit([0, 1], tile_of(act_hi, c), tile_of(act_lo, c), [2, 3], PLAIN)\
                        .then_inc(S["f_s"], 1)
                if not zero:
                    pe.wait_ge(S["f_y"], c)
                    if not (isinstance(c, int) and c == 1):
                        pe.wait_ge(S["f_ylo"], c - 1)
                    transposes(4, yb[:, 1 - j, :]).then_inc(S["f_T"], 1)
                if not done:
                    if not zero:
                        pe.wait_ge(S["f_x1"], c)
                    for s in range(T):
                        a = adj[:, s, ds(c * P, P)]
                        for hh in range(2):
                            pe.matmul(ps[:, 2 + hh, :], a, z_hi[:, s, hh * 512:(hh + 1) * 512], start=(s == 0), stop=False)
                            m = pe.matmul(ps[:, 2 + hh, :], a, z_lo[:, s, hh * 512:(hh + 1) * 512],
                                          start=False, stop=(s == T - 1))
                    m.then_inc(S["f_g"], 1)
                if not zero:
                    pe.wait_ge(S["f_ylo"], c)
                    for k in range(KC):
                        col = ds(c * P - P, P)
                        o = ps[:, 6, ds(c * EXPERTS - EXPERTS, EXPERTS)]
                        pe.matmul(o, act_hi[:, k, col], rw16[:, k, 0, :], start=(k == 0), stop=False)
                        pe.matmul(o, act_hi[:, k, col], rw16[:, k, 1, :], start=False, stop=False)
                        m = pe.matmul(o, act_lo[:, k, col], rw16[:, k, 0, :], start=False, stop=(k == KC - 1))
                    m.then_inc(S["f_lg"], 1)

            chunk_loop(pe, f_body)
            f_body(T, 0, None)

            pe.wait_ge(S["r_const"], 2)
            pe.wait_ge(S["r_tot"], 1)
            pe.matmul(ps[:, 7, 0:EXPERTS], upper2[:], msmall[:, 0, :], start=True, stop=True)
            pe.matmul(ps[:, 7, 16:16 + EXPERTS], ones2[:], msmall[:, 0, :], start=True, stop=True)\
              .then_inc(S["r_before"], 1)
            pe.wait_ge(S["r_1h"], 1)
            for k in range(TOP):
                for t in range(T):
                    m = pe.matmul(ps[:, 6, 0:MOE_TILES], row_1h[:, k, t, :], tile_1h[:, k, t, :],
                                  start=(k == 0 and t == 0), stop=(k == TOP - 1 and t == T - 1))
            m.then_inc(S["nodes_ready"], 1)
            pe.wait_ge(S["nodes_made"], 1)

            def turn(g, par, h, trip):
                pe.wait_ge(S[f"xg_in{par}{h}"], 16 * trip + 16)
                if not (isinstance(g, int) and g == 0 and h == 0):
                    pe.wait_ge(S["xT_lo"], 2 * g + h)
                transposes(0, xg[:, par, h, :]).then_inc(S["x_T"], 1)

            def expert_group(g, par, last):
                slot = 2 * par
                if not last:
                    turn(g + 1, 1 - par, 0, trips(g + 1))
                pe.wait_ge(S["w_lo"], 8 * g + 8 * (DENSE + 1))
                pe.wait_ge(S["xT_lo"], 2 * g + 2)
                for f in range(4):
                    if not (isinstance(g, int) and g == 0 and f < 2):
                        pe.wait_ge(S["g_gelu"], 4 * g + f - 1)
                    for k in range(KC):
                        rh, rl = xT_hi_t[:, par, k, :], xT_lo_t[:, par, k, :]
                        o = ps[:, 2 + f % 2, 0:2 * P]
                        pe.matmul(o, w_at(slot, k, 0, f * P, P), rh, start=(k == 0), stop=False)
                        pe.matmul(o, w_at(slot, k, 0, f * P, P), rl, start=False, stop=False)
                        m = pe.matmul(o, w_at(slot, k, 1, f * P, P), rh, start=False, stop=(k == KC - 1))
                    m.then_inc(S["g_ready"], 1)
                if not last:
                    turn(g + 1, 1 - par, 1, trips(g + 1))
                for k in range(4):
                    pe.wait_ge(S["g_lo"], 4 * g + k + 1)
                    for b in range(4):
                        h, hh = b // 2, b % 2
                        if k == 0 and not (isinstance(g, int) and g == 0):
                            pe.wait_ge(S["y_evac"], 4 * g + b - 3)
                        gh, gl = gelu_hi[:, k, h * P:(h + 1) * P], gelu_lo[:, k, h * P:(h + 1) * P]
                        wh, wl = (wslot[:, 4 * (slot + 1) + k, part, hh * 512:(hh + 1) * 512] for part in (0, 1))
                        pe.matmul(ps[:, 4 + b, :], gh, wh, start=(k == 0), stop=False)
                        pe.matmul(ps[:, 4 + b, :], gh, wl, start=False, stop=False)
                        m = pe.matmul(ps[:, 4 + b, :], gl, wh, start=False, stop=(k == 3))
                        if k == 3:
                            m.then_inc(S["y_ready"], 1)

            turn(0, 0, 0, 0)
            turn(0, 0, 1, 0)
            group_loop(pe, expert_group)

        @block.scalar
        def _(act):
            act.preload_act_table(ACT.Silu)

            def convert(batch, i, diag):
                for j in range(2):
                    if diag:
                        act.wait_ge(S["diag_added"], 8 * batch + 2 * i + j + 1)
                    else:
                        act.wait_ge(S[f"stage_in{j}"], 16 * (4 * batch + i + 1))
                    settle(act)
                    slot = 8 * (batch % 2) + 4 * j
                    act.activation(wslot[:, ds(slot + i, 1), 0, :].rearrange("p a d -> p (a d)"), stage[:, j, :],
                                   ACT.Copy, scale=SW).then_inc(S["w_hi"], 1)

            act.wait_ge(S["cols_in"], 64)
            act.activation(colv[:, 0, :], colraw[:, 0, :], ACT.Copy).then_inc(S["prep_step"], 1)
            act.activation(colv[:, 2:4, :], colraw[:, 1:3, :], ACT.Copy, scale=SX).then_inc(S["prep_step"], 1)
            act.activation(colv[:, 1, :], colraw[:, 0, :], ACT.Copy, scale=SX).then_inc(S["prep_step"], 1)
            act.wait_ge(S["prep_step"], 3)
            act.activation(rw16[:, :, 0, :], rw32[:], ACT.Copy, scale=SW).then_inc(S["prep_step"], 1)

            def ln0(c, j, conv):
                act.wait_ge(S["ln0_T"], c + 1)
                settle(act)
                act.activation(act_hi[:, :, ds(c * P, P)],
                               banks(2 * j, 2).rearrange("p (k n) -> p k n", n=P), ACT.Copy, scale=SX)\
                    .then_inc(S["ln0_hi"], 1)

            chunk_loop(act, ln0)
            with act.Fori(0, 4) as i:
                convert(0, i, True)
            act.wait_ge(S["consts_in"], 16 * 5)
            act.activation(bv_bc[:], bv_bc[:], ACT.Copy, scale=SX).then_inc(S["prep_step"], 1)

            for ph in range(4):
                def kv(c, j, conv, ph=ph):
                    g = T * ph + c
                    act.wait_ge(S["k_biased"], g + 1)
                    act.activation(ks[:, j, :], kb[:, j, :], ACT.Silu).then_inc(S["k_silu"], 1)
                    act.wait_ge(S["k_silu"], g + 1)
                    act.activation(ksq[:, j, :], ks[:, j, :], ACT.Square, bias=halfc[:]).then_inc(S["k_sq"], 1)
                    act.wait_ge(S["v_scaled"], g + 1)
                    if not (isinstance(c, int) and g < 2):
                        act.wait_ge(S["state_mm"], g - 1)
                    act.activation(v_hi_t[:, j, :], v16[:, j, :], ACT.Copy).then_inc(S["v_hi"], 1)
                    act.wait_ge(S["k_normed"], g + 1)
                    act.activation(k_hi_t[:, j, :], kb[:, j, :], ACT.Copy, scale=SX).then_inc(S["k_hi"], 1)
                    if conv is not None and j == 0:
                        convert(ph + 1, conv, True)

                chunk_loop(act, kv)

            def q_body(c, j, conv):
                if not (isinstance(c, int) and c >= T):
                    act.wait_ge(S["q_biased1"], c + 1)
                    act.activation(qs[:], qb[:], ACT.Silu).then_inc(S["q_silu"], 1)
                    act.wait_ge(S["q_silu"], c + 1)
                    act.activation(qb[:], qs[:], ACT.Square, bias=halfc[:]).then_inc(S["q_sq"], 1)
                if not (isinstance(c, int) and c < 2):
                    act.wait_ge(S["lnT_ready"], c - 1)
                    if not (isinstance(c, int) and c == 2):
                        act.wait_ge(S["lnT_lo"], c - 2)
                    for k in range(KC):
                        m = act.activation(lnf[:, k * P:(k + 1) * P], banks(6, 2)[:, k * P:(k + 1) * P], ACT.Identity,
                                           scale=colv[:, 2, k:k + 1], bias=colv[:, 3, k:k + 1])
                    m.then_inc(S["lnT_f"], 1)
                    act.wait_ge(S["lnT_f"], c - 1)
                    settle(act)
                    act.activation(ln_hi[:, :, ds(c * P - 2 * P, P)], lnf[:].rearrange("p (k n) -> p k n", n=P),
                                   ACT.Copy).then_inc(S["lnT_hi"], 1)
                if not (isinstance(c, int) and (c == 0 or c > T)):
                    act.wait_ge(S["qT_ready"], c)
                    if not (isinstance(c, int) and c < 3):
                        act.wait_ge(S["o_ready"], c - 2)
                    act.activation(qT_hi_t[:, 1 - j, :], banks(2, 2), ACT.Copy, scale=SX).then_inc(S["qT_hi"], 1)
                if conv is not None and j == 0:
                    convert(5, conv, False)

            q_loop(act, q_body)

            def wo_body(c, j, conv):
                if conv is not None and j == 0:
                    act.wait_ge(S["wo_ready"], c)
                    convert(6, conv, False)

            chunk_loop(act, wo_body)
            act.wait_ge(S["wo_ready"], T)

            def z_body(c, j, conv):
                for q in range(5):
                    g = 5 * c + q
                    if q == 3:
                        act.wait_ge(S["zp_ready"], c + 1)
                        settle(act)
                        act.activation(z_hi[:, ds(c, 1), :].rearrange("p a d -> p (a d)"), banks(6, 2), ACT.Copy,
                                       scale=1.0 / SW).then_inc(S["z_hi"], 1)
                    act.wait_ge(S["grp_ready"], g + 1)
                    if not (isinstance(c, int) and g == 0):
                        act.wait_ge(S["grp_added"], g)
                    act.activation(counts[:], banks(3 * ((5 * j + q) % 2), 3, N), ACT.Copy)\
                        .then_inc(S["grp_copied"], 1)
                if conv is not None and j == 0:
                    convert(7, conv, False)

            chunk_loop(act, z_body)

            def s_chunk(u, i, j):
                o = 4 * u + 2 * i + j
                act.wait_ge(S["s_ready"], o + 1)
                if not (u == 0 and isinstance(i, int) and i == 0):
                    act.wait_ge(S[f"s_out{j}"], 16 * (2 * u + i))
                settle(act)
                act.activation(s0[:, j, :], banks(3 * j, 3, N), ACT.Identity, scale=1.0 / (SW * SX),
                               bias=colv[:, 0, ds(o, 1)]).then_inc(S["s_biased"], 1)
                if j == 1:
                    convert_at(2 * u + i)

            def convert_at(i):
                convert(8, i, False)

            for u in range(2):
                if u == 0:
                    s_chunk(0, 0, 0)
                    s_chunk(0, 0, 1)
                with act.Fori(1 - u, 2) as i:
                    s_chunk(u, i, 0)
                    s_chunk(u, i, 1)

            def h_chunk(o, j):
                act.wait_ge(S["a_sum"], o + 1)
                settle(act)
                act.activation(act_hi[:, ds(o, 1), 0:N].rearrange("p a n -> p (a n)"), s0[:, j, :], ACT.Relu)\
                    .then_inc(S["h_hi"], 1)

            with act.Fori(0, KC // 2) as i:
                h_chunk(2 * i, 0)
                h_chunk(2 * i + 1, 1)

            def z1_body(c, j, conv):
                act.wait_ge(S["zp_ready"], T + c + 1)
                settle(act)
                act.activation(z_hi[:, ds(c, 1), :].rearrange("p a d -> p (a d)"), banks(2 * j, 2), ACT.Copy,
                               scale=1.0 / SW).then_inc(S["z_hi"], 1)
                if conv is not None and j == 0:
                    convert(9, conv, False)

            chunk_loop(act, z1_body)

            def f_body(c, j, conv):
                if not (isinstance(c, int) and c == 0):
                    act.wait_ge(S["f_T"], c)
                    settle(act)
                    act.activation(act_hi[:, :, ds(c * P - P, P)],
                                   banks(4, 2).rearrange("p (k n) -> p k n", n=P), ACT.Copy, scale=SX)\
                        .then_inc(S["f_yhi"], 1)
                if conv is not None and j == 0:
                    convert(10, conv, False)

            chunk_loop(act, f_body)
            f_body(T, 0, None)

            act.wait_ge(S["r_step"], 1)
            act.activation(sel[:, 2, :], sel[:, 1, :], ACT.Exp).then_inc(S["r_exp"], 1)
            act.preload_act_table(ACT.Gelu)

            def turned(g, par, h):
                act.wait_ge(S["x_T"], 2 * g + h + 1)
                settle(act)
                act.activation(xT_hi_t[:, par, :, h * P:(h + 1) * P], banks(0, 2).rearrange("p (k n) -> p k n", n=P),
                               ACT.Copy, scale=SX).then_inc(S["xT_hi"], 1)

            def expert_group(g, par, last):
                if not last:
                    turned(g + 1, 1 - par, 0)
                e = act.value_load(expert_i[0:1, ds(g, 1)], min_val=0, max_val=EXPERTS - 1)
                for f in range(4):
                    n = 4 * g + f
                    act.wait_ge(S["g_ready"], n + 1)
                    if not (isinstance(g, int) and g == 0 and f < 2):
                        act.wait_ge(S["g_lo"], n - 1)
                    settle(act)
                    act.activation(g32[:, f % 2, :], ps[:, 2 + f % 2, 0:2 * P], ACT.Gelu, scale=1.0 / (SW * SX),
                                   bias=b1c[:, ds(4 * e + f, 1)]).then_inc(S["g_gelu"], 1)
                    act.wait_ge(S["g_gelu"], n + 1)
                    act.activation(gelu_hi[:, f, :], g32[:, f % 2, :], ACT.Copy, scale=SX).then_inc(S["g_hi"], 1)
                    if not last:
                        for j in range(2):
                            buf = (2 * f + j) % 4
                            act.wait_ge(S[f"stage_in{buf}"], 32 * g + 16 * (f // 2 + 1 + (4 * (DENSE + 1) if buf < 2 else 0)))
                            t = stage[:, buf, :] if buf < 2 else stage2[:, buf - 2, :]
                            act.activation(wslot[:, 8 * (1 - par) + 4 * j + f, 0, :], t, ACT.Copy, scale=SW)\
                                .then_inc(S["w_hi"], 1)
                if not last:
                    turned(g + 1, 1 - par, 1)

            act.wait_ge(S["nodes_made"], 1)
            turned(0, 0, 0)
            turned(0, 0, 1)
            group_loop(act, expert_group)

            def end_body(c, j, conv):
                act.wait_ge(S["e_nmr"], c + 1)
                if not (isinstance(c, int) and c < 2):
                    act.wait_ge(S[f"out{j}"], 16 * (conv + 1))
                settle(act)
                act.activation(fin[:, j, :], acc[:, ds(c, 1), :].rearrange("p a d -> p (a d)"), ACT.Identity,
                               scale=rstd[:, j:j + 1], bias=nmr[:, j:j + 1]).then_inc(S["e_n"], 1)

            chunk_loop(act, end_body)

        @block.vector
        def _(dve):
            steps = [0]

            def then(ins):
                steps[0] += 1
                ins.then_inc(S["rank_step"], 1)
                dve.wait_ge(S["rank_step"], steps[0])

            def diag_add(batch, i):
                for j in range(2):
                    dve.wait_ge(S[f"stage_in{j}"], 16 * (4 * batch + i + 1))
                    d = stage[:, j, ds(i * P, P)]
                    dve.tensor_tensor(d, d, ident[:], ALU.add).then_inc(S["diag_added"], 1)

            def convert(batch, i):
                for j in range(2):
                    dve.wait_ge(S["w_hi"], 8 * batch + 2 * i + j + 1)
                    slot = 8 * (batch % 2) + 4 * j
                    at = lambda part: wslot[:, ds(slot + i, 1), part, :].rearrange("p a d -> p (a d)")
                    dve.scalar_tensor_tensor(at(1), stage[:, j, :], SW, at(0), ALU.mult, ALU.subtract)\
                        .then_inc(S["w_lo"], 1)

            then(dve.memset(mask[:], 0.0))
            dve.memset(mask[0:HD, :, 0:HD], SS)
            then(dve.memset(mask[HD:P, :, HD:P], SS))
            dve.wait_ge(S["edge_in"], 32)
            src_f, dst_f, rowf, tmp, loc = (es[:, n, :] for n in range(5))
            then(dve.tensor_copy(es[:, 0:2, :], e_i[:]))
            for b in range(T + 1):
                m = dve.tensor_scalar(ge[:, b, :], src_f, float(P * b), None, ALU.is_ge)
            then(m)
            dve.memset(tmp, 1.0)
            then(dve.tensor_tensor(member[:], ge[:, 0:T, :], ge[:, 1:T + 1, :], ALU.subtract))
            for b in range(T):
                m = dve.tensor_tensor_scan(cum[:, b, :], tmp, member[:, b, :], 0.0, ALU.mult, ALU.add)
            then(m)
            dve.tensor_copy(e_small[:, 0, 0:T], cum[:, :, EJ - 1]).then_inc(S["edge_tot"], 1)
            dve.wait_ge(S["const_made"], 9)
            dve.tensor_copy(iota_d[:], iota_i[:])
            dve.tensor_copy(giota[:], giota_i[:])
            dve.wait_ge(S["totals_made"], 1)
            before, size, ends, offs = (e_small[:, n, 0:T] for n in (1, 2, 3, 4))
            then(dve.tensor_scalar(size, ps[:, 7, 16:16 + T], float(TG * P - 1), None, ALU.add))
            then(dve.tensor_copy(ei_small[:, 0:T], size))
            then(dve.tensor_scalar(ei_small[:, 0:T], ei_small[:, 0:T], 9, 9, ALU.arith_shift_right,
                                   ALU.logical_shift_left))
            then(dve.tensor_copy(size, ei_small[:, 0:T]))
            then(dve.tensor_tensor_scan(ends, tmp[:, 0:T], size, 0.0, ALU.mult, ALU.add))
            then(dve.tensor_tensor(offs, ends, size, ALU.subtract))
            then(dve.scalar_tensor_tensor(offs, ps[:, 7, 0:T], -1.0, offs, ALU.add, ALU.add))
            for b in range(T):
                m = dve.scalar_tensor_tensor(posb[:, b, :], cum[:, b, :], offs[:, b:b + 1], member[:, b, :],
                                             ALU.add, ALU.mult)
            then(m)
            then(dve.tensor_reduce(rowf, posb[:].rearrange("p b j -> p j b"), AX.X, ALU.add))
            pi = e_i[:, 0, :]
            part = e_i[:, 1, :]
            then(dve.tensor_copy(pi, rowf))
            then(dve.tensor_scalar(part, pi, TG * P - 1, 2, ALU.bitwise_and, ALU.arith_shift_right))
            then(dve.tensor_copy(tmp, part))
            then(dve.tensor_scalar(part, pi, 9, 2, ALU.arith_shift_right, ALU.logical_shift_left))
            then(dve.tensor_copy(loc, part))
            then(dve.scalar_tensor_tensor(rowf, tmp, float(SPP), loc, ALU.mult, ALU.add))
            then(dve.tensor_scalar(part, pi, TG - 1, None, ALU.bitwise_and))
            then(dve.tensor_copy(tmp, part))
            then(dve.tensor_tensor(rowf, rowf, tmp, ALU.add))
            then(dve.tensor_copy(tmp, pid_i[:]))
            then(dve.tensor_tensor(rowf, rowf, tmp, ALU.subtract))
            then(dve.tensor_tensor(rowf, rowf, ge[:, 0, :], ALU.mult))
            then(dve.tensor_tensor(rowf, rowf, tmp, ALU.add))
            dve.tensor_copy(idx[:], rowf).then_inc(S["edge_placed"], 1)
            then(dve.tensor_reduce(loc, ge[:, 1:T, :].rearrange("p b j -> p j b"), AX.X, ALU.add))
            dve.tensor_copy(pay[:, :, 1], dst_f)
            dve.scalar_tensor_tensor(pay[:, :, 0], loc, -float(P), src_f, ALU.mult, ALU.add)\
                .then_inc(S["edge_placed"], 1)
            then(dve.memset(block_f[:], 0.0))
            for b in range(T - 1):
                then(dve.scalar_tensor_tensor(block_f[:], giota[:], ends[:, b:b + 1], block_f[:], ALU.is_ge, ALU.add))
            then(dve.tensor_copy(block_i[:], block_f[:]))

            dve.wait_ge(S["prep_step"], 4)
            dve.scalar_tensor_tensor(rw16[:, :, 1, :], rw32[:], SW, rw16[:, :, 0, :], ALU.mult, ALU.subtract)\
                .then_inc(S["rw_lo"], 1)

            def norm_tile(src, dst, count, stat, var, rstd_sem, eps, done):
                settle(dve)
                for hh in range(2):
                    m = dve.bn_stats(stats[:, 0, 6 * hh:6 * hh + 6], src[:, hh * 512:(hh + 1) * 512])
                m.then_inc(S[stat], 1)
                dve.wait_ge(S[stat], 2 * count + 1)
                settle(dve)
                dve.bn_aggr(mv[:, 0, :], stats[:, 0, :]).then_inc(S[stat], 1)
                dve.wait_ge(S[stat], 2 * count + 2)
                dve.tensor_scalar(mv[:, 0, 1:2], mv[:, 0, 1:2], eps, None, ALU.add).then_inc(S[var], 1)
                dve.wait_ge(S[rstd_sem], count + 1)
                return dve.tensor_scalar(dst, src, mv[:, 0, 0:1], rstd[:, 0:1], ALU.subtract, ALU.mult)\
                    .then_inc(S[done], 1)

            def ln0_lo(c, j):
                dve.wait_ge(S["ln0_hi"], c + 1)
                dve.scalar_tensor_tensor(act_lo[:, :, ds(c * P, P)], banks(2 * j, 2).rearrange("p (k n) -> p k n", n=P),
                                         SX, act_hi[:, :, ds(c * P, P)], ALU.mult, ALU.subtract)\
                    .then_inc(S["ln0_lo"], 1)

            def ln0(c, j, conv):
                i = c // 2 if isinstance(c, int) else conv + 1
                dve.wait_ge(S[f"x_in{j}"], 16 * (i + 1))
                if not (isinstance(c, int) and c < 2):
                    dve.wait_ge(S["ln0_T"], c - 1)
                norm_tile(xin0[:, j, :], xn0[:, j, :], c, "ln0_stat", "ln0_var", "ln0_rstd", 1e-5, "ln0_done")
                if not (isinstance(c, int) and c == 0):
                    ln0_lo(c - 1, 1 - j)

            chunk_loop(dve, ln0)
            ln0_lo(T - 1, 1)

            with dve.Fori(0, 4) as i:
                diag_add(0, i)
                convert(0, i)
            dve.memset(zeros16[:], 0.0).then_inc(S["edge_placed"], 1)
            dve.wait_ge(S["prep_step"], 5)

            for ph in range(4):
                kk, h = ph // 2, ph % 2

                def kv(c, j, conv, ph=ph, kk=kk, h=h):
                    g = T * ph + c
                    dve.wait_ge(S["kv_ready"], g + 1)
                    dve.scalar_tensor_tensor(kb[:, j, :], ps[:, 2 * j, :], 1.0 / (SW * SX),
                                             bk_bc[:, kk, h * 512:(h + 1) * 512], ALU.mult, ALU.add)\
                        .then_inc(S["k_biased"], 1)
                    dve.scalar_tensor_tensor(v16[:, j, :], ps[:, 2 * j + 1, :], 1.0 / SW,
                                             bv_bc[:, kk, h * 512:(h + 1) * 512], ALU.mult, ALU.add)\
                        .then_inc(S["v_scaled"], 1)
                    if conv is not None and j == 0:
                        diag_add(ph + 1, conv)
                    dve.wait_ge(S["k_sq"], g + 1)
                    dve.tensor_reduce(ssq[:, 0, 0:8], ksq[:, j, :].rearrange("p (a b) -> p a b", b=HD), AX.X, ALU.add)\
                        .then_inc(S["k_ssq"], 1)
                    dve.wait_ge(S["v_hi"], g + 1)
                    dve.tensor_tensor(v_lo_t[:, j, :], v16[:, j, :], v_hi_t[:, j, :], ALU.subtract)\
                        .then_inc(S["v_lo"], 1)
                    dve.wait_ge(S["k_nrm"], g + 1)
                    dve.tensor_scalar(nrm[:, 0, 0:8], nrm[:, 0, 0:8], 1e-6, None, ALU.add).then_inc(S["k_inv"], 1)
                    dve.wait_ge(S["k_inv"], 2 * (g) + 1)
                    dve.reciprocal(nrm[:, 0, 0:8], nrm[:, 0, 0:8]).then_inc(S["k_inv"], 1)
                    dve.wait_ge(S["k_inv"], 2 * g + 2)
                    dve.scalar_tensor_tensor(kb[:, j, :].rearrange("p (a b) -> p a b", b=HD),
                                             ks[:, j, :].rearrange("p (a b) -> p a b", b=HD), 0.5,
                                             nrm[:, 0, 0:8].unsqueeze(2).broadcast_to([P, 8, HD]),
                                             ALU.add, ALU.mult).then_inc(S["k_normed"], 1)
                    dve.wait_ge(S["k_hi"], g + 1)
                    dve.scalar_tensor_tensor(k_lo_t[:, j, :], kb[:, j, :], SX, k_hi_t[:, j, :], ALU.mult,
                                             ALU.subtract).then_inc(S["k_lo"], 1)
                    if conv is not None and j == 0:
                        convert(ph + 1, conv)

                chunk_loop(dve, kv)
                dve.wait_ge(S["state_mm"], T * (ph + 1))
                sb = ps[:, 4 + ph % 2, :]
                sc = 1.0 / (SX * SX * N)
                if kk == 0:
                    dve.tensor_scalar(st0[:, h, :], sb, sc, None, ALU.mult).then_inc(S["state_first"], 1)
                else:
                    dve.scalar_tensor_tensor(stp[:], sb, sc, st0[:, h, :], ALU.mult, ALU.mult)\
                        .then_inc(S["state_step"], 1)
                    dve.wait_ge(S["state_step"], 3 * h + 1)
                    dve.tensor_tensor(stp[:], stp[:], mask[:].rearrange("p a b -> p (a b)"), ALU.mult)\
                        .then_inc(S["state_step"], 1)
                    dve.wait_ge(S["state_step"], 3 * h + 2)
                    dve.tensor_copy(st_hi[:, h, :], stp[:]).then_inc(S["state_step"], 1)
                    dve.wait_ge(S["state_step"], 3 * h + 3)
                    dve.tensor_tensor(st_lo[:, h, :], stp[:], st_hi[:, h, :], ALU.subtract)\
                        .then_inc(S["state_lo"], 1)

            def q_body(c, j, conv):
                early = isinstance(c, int) and c < 2
                done = isinstance(c, int) and c >= T

                def evac(hh):
                    dve.wait_ge(S[f"q_ready{hh}"], c + 1)
                    dve.scalar_tensor_tensor(qb[:, hh * 512:(hh + 1) * 512], ps[:, hh, :], 1.0 / (SW * SX),
                                             bq_bc[:, hh * 512:(hh + 1) * 512], ALU.mult, ALU.add)\
                        .then_inc(S[f"q_biased{hh}"], 1)
                if not done:
                    evac(0)
                if not early:
                    dve.wait_ge(S["o_ready"], c - 1)
                    if not (isinstance(c, int) and c == 2):
                        dve.wait_ge(S["lnT_ready"], c - 2)
                    norm_tile(banks(4, 2), lnx[:], c - 2, "o_stat", "o_var", "o_rstd", 1e-5 * (SX * SS) ** 2, "o_normed")
                if not done:
                    evac(1)
                if not early:
                    dve.wait_ge(S["lnT_hi"], c - 1)
                    dve.tensor_tensor(ln_lo[:, :, ds(c * P - 2 * P, P)], lnf[:].rearrange("p (k n) -> p k n", n=P),
                                      ln_hi[:, :, ds(c * P - 2 * P, P)], ALU.subtract).then_inc(S["lnT_lo"], 1)
                if not (isinstance(c, int) and (c == 0 or c > T)):
                    dve.wait_ge(S["qT_hi"], c)
                    dve.scalar_tensor_tensor(qT_lo_t[:, 1 - j, :], banks(2, 2), SX, qT_hi_t[:, 1 - j, :], ALU.mult,
                                             ALU.subtract).then_inc(S["qT_lo"], 1)
                if not done:
                    dve.wait_ge(S["q_sq"], c + 1)
                    dve.tensor_reduce(ssq[:, 1, :], qb[:].rearrange("p (a b) -> p a b", b=HD), AX.X, ALU.add)\
                        .then_inc(S["q_ssq"], 1)
                    dve.wait_ge(S["q_nrm"], c + 1)
                    dve.tensor_scalar(nrm[:, 1, :], nrm[:, 1, :], 1e-6, None, ALU.add).then_inc(S["q_inv"], 1)
                    dve.wait_ge(S["q_inv"], 2 * c + 1)
                    dve.reciprocal(nrm[:, 1, :], nrm[:, 1, :]).then_inc(S["q_inv"], 1)
                    dve.wait_ge(S["q_inv"], 2 * c + 2)
                    dve.scalar_tensor_tensor(qn[:, j, :].rearrange("p (a b) -> p a b", b=HD),
                                             qs[:].rearrange("p (a b) -> p a b", b=HD), 0.5,
                                             nrm[:, 1, :].unsqueeze(2).broadcast_to([P, HEADS, HD]),
                                             ALU.add, ALU.mult).then_inc(S["q_normed"], 1)
                if conv is not None and j == 0:
                    convert(5, conv)

            q_loop(dve, q_body)

            dve.wait_ge(S["bias_in"], 16 * 2)
            then(dve.tensor_tensor(bsum[:], bsum[:], mo[:, 1, :], ALU.add))

            def wo_body(c, j, conv):
                i = c // 2 if isinstance(c, int) else conv + 1
                dve.wait_ge(S["wo_ready"], c + 1)
                if not (isinstance(c, int) and c < 2):
                    dve.wait_ge(S[f"res_out{j}"], 16 * i)
                dve.scalar_tensor_tensor(mo[:, j, :], banks(2 * j, 2), 1.0 / (SW * SX), bsum[:], ALU.mult,
                                         ALU.add).then_inc(S["wo_biased"], 1)
                dve.wait_ge(S["wo_biased"], c + 1)
                dve.wait_ge(S[f"xin_in{j}"], 16 * (i + 1))
                dve.tensor_tensor(mo[:, j, :], mo[:, j, :], xin[:, j, :], ALU.add).then_inc(S["wo_x"], 1)
                if conv is not None and j == 0:
                    convert(6, conv)

            chunk_loop(dve, wo_body)

            dve.wait_ge(S["table_in"], 16)
            dve.wait_ge(S["zeros_made"], 5)
            for j in range(2):
                dve.wait_ge(S[f"res_out{j}"], 16 * T // 2)

            def one_hots(g, par, first):
                if not first:
                    dve.wait_ge(S["grp_ready"], g - 1)
                for t in range(TG):
                    col = TG * g + t
                    dve.tensor_scalar(src_1h[:, par, t, :], iota_d[:, 0:P],
                                      edges[:, ds(col, 1), 0], None, ALU.is_equal)
                    m = dve.tensor_scalar(dst_1h[:, par, t, :], iota_d[:],
                                          edges[:, ds(col, 1), 1], None, ALU.is_equal)
                m.then_inc(S["onehot"], 1)

            def add_group(g):
                dve.wait_ge(S["grp_copied"], g + 1)
                if not (isinstance(g, int) and g == 0):
                    dve.wait_ge(S["grp_added"], g)
                blk = dve.value_load(block_i[0:1, ds(g, 1)], min_val=0, max_val=T - 1)
                row = adj[:, ds(blk, 1), 0:N].rearrange("p a n -> p (a n)")
                dve.tensor_tensor(row, counts[:], row, ALU.add).then_inc(S["grp_added"], 1)

            def z_low(c):
                dve.wait_ge(S["z_hi"], c + 1)
                at = lambda t: t[:, ds(c, 1), :].rearrange("p a d -> p (a d)")
                dve.scalar_tensor_tensor(at(z_lo), banks(6, 2), 1.0 / SW, at(z_hi), ALU.mult, ALU.subtract)\
                    .then_inc(S["z_lo"], 1)

            def z_body(c, j, conv):
                for q in range(5):
                    g = 5 * c + q
                    par = (5 * j + q) % 2
                    one_hots(g, par, isinstance(c, int) and g < 2)
                    if q == 4:
                        z_low(c)
                    if not (isinstance(c, int) and g == 0):
                        add_group(g - 1)
                if conv is not None and j == 0:
                    convert(7, conv)

            chunk_loop(dve, z_body)
            add_group(GROUPS - 1)
            dve.wait_ge(S["deg_ready"], 1)
            dve.tensor_scalar(dinv[:], banks(5, 3, NP), 1.0, None, ALU.max).then_inc(S["dinv_made"], 1)
            dve.wait_ge(S["dinv_made"], 1)
            dve.reciprocal(dinv[:], dinv[:]).then_inc(S["dinv_made"], 1)
            dve.wait_ge(S["dcol_ready"], 1)
            dve.tensor_scalar(dinv_col[:], ps[:, 7, 0:T], 1.0 / SX, None, ALU.mult).then_inc(S["dcol_made"], 1)

            with dve.Fori(0, 4) as i:
                convert(8, i)
            dve.wait_ge(S["dinv_made"], 2)

            def h_chunk(o, i, j):
                dve.wait_ge(S["a_ready"], o + 1)
                dve.tensor_tensor(tg[:], banks(3 * j, 3, N), dinv[:, 0:N], ALU.mult).then_inc(S["a_scaled"], 1)
                dve.wait_ge(S["a_scaled"], o + 1)
                dve.wait_ge(S[f"s_in{j}"], 16 * (i + 1))
                dve.scalar_tensor_tensor(s0[:, j, :], s0[:, j, :], SX, tg[:], ALU.mult, ALU.add)\
                    .then_inc(S["a_sum"], 1)
                dve.wait_ge(S["h_hi"], o + 1)
                at = lambda t: t[:, ds(o, 1), 0:N].rearrange("p a n -> p (a n)")
                dve.scalar_tensor_tensor(at(act_lo), s0[:, j, :], 0.0, at(act_hi), ALU.max, ALU.subtract)\
                    .then_inc(S["h_lo"], 1)

            with dve.Fori(0, KC // 2) as i:
                h_chunk(2 * i, i, 0)
                h_chunk(2 * i + 1, i, 1)

            def z1_body(c, j, conv):
                dve.wait_ge(S["z_hi"], T + c + 1)
                at = lambda t: t[:, ds(c, 1), :].rearrange("p a d -> p (a d)")
                dve.scalar_tensor_tensor(at(z_lo), banks(2 * j, 2), 1.0 / SW, at(z_hi), ALU.mult, ALU.subtract)\
                    .then_inc(S["z_lo"], 1)
                if conv is not None and j == 0:
                    convert(9, conv)

            chunk_loop(dve, z1_body)

            def f_body(c, j, conv):
                i = c // 2 if isinstance(c, int) else conv + 1
                done = isinstance(c, int) and c >= T
                if not done:
                    dve.wait_ge(S["f_s"], c + 1)
                    dve.wait_ge(S[f"res_in{j}"], 16 * (i + 1))
                    if not (isinstance(c, int) and c < 2):
                        dve.wait_ge(S[f"res_out{j}"], 16 * (T // 2 + i))
                    dve.scalar_tensor_tensor(x1[:, j, :], banks(0, 2), 1.0 / (SW * SX), xm[:, j, :], ALU.mult,
                                             ALU.add).then_inc(S["f_x1a"], 1)
                if not (isinstance(c, int) and c == 0):
                    dve.wait_ge(S["f_yhi"], c)
                    dve.scalar_tensor_tensor(act_lo[:, :, ds(c * P - P, P)],
                                             banks(4, 2).rearrange("p (k n) -> p k n", n=P), SX,
                                             act_hi[:, :, ds(c * P - P, P)], ALU.mult, ALU.subtract)\
                        .then_inc(S["f_ylo"], 1)
                if not done:
                    dve.wait_ge(S["f_g"], c + 1)
                    dve.wait_ge(S["f_x1a"], c + 1)
                    dve.scalar_tensor_tensor(x1[:, j, :], banks(2, 2), dinv_col[:, ds(c, 1)], x1[:, j, :], ALU.mult,
                                             ALU.add).then_inc(S["f_x1"], 1)
                    dve.wait_ge(S["f_x1"], c + 1)
                    if not (isinstance(c, int) and c < 2):
                        dve.wait_ge(S[f"rows_out{j}"], 16 * i)
                    norm_tile(x1[:, j, :], yb[:, j, :], c, "f_stat", "f_var", "f_rstd", 1e-5, "f_y")
                if conv is not None and j == 0:
                    convert(10, conv)

            chunk_loop(dve, f_body)
            f_body(T, 0, None)

            dve.wait_ge(S["r_const"], 6)
            dve.tensor_copy(iota_m[:], iota_m[:].bitcast(I32))
            dve.tensor_copy(node_f[:], node_f[:].bitcast(I32))
            dve.tensor_copy(count_down[:], count_down[:].bitcast(I32))
            dve.tensor_copy(mgroup[:, 0, :], mgroup[:, 0, :].bitcast(I32))
            dve.memset(reset[:], 1.0)
            then(dve.memset(mgroup[:, 1, :], 0.0))
            then(dve.memset(reset[:, :, 0], 0.0))
            then(dve.tensor_scalar(mpos[:, 2, 0, :], node_f[:], float(N), None, ALU.is_lt))
            then(dve.tensor_tensor(node_f[:], node_f[:], mpos[:, 2, 0, :], ALU.mult))
            dve.wait_ge(S["f_lg"], T)
            L, one1, one2, rest, tmp8 = (lg[:, n] for n in range(5))
            v1, dv, ex, v2, w1v, w2v = (sel[:, n, :] for n in range(6))
            bc = lambda a: a.unsqueeze(2).broadcast_to([P, T, EXPERTS])

            def first_largest(src, best, onehot):
                then(dve.tensor_reduce(best, src, AX.X, ALU.max))
                then(dve.tensor_tensor(tmp8, src, bc(best), ALU.is_equal))
                then(dve.tensor_tensor(tmp8, tmp8, count_down[:].unsqueeze(1).broadcast_to([P, T, EXPERTS]), ALU.mult))
                then(dve.tensor_reduce(w1v, tmp8, AX.X, ALU.max))
                then(dve.tensor_tensor(onehot, tmp8, bc(w1v), ALU.is_equal))

            then(dve.scalar_tensor_tensor(L, ps[:, 6, 0:T * EXPERTS].rearrange("p (t e) -> p t e", e=EXPERTS),
                                          1.0 / (SW * SX), rb[:].unsqueeze(1).broadcast_to([P, T, EXPERTS]),
                                          ALU.mult, ALU.add))
            first_largest(L, v1, one1)
            then(dve.scalar_tensor_tensor(rest, one1, -1e30, L, ALU.mult, ALU.add))
            first_largest(rest, v2, one2)
            dve.tensor_tensor(dv, v2, v1, ALU.subtract).then_inc(S["r_step"], 1)

            member_e, cum_e, at_e, picked = (mrank[:, n] for n in range(4))
            te = lambda a: a.rearrange("p t e -> p e t")
            then(dve.tensor_tensor(member_e, te(one1), te(one2), ALU.add))
            then(dve.tensor_tensor(member_e, member_e, mpos[:, 2, 0, :].unsqueeze(1).broadcast_to([P, EXPERTS, T]),
                                   ALU.mult))
            flat = lambda a: a.rearrange("p e t -> p (e t)")
            then(dve.tensor_tensor_scan(flat(cum_e), flat(reset[:]), flat(member_e), 0.0, ALU.mult, ALU.add))
            dve.tensor_copy(msmall[:, 0, :], cum_e[:, :, T - 1]).then_inc(S["r_tot"], 1)
            dve.wait_ge(S["r_before"], 1)
            size, ends, offs = (msmall[:, n, :] for n in (1, 2, 3))
            then(dve.tensor_scalar(size, ps[:, 7, 16:16 + EXPERTS], 1.0, float(2 * P - 1), ALU.max, ALU.add))
            then(dve.tensor_copy(msmall_i[:], size))
            then(dve.tensor_scalar(msmall_i[:], msmall_i[:], 8, 8, ALU.arith_shift_right, ALU.logical_shift_left))
            then(dve.tensor_copy(size, msmall_i[:]))
            then(dve.tensor_tensor_scan(ends, ones2[:, 0:EXPERTS], size, 0.0, ALU.mult, ALU.add))
            then(dve.tensor_tensor(offs, ends, size, ALU.subtract))
            then(dve.scalar_tensor_tensor(offs, ps[:, 7, 0:EXPERTS], -1.0, offs, ALU.add, ALU.add))
            then(dve.tensor_tensor(at_e, cum_e, offs.unsqueeze(2).broadcast_to([P, EXPERTS, T]), ALU.add))
            for k, one in enumerate((one1, one2)):
                then(dve.tensor_tensor(te(picked), one, te(at_e), ALU.mult))
                then(dve.tensor_reduce(mpos[:, 0, k, :], te(picked), AX.X, ALU.add))
                then(dve.tensor_tensor(mpos[:, 0, k, :], mpos[:, 0, k, :], mpos[:, 2, 0, :], ALU.mult))
            then(dve.tensor_copy(slot_i[:], mpos[:, 0]))
            dve.tensor_scalar(mpos_i[:, 0], slot_i[:], P - 1, None, ALU.bitwise_and)
            then(dve.tensor_scalar(mpos_i[:, 1], slot_i[:], 7, None, ALU.arith_shift_right))
            then(dve.tensor_copy(mpos[:, 0:2], mpos_i[:]))
            for k in range(TOP):
                for t in range(T):
                    dve.tensor_scalar(row_1h[:, k, t, :], iota_m[:], mpos[:, 0, k, t:t + 1], None, ALU.is_equal)
                    m = dve.tensor_scalar(tile_1h[:, k, t, :], iota_m[:, 0:MOE_TILES], mpos[:, 1, k, t:t + 1],
                                          node_f[:, t:t + 1], ALU.is_equal, ALU.mult)
            m.then_inc(S["r_1h"], 1)
            for e in range(EXPERTS - 1):
                then(dve.scalar_tensor_tensor(mgroup[:, 1, :], mgroup[:, 0, :], ends[:, e:e + 1], mgroup[:, 1, :],
                                              ALU.is_ge, ALU.add))
            dve.tensor_copy(expert_i[:], mgroup[:, 1, :]).then_inc(S["experts_made"], 1)
            dve.wait_ge(S["r_exp"], 1)
            then(dve.tensor_scalar(w2v, ex, 1.0, None, ALU.add))
            then(dve.reciprocal(cw[:, 0, :], w2v))
            then(dve.tensor_tensor(cw[:, 1, :], ex, cw[:, 0, :], ALU.mult))
            dve.wait_ge(S["nodes_ready"], 1)
            dve.tensor_copy(node_i[:], ps[:, 6, 0:MOE_TILES]).then_inc(S["nodes_made"], 1)

            def turned(g, par, h):
                dve.wait_ge(S["xT_hi"], 2 * g + h + 1)
                dve.scalar_tensor_tensor(xT_lo_t[:, par, :, h * P:(h + 1) * P],
                                         banks(0, 2).rearrange("p (k n) -> p k n", n=P), SX,
                                         xT_hi_t[:, par, :, h * P:(h + 1) * P], ALU.mult, ALU.subtract)\
                    .then_inc(S["xT_lo"], 1)

            def expert_group(g, par, last):
                if not last:
                    turned(g + 1, 1 - par, 0)
                for f in range(4):
                    dve.wait_ge(S["g_hi"], 4 * g + f + 1)
                    dve.scalar_tensor_tensor(gelu_lo[:, f, :], g32[:, f % 2, :], SX, gelu_hi[:, f, :], ALU.mult,
                                             ALU.subtract).then_inc(S["g_lo"], 1)
                    if not last:
                        for j in range(2):
                            buf = (2 * f + j) % 4
                            t = stage[:, buf, :] if buf < 2 else stage2[:, buf - 2, :]
                            dve.wait_ge(S["w_hi"], 8 * g + 8 * (DENSE + 1) + 2 * f + j + 1)
                            at = lambda part: wslot[:, 8 * (1 - par) + 4 * j + f, part, :]
                            dve.scalar_tensor_tensor(at(1), t, SW, at(0), ALU.mult, ALU.subtract)\
                                .then_inc(S["w_lo"], 1)
                if not last:
                    turned(g + 1, 1 - par, 1)
                dve.wait_ge(S[f"b2_in{par}"], 16 * trips(g) + 16)
                if not (isinstance(g, int) and g < 2):
                    dve.wait_ge(S[f"yo_out{par}"], 32 * trips(g))
                for b in range(4):
                    h, hh = b // 2, b % 2
                    dve.wait_ge(S["y_ready"], 4 * g + b + 1)
                    dve.scalar_tensor_tensor(yo[:, par, h, hh * 512:(hh + 1) * 512], ps[:, 4 + b, :], 1.0 / (SW * SX),
                                             b2_bc[:, par, hh * 512:(hh + 1) * 512], ALU.mult, ALU.add)\
                        .then_inc(S["y_evac"], 1)

            turned(0, 0, 0)
            turned(0, 0, 1)
            group_loop(dve, expert_group)

            dve.wait_ge(S["acc_in"], 16)

            def finish(c, j, i):
                dve.wait_ge(S["e_w"], c + 1)
                dve.wait_ge(S[f"x1_in{j}"], 16 * (i + 1))
                dve.tensor_tensor(fin[:, j, :], fin[:, j, :], x1in[:, j, :], ALU.add).then_inc(S["e_x"], 1)

            def end_body(c, j, conv):
                i = c // 2 if isinstance(c, int) else conv + 1
                a = acc[:, ds(c, 1), :].rearrange("p a d -> p (a d)")
                for k in range(TOP):
                    dve.wait_ge(S[f"xg_in{j}{k}"], 16 * i + 16 * (MOE_GROUPS // 2 + 2 - j))
                for k in range(TOP):
                    if k == 1:
                        dve.wait_ge(S["e_sum"], 2 * c + 1)
                    dve.scalar_tensor_tensor(a, yg[:, j, k, :], cw[:, k, ds(c, 1)], a, ALU.mult, ALU.add)\
                        .then_inc(S["e_sum"], 1)
                dve.wait_ge(S["e_sum"], 2 * c + 2)
                settle(dve)
                for hh in range(2):
                    m = dve.bn_stats(stats[:, j, 6 * hh:6 * hh + 6], a[:, hh * 512:(hh + 1) * 512])
                m.then_inc(S["f_stat"], 1)
                dve.wait_ge(S["f_stat"], 2 * T + 2 * c + 1)
                settle(dve)
                dve.bn_aggr(mv[:, j, :], stats[:, j, :]).then_inc(S["f_stat"], 1)
                dve.wait_ge(S["f_stat"], 2 * T + 2 * c + 2)
                dve.tensor_scalar(mv[:, j, 1:2], mv[:, j, 1:2], 1e-12, None, ALU.add).then_inc(S["f_var"], 1)
                if not (isinstance(c, int) and c == 0):
                    finish(c - 1, 1 - j, i - 1 + j)
                dve.wait_ge(S["f_rstd"], T + c + 1)
                dve.tensor_scalar(nmr[:, j:j + 1], mv[:, j, 0:1], rstd[:, j:j + 1], -1.0, ALU.mult, ALU.mult)\
                    .then_inc(S["e_nmr"], 1)

            chunk_loop(dve, end_body)
            finish(T - 1, 1, T // 2 - 1)


def trips(g):
    return g // 2


def unit(w, order):
    import numpy as np
    v = w.reshape(KC, P, 512)[order].reshape(4, 2, P, 512)
    return np.ascontiguousarray(v.transpose(0, 2, 1, 3)).reshape(4, P, D)


def kernel(**inputs):
    import numpy as np
    import concourse.bacc as bacc
    from concourse import mybir as mb
    from concourse.bass_utils import run_bass_kernel_spmd

    g = {k.replace("L0_", ""): np.asarray(v) for k, v in inputs.items()}
    x = np.zeros((NP, D), np.float32)
    x[:N] = g["x"]

    def edge_grid(e):
        v = np.full(EJ * P, -1, np.int32)
        v[:E] = e
        return np.ascontiguousarray(v.reshape(EJ, P).T)

    units = []
    for kk in range(2):
        for h in range(2):
            for name in ("mix_Wk", "mix_Wv"):
                units.append(unit(g[name][kk].T[:, h * 512:(h + 1) * 512], DIAG[h]))
    for w, orders in ((g["mix_Wq"].T, DIAG), (g["mix_Wo"].T, (PLAIN, PLAIN)), (g["gnn_W_neigh0"], (PLAIN, PLAIN)),
                      (g["gnn_W_self0"], (PLAIN, PLAIN)), (g["gnn_W_neigh1"], (PLAIN, PLAIN)),
                      (g["gnn_W_self1"], (PLAIN, PLAIN))):
        for h in range(2):
            units.append(unit(w[:, h * 512:(h + 1) * 512], orders[h]))
    for e in range(EXPERTS):
        units.append(unit(g["ffn_w1"][e].T, PLAIN))
        units.append(np.ascontiguousarray(g["ffn_w2"][e].T).reshape(4, P, D))

    def columns(v):
        return v.reshape(-1, P).T

    arrays = {
        "x": x, "edge_src": edge_grid(g["src"]), "edge_dst": edge_grid(g["dst"]),
        "weights": np.concatenate(units),
        "rows": np.stack([g["mix_bq"], g["mix_bk"][0], g["mix_bk"][1], g["mix_bv"][0], g["mix_bv"][1], g["gnn_b1"],
                          g["mix_bo"], g["ffn_ln_w"], g["ffn_ln_b"]]),
        "cols": np.stack([columns(g["gnn_b0"]), columns(g["mix_ln_g"]), columns(g["mix_ln_b"])], axis=1),
        "b1col": columns(g["ffn_b1"]),
        "router": g["ffn_router_w"].T.reshape(KC, P, EXPERTS).transpose(1, 0, 2),
        "router_b": g["ffn_router_b"], "b2": g["ffn_b2"],
    }
    arrays = {k: np.ascontiguousarray(v) for k, v in arrays.items()}
    nc = bacc.Bacc("TRN2", target_bir_lowering=False, num_devices=1)
    aps = [nc.dram_tensor("in_" + k, v.shape, mb.dt.from_np(v.dtype), kind="ExternalInput").ap()
           for k, v in arrays.items()]
    aps.append(nc.dram_tensor("out_y", (NP, D), mb.dt.float32, kind="ExternalOutput").ap())
    program(nc, *aps)
    r = run_bass_kernel_spmd(nc, [{"in_" + k: v for k, v in arrays.items()}], core_ids=[0])
    return r.results[0]["out_y"][:N]
```

```python
from contextlib import ExitStack

import concourse.bass as bass
from concourse import mybir

ALU = mybir.AluOpType
ACT = mybir.ActivationFunctionType
F32 = mybir.dt.float32
F16 = mybir.dt.float16
I32 = mybir.dt.int32
U32 = mybir.dt.uint32
AX = mybir.AxisListType

P = 128
N = 1250
T = -(-N // P)
NP = T * P
LAST = N - (T - 1) * P
D = 1024
KC = D // P
HD = 64
HEADS = D // HD
E = 20000
EJ = 160
TG = 4
GROUPS = 50
SPP = GROUPS * TG
ROWS = P * SPP
EXPERTS = 8
FF = 512
DENSE = 10
TOP = 2
MOE_GROUPS = TOP * N // (2 * P) + EXPERTS
MOE_TILES = 2 * MOE_GROUPS
EDGE_COPIES = 2 * EJ
SW = 256.0
SX = 16.0
SS = 4096.0
COLS = [(0, 512), (512, 512), (1024, N - 1024)]
assert GROUPS >= E // (TG * P) + T and GROUPS == 5 * T

PLAIN = list(range(KC))
DIAG = [[4 * h + q + d * (4 if h == 0 else -4) for q in range(4) for d in (0, 1)] for h in (0, 1)]


def program(nc, x, edge_src, edge_dst, weights, rows, cols, b1col, router, router_b, b2, out):
    x_t = x.rearrange("(t p) d -> p t d", p=P)
    out_t = out.rearrange("(t p) d -> p t d", p=P)
    with ExitStack() as ctx:
        dram = lambda name, shape: nc.dram_tensor(name, shape, F32, kind="Internal").ap()
        bucket_rows = dram("bucket_rows", [ROWS + P * (EJ - E // P), 2])
        mixed = dram("mixed", [NP, D]).rearrange("(t p) d -> p t d", p=P)
        selfT = dram("selfT", [D, N]).rearrange("(o p) n -> p o n", p=P)
        x1_d = dram("x1", [NP, D]).rearrange("(t p) d -> p t d", p=P)
        y_rows = dram("y", [NP, D])
        y_d = y_rows.rearrange("(t p) d -> p t d", p=P)
        moe_rows = dram("moe_rows", [MOE_TILES * P, D])

        top = [-(-nc.sbuf_base // 64) * 64]

        def region(nbytes):
            at = top[0]
            top[0] += -(-nbytes // 64) * 64
            return at

        def put(name, shape, dt, at):
            return nc.alloc_sbuf_tensor_at(name, shape, dt, offset=at)

        r1, r2 = region(4 * KC * NP), region(4 * KC * NP)
        r_adj = region(2 * T * NP)
        r_slot, r_stage = region(4 * 4 * 4096), region(2 * 4 * D)

        def small(name, shape, dt=F32):
            n = 1
            for s in shape[1:]:
                n *= s
            at = region(n * (2 if dt == F16 else 4))
            return put(name, shape, dt, at)

        act_hi = put("act_hi", [P, KC, NP], F16, r1)
        act_lo = put("act_lo", [P, KC, NP], F16, r1 + 2 * KC * NP)
        ln_hi = put("ln_hi", [P, KC, NP], F16, r2)
        ln_lo = put("ln_lo", [P, KC, NP], F16, r2 + 2 * KC * NP)
        z_hi = put("z_hi", [P, T, D], F16, r2)
        z_lo = put("z_lo", [P, T, D], F16, r2 + 2 * T * D)
        acc = put("acc", [P, T, D], F32, r2)
        adj = put("adj", [P, T, NP], F16, r_adj)
        wslot = put("wslot", [P, 16, 2, D], F16, r_slot)
        stage = put("stage", [P, 2, D], F32, r_stage)

        ident = small("ident", [P, P])
        colv = small("colv", [P, 4, KC])
        b1c = small("b1c", [P, EXPERTS * 4])
        rw16 = small("rw16", [P, KC, 2, EXPERTS], F16)
        rb = small("rb", [P, EXPERTS])
        dinv_col = small("dinv_col", [P, T])
        stats = small("stats", [P, 2, 12])
        mv = small("mv", [P, 2, 2])
        rstd = small("rstd", [P, 2])
        ssq = put("ssq", [P, 2, HEADS], F32, r_adj + 4 * 6 * D)
        nrm = put("nrm", [P, 2, HEADS], F32, r_adj + 4 * 6 * D + 4 * 2 * HEADS)
        half_pow = small("half_pow", [P, HEADS])
        mhalf_pow = small("mhalf_pow", [P, 2])
        halfc = small("halfc", [P, 1])
        r_late = top[0]
        ones16 = small("ones16", [P, P], F16)
        block_f = small("block_f", [P, GROUPS])
        block_i = small("block_i", [P, GROUPS], I32)
        colraw = small("colraw", [P, 3, KC])
        rw32 = small("rw32", [P, KC, EXPERTS])
        iota_d = small("iota_d", [P, N], F16)
        edges = small("edges", [P, SPP, 2])
        r_work = top[0]

        class Work:
            def __init__(self, at, end):
                self.at, self.end = at, end

            def __call__(self, name, shape, dt=F32):
                n = 1
                for s in shape[1:]:
                    n *= s
                t = put(name, shape, dt, self.at)
                self.at += -(-n * (2 if dt == F16 else 4) // 64) * 64
                assert self.at <= self.end, (name, self.at, self.end)
                return t

        end = nc.sbuf_usable_end
        w = Work(r2, r_adj)
        xin0 = w("xin0", [P, 2, D])
        xn0 = w("xn0", [P, 2, D])
        w = Work(r_slot + 2 * 4 * 4096, r_stage)
        ge = w("ge", [P, T + 1, EJ])
        member = w("member", [P, T, EJ])
        cum = w("cum", [P, T, EJ])
        posb = w("posb", [P, T, EJ])
        e_i = w("e_i", [P, 2, EJ], I32)
        w = Work(r2, r_adj)
        kb = w("kb", [P, 2, 512])
        ks = w("ks", [P, 2, 512])
        ksq = w("ksq", [P, 2, 512])
        v16 = w("v16", [P, 2, 512])
        k_hi_t, k_lo_t, v_hi_t, v_lo_t = (w(n, [P, 2, 512], F16) for n in ("k_hi", "k_lo", "v_hi", "v_lo"))
        bk_bc = w("bk_bc", [P, 2, D])
        bv_bc = w("bv_bc", [P, 2, D])
        w = Work(r_work, end)
        st0 = w("st0", [P, 2, 512])
        stp = w("stp", [P, 512])
        zeros16 = w("zeros16", [P, 512], F16)
        idx = w("idx", [P, EJ], I32)
        pay = w("pay", [P, EJ, 2])
        idx_b = w("idx_b", [P, 4, 1], I32)
        pay_b = w("pay_b", [P, 4, 2])
        st_hi = w("st_hi", [P, 2, 512], F16)
        st_lo = w("st_lo", [P, 2, 512], F16)
        mask = w("mask", [P, 4, P])
        bq_bc = w("bq_bc", [P, D])
        bsum_free = w.at
        w = Work(r_adj, r_slot)
        es = w("es", [P, 5, EJ])
        e_small = w("e_small", [P, 5, 16])
        ei_small = w("ei_small", [P, 16], I32)
        upper = w("upper", [P, P])
        ones32 = w("ones32", [P, P])
        minus1 = w("minus1", [P, 2 * SPP])
        bo_bc = put("bo_bc", [P, D], F32, w.at)
        iota_i = w("iota_i", [P, N], I32)
        giota_i = w("giota_i", [P, GROUPS], I32)
        giota = w("giota", [P, GROUPS])
        pid_i = w("pid_i", [P, EJ], I32)
        lnx = put("lnx", [P, D], F32, r_work)
        lnf = put("lnf", [P, D], F32, r_work + 4 * D)
        w = Work(r_adj, r_slot)
        qn = w("qn", [P, 2, D])
        qT_hi_t = w("qT_hi", [P, 2, D], F16)
        qT_lo_t = w("qT_lo", [P, 2, D], F16)
        qb = w("qb", [P, D])
        qs = w("qs", [P, D])
        w = Work(r_work, end)
        xin = w("xin", [P, 2, D])
        mo = w("mo", [P, 2, D])
        bsum = put("bsum", [P, D], F32, end // 64 * 64 - 4 * D)
        assert bsum_free <= end // 64 * 64 - 4 * D and w.at <= end // 64 * 64 - 4 * D
        w = Work(r_work, end)
        dst_1h = w("dst_1h", [P, 2, TG, N], F16)
        src_1h = w("src_1h", [P, 2, TG, P], F16)
        counts = w("counts", [P, N], F16)
        w = Work(r_work, end)
        dinv = w("dinv", [P, NP])
        s0 = w("s0", [P, 2, N])
        tg = w("tg", [P, N])
        w = Work(r_late, end)
        xm = w("xm", [P, 2, D])
        x1 = w("x1b", [P, 2, D])
        yb = w("yb", [P, 2, D])
        lnb_bc = w("lnb_bc", [P, D])
        w = Work(r_adj, r_slot)
        lg = w("lg", [P, 6, T, EXPERTS])
        sel = w("sel", [P, 6, T])
        mrank = w("mrank", [P, 4, EXPERTS, T])
        msmall = w("msmall", [P, 6, EXPERTS])
        msmall_i = w("msmall_i", [P, EXPERTS], I32)
        mgroup = w("mgroup", [P, 2, MOE_GROUPS])
        mpos = w("mpos", [P, 3, TOP, T])
        mpos_i = w("mpos_i", [P, 2, TOP, T], I32)
        node_f = w("node_f", [P, T])
        reset = w("reset", [P, EXPERTS, T])
        count_down = w("count_down", [P, EXPERTS])
        upper2 = w("upper2", [P, P])
        ones2 = w("ones2", [P, P])
        iota_m = w("iota_m", [P, P])
        row_1h = w("row_1h", [P, TOP, T, P], F16)
        tile_1h = w("tile_1h", [P, TOP, T, MOE_TILES], F16)
        assert w.at <= r_adj + 4 * 6 * D
        w = Work(r1, r2)
        xg = w("xg", [P, 2, 2, D])
        xT_hi_t = w("xT_hi", [P, 2, KC, 2 * P], F16)
        xT_lo_t = w("xT_lo", [P, 2, KC, 2 * P], F16)
        gelu_hi = w("gelu_hi", [P, 4, 2 * P], F16)
        gelu_lo = w("gelu_lo", [P, 4, 2 * P], F16)
        g32 = w("g32", [P, 2, 2 * P])
        w = Work(r_adj, r_slot)
        yo = w("yo", [P, 2, 2, D])
        b2_bc = w("b2_bc", [P, 2, D])
        cw = w("cw", [P, TOP, T])
        slot_i = w("slot_i", [P, TOP, T], I32)
        expert_i = w("expert_i", [P, MOE_GROUPS], I32)
        node_i = w("node_i", [P, MOE_TILES], I32)
        gidx = w("gidx", [P, 4, 1], I32)
        nmr = w("nmr", [P, 2])
        w = Work(r_late, end)
        lnw_bc = w("lnw_bc", [P, D])
        stage2 = w("stage2", [P, 2, D])
        x1in = put("x1in", [P, T, D], F32, r_slot + 2 * 4 * 4096)
        assert r_slot + 2 * 4 * 4096 + 4 * T * D <= r_stage + 2 * 4 * D
        w = Work(r1, r2)
        yg = w("yg", [P, 2, TOP, D])
        fin = w("fin", [P, 2, D])

        ps = ctx.enter_context(nc.psum_tensor("ps", [P, 8, 512], F32))

        def banks(b, n, width=None):
            v = ps[:, b:b + n, :].rearrange("p b n -> p (b n)")
            return v if width is None else v[:, 0:width]

        names = """x_in0 x_in1 consts_in cols_in const_made edge_in rank_step minus_out edge_tot edge_placed
            totals_made ln0_var ln0_rstd ln0_done ln0_T ln0_hi ln0_lo stage_in0 stage_in1 diag_added w_hi
            w_lo k_biased v_scaled kv_ready k_silu k_sq v_hi v_lo k_ssq k_nrm k_inv k_normed k_hi k_lo
            state_mm state_first state_step state_lo zeros_made scat0 scat1 scat2 scat3 table_in q_ready0
            q_ready1 q_biased0 q_biased1 q_silu q_sq q_ssq q_nrm q_inv q_normed qT_ready qT_hi qT_lo
            o_ready o_stat o_var o_rstd o_normed lnT_ready lnT_f lnT_hi lnT_lo wo_ready wo_biased wo_x
            zp_ready z_hi z_lo onehot grp_ready grp_copied grp_added deg_ready dinv_made dcol_ready
            dcol_made s_ready s_biased s_out0 s_out1 s_in0 s_in1 a_ready a_scaled a_sum h_hi h_lo f_s f_g
            f_x1a f_x1 f_stat f_var f_rstd f_y f_T f_yhi f_ylo f_lg rw_lo r_step r_exp acc_in r_const r_tot
            r_before experts_made r_1h nodes_ready nodes_made stage_in2 stage_in3 xg_in00 xg_in01 xg_in10
            xg_in11 x_T xT_hi xT_lo g_ready g_gelu g_hi g_lo y_ready y_evac b2_in0 b2_in1 yo_out0 yo_out1
            x1_plus e_nmr e_n e_w e_x prep_step ln0_stat passed res_in0 res_in1 res_out0 res_out1 rows_out0
            rows_out1 e_sum idx_copied bias_in xin_in0 xin_in1 out0 out1 x1_in bsum_in""".split()
        S = {n: ctx.enter_context(nc.semaphore(n)) for n in names}
        block = ctx.enter_context(nc.Block())
        ds = bass.ds

        def chunk_loop(eng, body):
            body(0, 0, None)
            body(1, 1, None)
            with eng.Fori(1, T // 2) as i:
                body(2 * i, 0, i - 1)
                body(2 * i + 1, 1, i - 1)

        def settle(eng):
            eng.sem_inc(S["passed"], 1)

        def q_loop(eng, body):
            for c in range(4):
                body(c, c % 2, None if c < 2 else 0)
            with eng.Fori(2, T // 2) as i:
                body(2 * i, 0, i - 1)
                body(2 * i + 1, 1, i - 1)
            body(T, 0, None)
            body(T + 1, 1, None)
            body(T + 2, 0, None)

        def stage_runs(c, lo, hi):
            return lo <= c < hi if isinstance(c, int) else lo <= 4 and hi >= T

        def group_loop(eng, body):
            body(0, 0, False)
            body(1, 1, False)
            with eng.Fori(1, MOE_GROUPS // 2) as i:
                body(2 * i, 0, False)
                body(2 * i + 1, 1, False)
            body(MOE_GROUPS - 1, 0, True)

        @block.sync
        def _(sp):
            def stage_load(batch, i, j):
                if batch == 0 and isinstance(i, int) and i == 0:
                    pass
                else:
                    sp.wait_ge(S["w_lo"], 8 * batch + 2 * i + j - 1)
                sp.dma_start(stage[:, j, :], weights[ds(8 * batch + 4 * j + i, 1)].rearrange("a p d -> p (a d)")).then_inc(S[f"stage_in{j}"], 16)

            def batch_load(batch):
                with sp.Fori(0, 4) as i:
                    for j in range(2):
                        stage_load(batch, i, j)

            sp.dma_start(e_i[:, 0, :], edge_src).then_inc(S["edge_in"], 16)
            sp.dma_start(e_i[:, 1, :], edge_dst).then_inc(S["edge_in"], 16)
            for c in range(2):
                sp.dma_start(xin0[:, c, :], x_t[:, c, :]).then_inc(S[f"x_in{c}"], 16)
            for j in range(2):
                stage_load(0, 0, j)
            sp.dma_start(colraw[:], cols).then_inc(S["cols_in"], 16)
            sp.dma_start(b1c[:], b1col).then_inc(S["cols_in"], 16)
            sp.dma_start(rw32[:], router).then_inc(S["cols_in"], 16)
            sp.dma_start(rb[:], router_b.partition_broadcast(P)).then_inc(S["cols_in"], 16)

            def x_load(i, j):
                sp.wait_ge(S["ln0_done"], 2 * i + j - 1)
                sp.dma_start(xin0[:, j, :], x_t[:, ds(2 * i + j, 1), :].rearrange("p a d -> p (a d)"))\
                  .then_inc(S[f"x_in{j}"], 16)

            for j in range(2):
                x_load(1, j)
            sp.dma_start(bq_bc[:], rows[0].partition_broadcast(P)).then_inc(S["consts_in"], 16)
            for k in range(2):
                sp.dma_start(bk_bc[:, k, :], rows[1 + k].partition_broadcast(P)).then_inc(S["consts_in"], 16)
                sp.dma_start(bv_bc[:, k, :], rows[3 + k].partition_broadcast(P)).then_inc(S["consts_in"], 16)
            with sp.Fori(1, 4) as i:
                x_load(i + 1, 0)
                for j in range(2):
                    stage_load(0, i, j)
                x_load(i + 1, 1)
            batch_load(1)
            sp.wait_ge(S["edge_placed"], 2)
            sp.dma_start(bsum[:], rows[5].partition_broadcast(P)).then_inc(S["bsum_in"], 16)
            sp.dma_start(bo_bc[:], rows[6].partition_broadcast(P)).then_inc(S["bsum_in"], 16)
            for batch in range(2, DENSE + 1):
                batch_load(batch)
            sp.wait_ge(S["experts_made"], 1)
            sp.wait_ge(S["w_lo"], 8 * (DENSE + 1))
            sp.wait_ge(S["nodes_made"], 1)
            for j in range(2):
                sp.wait_ge(S[f"res_out{j}"], 16 * T)
            sp.dma_start(b2_bc[:, 0, :], b2[0].partition_broadcast(P)).then_inc(S["b2_in0"], 16)

            def group_load(g, par, last):
                if last:
                    return
                e = sp.value_load(expert_i[0:1, ds(g + 1, 1)], min_val=0, max_val=EXPERTS - 1)
                for i in range(4):
                    for j in range(2):
                        buf = (2 * i + j) % 4
                        if not (isinstance(g, int) and g == 0 and i < 2):
                            sp.wait_ge(S["w_lo"], 8 * g + 8 * (DENSE + 1) + 2 * i + j - 3)
                        t = stage[:, buf, :] if buf < 2 else stage2[:, buf - 2, :]
                        sp.dma_start(t, weights[ds(8 * e + (8 * DENSE + 4 * j + i), 1)].rearrange("a p d -> p (a d)"))\
                            .then_inc(S[f"stage_in{buf}"], 16)
                if not (isinstance(g, int) and g < 1):
                    sp.wait_ge(S["y_evac"], 4 * g)
                sp.dma_start(b2_bc[:, 1 - par, :], b2[ds(e, 1), :].rearrange("a d -> (a d)").partition_broadcast(P))\
                    .then_inc(S[f"b2_in{1 - par}"], 16)

            group_loop(sp, group_load)

            sp.wait_ge(S["y_ready"], 4 * (MOE_GROUPS - 1))
            sp.wait_ge(S["w_lo"], 8 * (DENSE + MOE_GROUPS))
            sp.dma_start(x1in[:], x1_d).then_inc(S["x1_in"], 16)

            def end_move(c, j):
                sp.wait_ge(S["e_x"], c + 1)
                sp.dma_start(out_t[:, ds(c, 1), :].rearrange("p a d -> p (a d)"), fin[:, j, :])\
                    .then_inc(S[f"out{j}"], 16)

            with sp.Fori(0, T // 2) as i:
                for j in range(2):
                    end_move(2 * i + j, j)
            for j in range(2):
                sp.wait_ge(S[f"out{j}"], 16 * T // 2)

        @block.gpsimd
        def _(pool):
            pool.memset(minus1[:], -1.0).then_inc(S["zeros_made"], 1)
            pool.memset(ident[:], 0.0).then_inc(S["zeros_made"], 1)
            pool.memset(ones32[:], 1.0).then_inc(S["zeros_made"], 1)
            pool.memset(upper[:], 0.0).then_inc(S["zeros_made"], 1)
            pool.wait_ge(S["zeros_made"], 4)
            pool.affine_select(out=ident[:], in_=ident[:], compare_op=ALU.not_equal, fill=1.0, base=0,
                               pattern=[[-1, P]], channel_multiplier=1).then_inc(S["const_made"], 1)
            pool.affine_select(out=upper[:], in_=ones32[:], compare_op=ALU.is_gt, fill=0.0, base=0,
                               pattern=[[1, P]], channel_multiplier=-1).then_inc(S["const_made"], 1)
            pool.memset(ones16[:], 1.0).then_inc(S["const_made"], 1)
            pool.memset(half_pow[:], 0.5).then_inc(S["const_made"], 1)
            pool.memset(mhalf_pow[:], -0.5).then_inc(S["const_made"], 1)
            pool.memset(halfc[:], 0.5).then_inc(S["const_made"], 1)
            pool.memset(zeros16[:], 0.0).then_inc(S["const_made"], 1)
            pool.iota(iota_i[:], pattern=[[1, N]], base=0, channel_multiplier=0).then_inc(S["const_made"], 1)
            pool.iota(giota_i[:], pattern=[[TG * P, GROUPS]], base=0, channel_multiplier=0)\
                .then_inc(S["const_made"], 1)
            pool.iota(pid_i[:], pattern=[[P, EJ]], base=ROWS - P * (E // P), channel_multiplier=1).then_inc(S["const_made"], 1)
            pool.wait_ge(S["zeros_made"], 1)
            pool.dma_start(bucket_rows[0:ROWS, :].rearrange("(p s) c -> p (s c)", p=P), minus1[:])\
                .then_inc(S["minus_out"], 16)
            pool.wait_ge(S["const_made"], 10)
            with pool.Fori(0, T) as c:
                pool.wait_ge(S["ln0_var"], c + 1)
                pool.tensor_tensor(rstd[:, 0:1], mv[:, 0, 1:2], mhalf_pow[:, 0:1], ALU.pow).then_inc(S["ln0_rstd"], 1)

            def kv(g):
                pool.wait_ge(S["k_ssq"], g + 1)
                pool.tensor_tensor(nrm[:, 0, 0:8], ssq[:, 0, 0:8], half_pow[:, 0:8], ALU.pow).then_inc(S["k_nrm"], 1)

            def place(g, first):
                for q in range(4):
                    if not first:
                        pool.wait_ge(S[f"scat{q}"], 16 * g)
                    pool.tensor_copy(idx_b[:, q, :], idx[:, ds(4 * g + q, 1)]).then_inc(S["idx_copied"], 1)
                    pool.tensor_copy(pay_b[:, q, :], pay[:, ds(4 * g + q, 1), :].rearrange("p a c -> p (a c)"))\
                        .then_inc(S["idx_copied"], 1)
                    pool.wait_ge(S["idx_copied"], 8 * g + 2 * q + 2)
                    settle(pool)
                    pool.indirect_dma_start(
                        out=bucket_rows, out_offset=bass.IndirectOffsetOnAxis(ap=idx_b[:, q, :].bitcast(U32), axis=0),
                        in_=pay_b[:, q, :], in_offset=None).then_inc(S[f"scat{q}"], 16)

            for g in range(3):
                kv(g)
            pool.wait_ge(S["edge_placed"], 2)
            pool.wait_ge(S["minus_out"], 16)
            place(0, True)
            with pool.Fori(3, 4 * T) as g:
                kv(g)
                place(g - 2, False)
            place(4 * T - 2, False)

            def q_body(c, j, conv):
                at = lambda lo, hi: stage_runs(c, lo, hi)
                if at(1, T + 1):
                    pool.wait_ge(S["q_ssq"], c)
                    pool.tensor_tensor(nrm[:, 1, :], ssq[:, 1, :], half_pow[:], ALU.pow).then_inc(S["q_nrm"], 1)
                if at(1, 2):
                    place(4 * T - 1, False)
                    for q in range(4):
                        pool.wait_ge(S[f"scat{q}"], 16 * 4 * T)
                    pool.dma_start(edges[:].rearrange("p s c -> p (s c)"),
                                   bucket_rows[0:ROWS, :].rearrange("(p s) c -> p (s c)", p=P)).then_inc(S["table_in"], 16)
                if at(2, T + 2):
                    pool.wait_ge(S["o_var"], c - 1)
                    pool.tensor_tensor(rstd[:, 0:1], mv[:, 0, 1:2], mhalf_pow[:, 0:1], ALU.pow).then_inc(S["o_rstd"], 1)

            q_loop(pool, q_body)

            pool.wait_ge(S["lnT_lo"], T)
            for j in range(2):
                pool.dma_start(xin[:, j, :], x_t[:, j, :]).then_inc(S[f"xin_in{j}"], 16)
            pool.memset(adj[:], 0.0).then_inc(S["zeros_made"], 1)

            def wo_body(c, j, conv):
                pool.wait_ge(S["wo_x"], c + 1)
                pool.dma_start(mixed[:, ds(c, 1), :].rearrange("p a d -> p (a d)"), mo[:, j, :])\
                    .then_inc(S[f"res_out{j}"], 16)

            def wo_load(c, j):
                pool.dma_start(xin[:, j, :], x_t[:, ds(c, 1), :].rearrange("p a d -> p (a d)"))\
                    .then_inc(S[f"xin_in{j}"], 16)

            with pool.Fori(0, T // 2 - 1) as i:
                for j in range(2):
                    wo_body(2 * i + j, j, None)
                    wo_load(2 * i + j + 2, j)
            wo_body(T - 2, 0, None)
            wo_body(T - 1, 1, None)

            with pool.Fori(0, KC // 2) as i:
                for j in range(2):
                    pool.wait_ge(S["s_biased"], 2 * i + j + 1)
                    pool.dma_start(selfT[:, ds(2 * i + j, 1), :].rearrange("p a d -> p (a d)"), s0[:, j, :])\
                        .then_inc(S[f"s_out{j}"], 16)
            for j in range(2):
                pool.wait_ge(S[f"s_out{j}"], 16 * KC // 2)
            for j in range(2):
                pool.dma_start(s0[:, j, :], selfT[:, j, :]).then_inc(S[f"s_in{j}"], 16)
            with pool.Fori(1, KC // 2) as i:
                for j in range(2):
                    pool.wait_ge(S["h_lo"], 2 * i + j - 1)
                    pool.dma_start(s0[:, j, :], selfT[:, ds(2 * i + j, 1), :].rearrange("p a d -> p (a d)"))\
                        .then_inc(S[f"s_in{j}"], 16)

            pool.wait_ge(S["h_lo"], KC)
            for j in range(2):
                pool.wait_ge(S[f"res_out{j}"], 16 * T // 2)
            for j in range(2):
                pool.dma_start(xm[:, j, :], mixed[:, j, :]).then_inc(S[f"res_in{j}"], 16)
            pool.dma_start(lnb_bc[:], rows[8].partition_broadcast(P)).then_inc(S["bias_in"], 16)
            pool.wait_ge(S["bias_in"], 16)

            def f_body(c, j, last):
                pool.wait_ge(S["f_var"], c + 1)
                pool.tensor_tensor(rstd[:, 0:1], mv[:, 0, 1:2], mhalf_pow[:, 0:1], ALU.pow).then_inc(S["f_rstd"], 1)
                if not last:
                    pool.wait_ge(S["f_x1a"], c + 1)
                    pool.dma_start(xm[:, j, :], mixed[:, ds(c + 2, 1), :].rearrange("p a d -> p (a d)"))\
                        .then_inc(S[f"res_in{j}"], 16)
                pool.wait_ge(S["f_y"], c + 1)
                settle(pool)
                pool.dma_start(y_d[:, ds(c, 1), :].rearrange("p a d -> p (a d)"), yb[:, j, :])\
                    .then_inc(S[f"rows_out{j}"], 16)
                pool.tensor_tensor(x1[:, j, :], x1[:, j, :], lnb_bc[:], ALU.add).then_inc(S["x1_plus"], 1)
                pool.wait_ge(S["x1_plus"], c + 1)
                settle(pool)
                pool.dma_start(x1_d[:, ds(c, 1), :].rearrange("p a d -> p (a d)"), x1[:, j, :])\
                    .then_inc(S[f"res_out{j}"], 16)

            with pool.Fori(0, T // 2 - 1) as i:
                for j in range(2):
                    f_body(2 * i + j, j, False)
            f_body(T - 2, 0, True)
            pool.wait_ge(S["f_g"], T)
            pool.memset(ones2[:], 1.0).then_inc(S["r_const"], 1)
            pool.wait_ge(S["r_const"], 1)
            pool.affine_select(out=upper2[:], in_=ones2[:], compare_op=ALU.is_gt, fill=0.0, base=0,
                               pattern=[[1, P]], channel_multiplier=-1).then_inc(S["r_const"], 1)
            pool.iota(iota_m[:].bitcast(I32), pattern=[[1, P]], base=0, channel_multiplier=0).then_inc(S["r_const"], 1)
            pool.iota(node_f[:].bitcast(I32), pattern=[[P, T]], base=0, channel_multiplier=1).then_inc(S["r_const"], 1)
            pool.iota(count_down[:].bitcast(I32), pattern=[[-1, EXPERTS]], base=EXPERTS, channel_multiplier=0)\
                .then_inc(S["r_const"], 1)
            pool.iota(mgroup[:, 0, :].bitcast(I32), pattern=[[2 * P, MOE_GROUPS]], base=0, channel_multiplier=0)\
                .then_inc(S["r_const"], 1)
            f_body(T - 1, 1, True)
            for j in range(2):
                pool.wait_ge(S[f"rows_out{j}"], 16 * T // 2)
            for j in range(2):
                pool.wait_ge(S[f"res_out{j}"], 16 * T)
            pool.dma_start(acc[:], y_d).then_inc(S["acc_in"], 16)
            pool.wait_ge(S["f_ylo"], T)
            pool.dma_start(lnw_bc[:], rows[7].partition_broadcast(P)).then_inc(S["bias_in"], 16)
            pool.wait_ge(S["f_lg"], T)
            pool.wait_ge(S["nodes_made"], 1)

            def gather(g, par):
                for h in range(2):
                    n = 2 * g + h
                    b = 2 * par + h
                    if not (isinstance(g, int) and g < 2):
                        pool.wait_ge(S["x_T"], n - 3)
                    pool.tensor_copy(gidx[:, b, :], node_i[:, ds(n, 1)]).then_inc(S["idx_copied"], 1)
                    pool.wait_ge(S["idx_copied"], EDGE_COPIES + n + 1)
                    settle(pool)
                    pool.indirect_dma_start(
                        out=xg[:, par, h, :], out_offset=None, in_=y_rows,
                        in_offset=bass.IndirectOffsetOnAxis(ap=gidx[:, b, :].bitcast(U32), axis=0))\
                        .then_inc(S[f"xg_in{par}{h}"], 16)

            gather(0, 0)
            gather(1, 1)

            def group_move(g, par, ahead=True):
                if ahead:
                    gather(g + 2, par)
                for h in range(2):
                    pool.wait_ge(S["y_evac"], 4 * g + 2 * h + 2)
                    settle(pool)
                    pool.dma_start(moe_rows[ds(256 * g + P * h, P), :], yo[:, par, h, :]).then_inc(S[f"yo_out{par}"], 16)

            with pool.Fori(0, MOE_GROUPS // 2 - 1) as i:
                group_move(2 * i, 0)
                group_move(2 * i + 1, 1)
            group_move(MOE_GROUPS - 3, 0)
            group_move(MOE_GROUPS - 2, 1, False)
            group_move(MOE_GROUPS - 1, 0, False)
            pool.wait_ge(S["bias_in"], 16 * 2)
            pool.wait_ge(S["yo_out0"], 16 * 2 * (MOE_GROUPS // 2 + 1))
            pool.wait_ge(S["yo_out1"], 16 * 2 * (MOE_GROUPS // 2))

            def take(c, j):
                for k in range(TOP):
                    n = TOP * c + k
                    pool.tensor_copy(gidx[:, 2 * j + k, :], slot_i[:, k, ds(c, 1)]).then_inc(S["idx_copied"], 1)
                    pool.wait_ge(S["idx_copied"], EDGE_COPIES + MOE_TILES + n + 1)
                    settle(pool)
                    pool.indirect_dma_start(
                        out=yg[:, j, k, :], out_offset=None, in_=moe_rows,
                        in_offset=bass.IndirectOffsetOnAxis(ap=gidx[:, 2 * j + k, :].bitcast(U32), axis=0))\
                        .then_inc(S[f"xg_in{j}{k}"], 16)

            def end_body(c, j, last):
                pool.wait_ge(S["f_var"], T + c + 1)
                pool.tensor_tensor(rstd[:, j:j + 1], mv[:, j, 1:2], mhalf_pow[:, 0:1], ALU.pow).then_inc(S["f_rstd"], 1)
                if not last:
                    take(c + 2, j)
                pool.wait_ge(S["e_n"], c + 1)
                pool.tensor_tensor(fin[:, j, :], fin[:, j, :], lnw_bc[:], ALU.mult).then_inc(S["e_w"], 1)

            take(0, 0)
            take(1, 1)
            with pool.Fori(0, T // 2 - 1) as i:
                for j in range(2):
                    end_body(2 * i + j, j, False)
            end_body(T - 2, 0, True)
            end_body(T - 1, 1, True)

        @block.tensor
        def _(pe):
            def w_at(slot, pos, part, c0, n):
                o = (pos % 2) * 512 + c0
                return wslot[:, 4 * slot + pos // 2, part, o:o + n]

            def nodes_unit(bank, hi, lo, slots, order, part=range(KC)):
                for pos in part:
                    for s, b in zip(slots, bank):
                        lh, ll = hi(order[pos]), lo(order[pos])
                        pe.matmul(ps[:, b, :], lh, w_at(s, pos, 0, 0, 512), start=(pos == 0), stop=False)
                        pe.matmul(ps[:, b, :], lh, w_at(s, pos, 1, 0, 512), start=False, stop=False)
                        m = pe.matmul(ps[:, b, :], ll, w_at(s, pos, 0, 0, 512), start=False, stop=(pos == KC - 1))
                return m

            def tile_of(t, c):
                return lambda k: t[:, k, ds(c * P, P)] if not isinstance(c, int) else t[:, k, c * P:(c + 1) * P]

            def transposes(bank, src):
                for k in range(KC):
                    m = pe.matmul(ps[:, bank + k // 4, (k % 4) * P:(k % 4 + 1) * P], src[:, k * P:(k + 1) * P],
                                  ident[:], start=True, stop=True, is_transpose=True)
                return m

            pe.wait_ge(S["const_made"], 10)
            pe.wait_ge(S["edge_tot"], 1)
            pe.matmul(ps[:, 7, 0:T], upper[:], e_small[:, 0, 0:T], start=True, stop=True)
            pe.matmul(ps[:, 7, 16:16 + T], ones32[:], e_small[:, 0, 0:T], start=True, stop=True)\
              .then_inc(S["totals_made"], 1)

            def ln0(c, j, conv):
                pe.wait_ge(S["ln0_done"], c + 1)
                if not (isinstance(c, int) and c < 2):
                    pe.wait_ge(S["ln0_lo"], c - 1)
                transposes(4 + 2 * j, xn0[:, j, :]).then_inc(S["ln0_T"], 1)

            def early_kv(tile, chunks):
                return nodes_unit([2 * tile, 2 * tile + 1], tile_of(act_hi, tile), tile_of(act_lo, tile), [0, 1],
                                  DIAG[0], chunks)

            for c in range(4):
                ln0(c, c % 2, None)
            for i in range(2, T // 2):
                pe.wait_ge(S["w_lo"], 2 * (i - 1))
                for j in range(2):
                    ln0(2 * i + j, j, None)
                    early_kv(j, range(2 * (i - 2), 2 * (i - 1)))
            pe.wait_ge(S["w_lo"], 8)
            for tile in range(2):
                early_kv(tile, range(KC - 2, KC)).then_inc(S["kv_ready"], 1)

            def states(g, j, rows_, sbank):
                pe.wait_ge(S["v_lo"], g + 1)
                pe.wait_ge(S["k_lo"], g + 1)
                for p in range(4):
                    o = ps[:, sbank, p * P:(p + 1) * P]
                    for a, b in ((k_hi_t, v_hi_t), (k_hi_t, v_lo_t), (k_lo_t, v_hi_t)):
                        m = pe.matmul(o, a[0:rows_, j, p * P:(p + 1) * P], b[0:rows_, j, p * P:(p + 1) * P],
                                      start=False, stop=False, skip_group_check=True)
                m.then_inc(S["state_mm"], 1)

            for ph in range(4):
                h = ph % 2
                slot = 2 * (ph % 2)
                sbank = 4 + ph % 2
                pe.wait_ge(S["w_lo"], 8 * (ph + 1))
                if ph == 0:
                    pe.wait_ge(S["ln0_lo"], T)
                if ph >= 2:
                    pe.wait_ge(S["state_first"], ph - 1)
                pe.matmul(ps[:, sbank, :], zeros16[:, 0:P], zeros16[:], start=True, stop=False,
                          skip_group_check=True)

                def kv(c, j, conv, ph=ph, h=h, slot=slot, sbank=sbank):
                    g = T * ph + c
                    if not (isinstance(c, int) and g < 2):
                        pe.wait_ge(S["v_scaled"], g - 1)
                        nodes_unit([2 * j, 2 * j + 1], tile_of(act_hi, c), tile_of(act_lo, c),
                                   [slot, slot + 1], DIAG[h]).then_inc(S["kv_ready"], 1)
                    if not (isinstance(c, int) and c == 0):
                        states(g - 1, 1 - j, P, sbank)
                    elif ph > 0:
                        states(g - 1, 1 - j, LAST, 9 - sbank)

                kv(0, 0, None)
                kv(1, 1, None)
                with pe.Fori(1, T // 2) as i:
                    kv(2 * i, 0, None)
                    kv(2 * i + 1, 1, None)

            pe.wait_ge(S["w_lo"], 8 * 5)
            pe.wait_ge(S["v_scaled"], 4 * T - 1)

            def q_body(c, j, conv):
                at = lambda lo, hi: stage_runs(c, lo, hi)
                hi, lo = tile_of(act_hi, c), tile_of(act_lo, c)
                if at(T, T + 1):
                    wo_body(0, 0, range(4))
                if at(0, T):
                    if at(1, T):
                        pe.wait_ge(S["q_biased0"], c)
                    nodes_unit([0], hi, lo, [0], DIAG[0]).then_inc(S["q_ready0"], 1)
                if at(2, T + 2):
                    if at(2, 3):
                        pe.wait_ge(S["state_lo"], 2)
                    pe.wait_ge(S["qT_lo"], c - 1)
                    if at(3, T + 2):
                        pe.wait_ge(S["o_normed"], c - 2)
                    for p in range(KC):
                        o = ps[:, 4 + p // 4, (p % 4) * P:(p % 4 + 1) * P]
                        s = lambda t: t[:, p // 4, (p % 4) * P:(p % 4 + 1) * P]
                        q = lambda t: t[:, j, p * P:(p + 1) * P]
                        pe.matmul(o, q(qT_hi_t), s(st_hi), start=True, stop=False)
                        pe.matmul(o, q(qT_hi_t), s(st_lo), start=False, stop=False)
                        m = pe.matmul(o, q(qT_lo_t), s(st_hi), start=False, stop=True)
                    m.then_inc(S["o_ready"], 1)
                if at(3, T + 3):
                    pe.wait_ge(S["o_normed"], c - 2)
                    if at(4, T + 3):
                        pe.wait_ge(S["lnT_f"], c - 3)
                    transposes(6, lnx).then_inc(S["lnT_ready"], 1)
                if at(0, T):
                    if at(1, T):
                        pe.wait_ge(S["q_biased1"], c)
                    nodes_unit([1], hi, lo, [1], DIAG[1]).then_inc(S["q_ready1"], 1)
                if at(0, 1):
                    states(4 * T - 1, 1, LAST, 5)
                if at(T, T + 1):
                    wo_body(0, 0, range(4, KC))
                if at(T + 1, T + 2):
                    wo_body(1, 1)
                if at(1, T + 1):
                    pe.wait_ge(S["q_normed"], c)
                    if at(2, T + 1):
                        pe.wait_ge(S["qT_lo"], c - 1)
                    transposes(2, qn[:, 1 - j, :]).then_inc(S["qT_ready"], 1)

            def wo_body(c, j, part=range(KC)):
                if isinstance(c, int) and c == 0:
                    pe.wait_ge(S["w_lo"], 8 * 6)
                    pe.wait_ge(S["q_biased1"], T)
                    pe.wait_ge(S["lnT_lo"], 1)
                elif isinstance(c, int) and c == 1:
                    pe.wait_ge(S["qT_lo"], T)
                    pe.wait_ge(S["lnT_lo"], 2)
                elif isinstance(c, int):
                    pe.wait_ge(S["o_normed"], T)
                    pe.wait_ge(S["lnT_f" if c == 3 else "lnT_lo"], T if c == 3 else 3)
                    if c == 3:
                        pe.wait_ge(S["lnT_lo"], 4)
                else:
                    pe.wait_ge(S["wo_biased"], c - 1)
                b = 2 * c if isinstance(c, int) else 2 * j
                m = nodes_unit([b, b + 1], tile_of(ln_hi, c), tile_of(ln_lo, c), [2, 3], PLAIN, part)
                if KC - 1 in part:
                    m.then_inc(S["wo_ready"], 1)

            q_loop(pe, q_body)

            wo_body(2, 0)
            wo_body(3, 1)
            pe.wait_ge(S["lnT_lo"], T)
            with pe.Fori(2, T // 2) as i:
                wo_body(2 * i, 0)
                wo_body(2 * i + 1, 1)

            pe.wait_ge(S["w_lo"], 8 * 7)
            pe.wait_ge(S["wo_biased"], T)
            pe.wait_ge(S["lnT_f"], T)

            def group(g, par, first):
                pe.wait_ge(S["onehot"], g + 1)
                if not first:
                    pe.wait_ge(S["grp_copied"], g - 1)
                for t in range(TG):
                    for n, (c0, w_) in enumerate(COLS):
                        m = pe.matmul(ps[:, 3 * par + n, 0:w_], src_1h[:, par, t, :], dst_1h[:, par, t, c0:c0 + w_],
                                      start=(t == 0), stop=(t == TG - 1))
                m.then_inc(S["grp_ready"], 1)

            def z_body(c, j, conv):
                if not (isinstance(c, int) and c == 0):
                    pe.wait_ge(S["z_lo"], c)
                whole = isinstance(c, int) and c == 0
                for q in range(5):
                    if q == 0 or (q < 4 and not whole):
                        m = nodes_unit([6, 7], tile_of(act_hi, c), tile_of(act_lo, c), [0, 1], PLAIN,
                                       range(KC) if whole else range(2 * q, 2 * q + 2))
                    if q == (0 if whole else 3):
                        m.then_inc(S["zp_ready"], 1)
                    group(5 * c + q, (5 * j + q) % 2, isinstance(c, int) and 5 * c + q < 2)

            chunk_loop(pe, z_body)
            pe.wait_ge(S["w_lo"], 8 * 8)
            pe.wait_ge(S["grp_copied"], GROUPS - 1)

            def feature_unit(bank, lhs, last_k, rhs_hi, rhs_lo):
                for k in range(last_k):
                    lh, ll = lhs(k)
                    for n, (c0, w_) in enumerate(COLS):
                        pe.matmul(ps[:, bank + n, 0:w_], lh, rhs_hi(k, c0, w_), start=(k == 0), stop=False)
                    if rhs_lo is not None:
                        for n, (c0, w_) in enumerate(COLS):
                            pe.matmul(ps[:, bank + n, 0:w_], lh, rhs_lo(k, c0, w_), start=False, stop=False)
                    for n, (c0, w_) in enumerate(COLS):
                        m = pe.matmul(ps[:, bank + n, 0:w_], ll, rhs_hi(k, c0, w_), start=False, stop=(k == last_k - 1))
                return m

            def s_chunk(u, i, j):
                o = 4 * u + 2 * i + j
                if not (u == 0 and isinstance(i, int) and i == 0):
                    pe.wait_ge(S["s_biased"], o - 1)

                def lhs(k):
                    at = lambda part: wslot[:, 4 * (2 + u) + k // 2, part, ds((k % 2) * 512 + (2 * i + j) * P, P)]
                    return at(0), at(1)
                feature_unit(3 * j, lhs, KC, lambda k, c0, w_: act_hi[:, k, c0:c0 + w_],
                             lambda k, c0, w_: act_lo[:, k, c0:c0 + w_]).then_inc(S["s_ready"], 1)

            for u in range(2):
                if u == 0:
                    s_chunk(0, 0, 0)
                    pe.wait_ge(S["grp_added"], GROUPS)
                    for n, w_ in enumerate((512, 512, NP - 1024)):
                        for s in range(T):
                            m = pe.matmul(ps[:, 5 + n, 0:w_], ones16[:], adj[:, s, n * 512:n * 512 + w_],
                                          start=(s == 0), stop=(s == T - 1))
                    m.then_inc(S["deg_ready"], 1)
                    pe.wait_ge(S["dinv_made"], 1)
                    s_chunk(0, 0, 1)
                    pe.wait_ge(S["dinv_made"], 2)
                    for t in range(T):
                        m = pe.matmul(ps[:, 7, t:t + 1], dinv[0:1, t * P:(t + 1) * P], ident[0:1, 0:1],
                                      start=True, stop=True)
                    m.then_inc(S["dcol_ready"], 1)
                with pe.Fori(1 - u, 2) as i:
                    s_chunk(u, i, 0)
                    s_chunk(u, i, 1)

            pe.wait_ge(S["s_biased"], KC)
            pe.wait_ge(S["z_lo"], T)

            def a_chunk(o, j, first):
                if not first:
                    pe.wait_ge(S["a_scaled"], o - 1)
                feature_unit(3 * j, lambda s: (z_hi[:, s, ds(o * P, P)], z_lo[:, s, ds(o * P, P)]), T,
                             lambda s, c0, w_: adj[:, s, c0:c0 + w_], None).then_inc(S["a_ready"], 1)

            a_chunk(0, 0, True)
            a_chunk(1, 1, True)
            with pe.Fori(1, KC // 2) as i:
                a_chunk(2 * i, 0, False)
                a_chunk(2 * i + 1, 1, False)

            pe.wait_ge(S["w_lo"], 8 * 9)
            pe.wait_ge(S["h_lo"], KC - 1)

            def z1_body(c, j, conv):
                if not (isinstance(c, int) and c < 2):
                    pe.wait_ge(S["z_lo"], T + c - 1)
                first = isinstance(c, int) and c == 0
                if first:
                    nodes_unit([0, 1], tile_of(act_hi, c), tile_of(act_lo, c), [0, 1], PLAIN, range(KC - 1))
                    pe.wait_ge(S["h_lo"], KC)
                nodes_unit([2 * j, 2 * j + 1], tile_of(act_hi, c), tile_of(act_lo, c), [0, 1], PLAIN,
                           range(KC - 1 if first else 0, KC)).then_inc(S["zp_ready"], 1)

            chunk_loop(pe, z1_body)

            pe.wait_ge(S["w_lo"], 8 * 10)
            pe.wait_ge(S["z_lo"], 2 * T - 1)
            pe.wait_ge(S["rw_lo"], 1)

            def f_body(c, j, conv):
                done = isinstance(c, int) and c >= T
                zero = isinstance(c, int) and c == 0
                if not done:
                    if not zero:
                        pe.wait_ge(S["f_x1a"], c)
                    nodes_unit([0, 1], tile_of(act_hi, c), tile_of(act_lo, c), [2, 3], PLAIN)\
                        .then_inc(S["f_s"], 1)
                if not zero:
                    pe.wait_ge(S["f_y"], c)
                    if not (isinstance(c, int) and c == 1):
                        pe.wait_ge(S["f_ylo"], c - 1)
                    transposes(4, yb[:, 1 - j, :]).then_inc(S["f_T"], 1)
                if not done:
                    if zero:
                        pe.wait_ge(S["z_lo"], 2 * T)
                    else:
                        pe.wait_ge(S["f_x1"], c)
                    for s in range(T):
                        a = adj[:, s, ds(c * P, P)]
                        for hh in range(2):
                            pe.matmul(ps[:, 2 + hh, :], a, z_hi[:, s, hh * 512:(hh + 1) * 512], start=(s == 0), stop=False)
                            m = pe.matmul(ps[:, 2 + hh, :], a, z_lo[:, s, hh * 512:(hh + 1) * 512],
                                          start=False, stop=(s == T - 1))
                    m.then_inc(S["f_g"], 1)
                if not zero:
                    pe.wait_ge(S["f_ylo"], c)
                    for k in range(KC):
                        col = ds(c * P - P, P)
                        o = ps[:, 6, ds(c * EXPERTS - EXPERTS, EXPERTS)]
                        pe.matmul(o, act_hi[:, k, col], rw16[:, k, 0, :], start=(k == 0), stop=False)
                        pe.matmul(o, act_hi[:, k, col], rw16[:, k, 1, :], start=False, stop=False)
                        m = pe.matmul(o, act_lo[:, k, col], rw16[:, k, 0, :], start=False, stop=(k == KC - 1))
                    m.then_inc(S["f_lg"], 1)

            chunk_loop(pe, f_body)
            f_body(T, 0, None)

            pe.wait_ge(S["r_const"], 2)
            pe.wait_ge(S["r_tot"], 1)
            pe.matmul(ps[:, 7, 0:EXPERTS], upper2[:], msmall[:, 0, :], start=True, stop=True)
            pe.matmul(ps[:, 7, 16:16 + EXPERTS], ones2[:], msmall[:, 0, :], start=True, stop=True)\
              .then_inc(S["r_before"], 1)
            pe.wait_ge(S["r_1h"], 1)
            for k in range(TOP):
                for t in range(T):
                    m = pe.matmul(ps[:, 6, 0:MOE_TILES], row_1h[:, k, t, :], tile_1h[:, k, t, :],
                                  start=(k == 0 and t == 0), stop=(k == TOP - 1 and t == T - 1))
            m.then_inc(S["nodes_ready"], 1)
            pe.wait_ge(S["nodes_made"], 1)

            def turn(g, par, h, trip, bank=0):
                pe.wait_ge(S[f"xg_in{par}{h}"], 16 * trip + 16)
                if not (isinstance(g, int) and g == 0):
                    pe.wait_ge(S["xT_lo"], 2 * g + h)
                transposes(bank, xg[:, par, h, :]).then_inc(S["x_T"], 1)

            def expert_group(g, par, last):
                slot = 2 * par
                if not last:
                    turn(g + 1, 1 - par, 0, trips(g + 1))
                pe.wait_ge(S["w_lo"], 8 * g + 8 * (DENSE + 1))
                pe.wait_ge(S["xT_lo"], 2 * g + 2)
                for f in range(4):
                    if not (isinstance(g, int) and g == 0 and f < 2):
                        pe.wait_ge(S["g_gelu"], 4 * g + f - 1)
                    for k in range(KC):
                        rh, rl = xT_hi_t[:, par, k, :], xT_lo_t[:, par, k, :]
                        o = ps[:, 2 + f % 2, 0:2 * P]
                        pe.matmul(o, w_at(slot, k, 0, f * P, P), rh, start=(k == 0), stop=False)
                        pe.matmul(o, w_at(slot, k, 0, f * P, P), rl, start=False, stop=False)
                        m = pe.matmul(o, w_at(slot, k, 1, f * P, P), rh, start=False, stop=(k == KC - 1))
                    m.then_inc(S["g_ready"], 1)
                if not last:
                    turn(g + 1, 1 - par, 1, trips(g + 1))
                for k in range(4):
                    pe.wait_ge(S["g_lo"], 4 * g + k + 1)
                    for b in range(4):
                        h, hh = b // 2, b % 2
                        if k == 0 and not (isinstance(g, int) and g == 0):
                            pe.wait_ge(S["y_evac"], 4 * g + b - 3)
                        gh, gl = gelu_hi[:, k, h * P:(h + 1) * P], gelu_lo[:, k, h * P:(h + 1) * P]
                        wh, wl = (wslot[:, 4 * (slot + 1) + k, part, hh * 512:(hh + 1) * 512] for part in (0, 1))
                        pe.matmul(ps[:, 4 + b, :], gh, wh, start=(k == 0), stop=False)
                        pe.matmul(ps[:, 4 + b, :], gh, wl, start=False, stop=False)
                        m = pe.matmul(ps[:, 4 + b, :], gl, wh, start=False, stop=(k == 3))
                        if k == 3:
                            m.then_inc(S["y_ready"], 1)

            turn(0, 0, 0, 0)
            turn(0, 0, 1, 0, bank=6)
            group_loop(pe, expert_group)

        @block.scalar
        def _(act):
            act.preload_act_table(ACT.Silu)

            def convert(batch, i, diag):
                for j in range(2):
                    if diag:
                        act.wait_ge(S["diag_added"], 8 * batch + 2 * i + j + 1)
                    else:
                        act.wait_ge(S[f"stage_in{j}"], 16 * (4 * batch + i + 1))
                    settle(act)
                    slot = 8 * (batch % 2) + 4 * j
                    act.activation(wslot[:, ds(slot + i, 1), 0, :].rearrange("p a d -> p (a d)"), stage[:, j, :],
                                   ACT.Copy, scale=SW).then_inc(S["w_hi"], 1)

            act.wait_ge(S["cols_in"], 64)
            act.activation(colv[:, 0, :], colraw[:, 0, :], ACT.Copy).then_inc(S["prep_step"], 1)
            act.activation(colv[:, 2:4, :], colraw[:, 1:3, :], ACT.Copy, scale=SX).then_inc(S["prep_step"], 1)
            act.activation(colv[:, 1, :], colraw[:, 0, :], ACT.Copy, scale=SX).then_inc(S["prep_step"], 1)
            act.wait_ge(S["prep_step"], 3)
            act.activation(rw16[:, :, 0, :], rw32[:], ACT.Copy, scale=SW).then_inc(S["prep_step"], 1)

            def ln0(c, j, conv):
                act.wait_ge(S["ln0_T"], c + 1)
                settle(act)
                act.activation(act_hi[:, :, ds(c * P, P)],
                               banks(4 + 2 * j, 2).rearrange("p (k n) -> p k n", n=P), ACT.Copy, scale=SX)\
                    .then_inc(S["ln0_hi"], 1)
                if conv is not None and j == 0:
                    convert(0, conv, True)

            chunk_loop(act, ln0)
            act.wait_ge(S["consts_in"], 16 * 5)
            act.activation(bv_bc[:], bv_bc[:], ACT.Copy, scale=SX).then_inc(S["prep_step"], 1)

            for ph in range(4):
                def kv(c, j, conv, ph=ph):
                    g = T * ph + c
                    act.wait_ge(S["k_biased"], g + 1)
                    act.activation(ks[:, j, :], kb[:, j, :], ACT.Silu).then_inc(S["k_silu"], 1)
                    act.wait_ge(S["k_silu"], g + 1)
                    act.activation(ksq[:, j, :], ks[:, j, :], ACT.Square, bias=halfc[:]).then_inc(S["k_sq"], 1)
                    act.wait_ge(S["v_scaled"], g + 1)
                    if not (isinstance(c, int) and g < 2):
                        act.wait_ge(S["state_mm"], g - 1)
                    act.activation(v_hi_t[:, j, :], v16[:, j, :], ACT.Copy).then_inc(S["v_hi"], 1)
                    act.wait_ge(S["k_normed"], g + 1)
                    act.activation(k_hi_t[:, j, :], kb[:, j, :], ACT.Copy, scale=SX).then_inc(S["k_hi"], 1)
                    if conv is not None and j == 0:
                        convert(ph + 1, conv, True)

                chunk_loop(act, kv)

            def q_body(c, j, conv):
                at = lambda lo, hi: stage_runs(c, lo, hi)
                if at(1, T + 1):
                    act.wait_ge(S["q_biased1"], c)
                    act.activation(qs[:], qb[:], ACT.Silu).then_inc(S["q_silu"], 1)
                    act.wait_ge(S["q_silu"], c)
                    act.activation(qb[:], qs[:], ACT.Square, bias=halfc[:]).then_inc(S["q_sq"], 1)
                if at(2, T + 2):
                    act.wait_ge(S["qT_ready"], c - 1)
                    if at(4, T + 2):
                        act.wait_ge(S["o_ready"], c - 3)
                    act.activation(qT_hi_t[:, j, :], banks(2, 2), ACT.Copy, scale=SX).then_inc(S["qT_hi"], 1)
                if conv is not None and j == 0:
                    convert(5, conv, False)
                if at(3, T + 3):
                    act.wait_ge(S["lnT_ready"], c - 2)
                    if at(4, T + 3):
                        act.wait_ge(S["lnT_lo"], c - 3)
                    for k in range(KC):
                        m = act.activation(lnf[:, k * P:(k + 1) * P], banks(6, 2)[:, k * P:(k + 1) * P], ACT.Identity,
                                           scale=colv[:, 2, k:k + 1], bias=colv[:, 3, k:k + 1])
                    m.then_inc(S["lnT_f"], 1)
                    act.wait_ge(S["lnT_f"], c - 2)
                    settle(act)
                    act.activation(ln_hi[:, :, ds(c * P - 3 * P, P)], lnf[:].rearrange("p (k n) -> p k n", n=P),
                                   ACT.Copy).then_inc(S["lnT_hi"], 1)

            q_loop(act, q_body)

            def wo_body(c, j, conv):
                if conv is not None and j == 0:
                    act.wait_ge(S["wo_ready"], c)
                    convert(6, conv, False)

            chunk_loop(act, wo_body)
            act.wait_ge(S["wo_ready"], T)

            def z_body(c, j, conv):
                for q in range(5):
                    g = 5 * c + q
                    if q == 3:
                        act.wait_ge(S["zp_ready"], c + 1)
                        settle(act)
                        act.activation(z_hi[:, ds(c, 1), :].rearrange("p a d -> p (a d)"), banks(6, 2), ACT.Copy,
                                       scale=1.0 / SW).then_inc(S["z_hi"], 1)
                    act.wait_ge(S["grp_ready"], g + 1)
                    if not (isinstance(c, int) and g == 0):
                        act.wait_ge(S["grp_added"], g)
                    act.activation(counts[:], banks(3 * ((5 * j + q) % 2), 3, N), ACT.Copy)\
                        .then_inc(S["grp_copied"], 1)
                    if q == 2 and conv is not None and j == 0:
                        convert(7, conv, False)

            chunk_loop(act, z_body)

            def s_chunk(u, i, j):
                o = 4 * u + 2 * i + j
                act.wait_ge(S["s_ready"], o + 1)
                if not (u == 0 and isinstance(i, int) and i == 0):
                    act.wait_ge(S[f"s_out{j}"], 16 * (2 * u + i))
                settle(act)
                act.activation(s0[:, j, :], banks(3 * j, 3, N), ACT.Identity, scale=1.0 / (SW * SX),
                               bias=colv[:, 0, ds(o, 1)]).then_inc(S["s_biased"], 1)
                if j == 1:
                    convert_at(2 * u + i)

            def convert_at(i):
                convert(8, i, False)

            for u in range(2):
                if u == 0:
                    s_chunk(0, 0, 0)
                    s_chunk(0, 0, 1)
                with act.Fori(1 - u, 2) as i:
                    s_chunk(u, i, 0)
                    s_chunk(u, i, 1)

            def h_chunk(o, j):
                act.wait_ge(S["a_sum"], o + 1)
                settle(act)
                act.activation(act_hi[:, ds(o, 1), 0:N].rearrange("p a n -> p (a n)"), s0[:, j, :], ACT.Relu)\
                    .then_inc(S["h_hi"], 1)

            with act.Fori(0, KC // 2) as i:
                h_chunk(2 * i, 0)
                h_chunk(2 * i + 1, 1)

            def z1_body(c, j, conv):
                act.wait_ge(S["zp_ready"], T + c + 1)
                settle(act)
                act.activation(z_hi[:, ds(c, 1), :].rearrange("p a d -> p (a d)"), banks(2 * j, 2), ACT.Copy,
                               scale=1.0 / SW).then_inc(S["z_hi"], 1)
                if conv is not None and j == 0:
                    convert(9, conv, False)

            chunk_loop(act, z1_body)

            def f_body(c, j, conv):
                if not (isinstance(c, int) and c == 0):
                    act.wait_ge(S["f_T"], c)
                    settle(act)
                    act.activation(act_hi[:, :, ds(c * P - P, P)],
                                   banks(4, 2).rearrange("p (k n) -> p k n", n=P), ACT.Copy, scale=SX)\
                        .then_inc(S["f_yhi"], 1)
                if conv is not None and j == 0:
                    convert(10, conv, False)

            chunk_loop(act, f_body)
            f_body(T, 0, None)

            act.wait_ge(S["r_step"], 1)
            act.activation(sel[:, 2, :], sel[:, 1, :], ACT.Exp).then_inc(S["r_exp"], 1)
            act.preload_act_table(ACT.Gelu)

            def turned(g, par, h, bank=0):
                act.wait_ge(S["x_T"], 2 * g + h + 1)
                settle(act)
                act.activation(xT_hi_t[:, par, :, h * P:(h + 1) * P], banks(bank, 2).rearrange("p (k n) -> p k n", n=P),
                               ACT.Copy, scale=SX).then_inc(S["xT_hi"], 1)

            def expert_group(g, par, last):
                if not last:
                    turned(g + 1, 1 - par, 0)
                e = act.value_load(expert_i[0:1, ds(g, 1)], min_val=0, max_val=EXPERTS - 1)
                for f in range(4):
                    n = 4 * g + f
                    act.wait_ge(S["g_ready"], n + 1)
                    if not (isinstance(g, int) and g == 0 and f < 2):
                        act.wait_ge(S["g_lo"], n - 1)
                    settle(act)
                    act.activation(g32[:, f % 2, :], ps[:, 2 + f % 2, 0:2 * P], ACT.Gelu, scale=1.0 / (SW * SX),
                                   bias=b1c[:, ds(4 * e + f, 1)]).then_inc(S["g_gelu"], 1)
                    act.wait_ge(S["g_gelu"], n + 1)
                    act.activation(gelu_hi[:, f, :], g32[:, f % 2, :], ACT.Copy, scale=SX).then_inc(S["g_hi"], 1)
                    if not last:
                        for j in range(2):
                            buf = (2 * f + j) % 4
                            act.wait_ge(S[f"stage_in{buf}"], 32 * g + 16 * (f // 2 + 1 + (4 * (DENSE + 1) if buf < 2 else 0)))
                            t = stage[:, buf, :] if buf < 2 else stage2[:, buf - 2, :]
                            act.activation(wslot[:, 8 * (1 - par) + 4 * j + f, 0, :], t, ACT.Copy, scale=SW)\
                                .then_inc(S["w_hi"], 1)
                if not last:
                    turned(g + 1, 1 - par, 1)

            turned(0, 0, 0)
            turned(0, 0, 1, bank=6)
            act.wait_ge(S["experts_made"], 1)
            group_loop(act, expert_group)

            def end_body(c, j, conv):
                act.wait_ge(S["e_nmr"], c + 1)
                if not (isinstance(c, int) and c < 2):
                    act.wait_ge(S[f"out{j}"], 16 * (conv + 1))
                settle(act)
                act.activation(fin[:, j, :], acc[:, ds(c, 1), :].rearrange("p a d -> p (a d)"), ACT.Identity,
                               scale=rstd[:, j:j + 1], bias=nmr[:, j:j + 1]).then_inc(S["e_n"], 1)

            chunk_loop(act, end_body)

        @block.vector
        def _(dve):
            steps = [0]

            def then(ins):
                steps[0] += 1
                ins.then_inc(S["rank_step"], 1)
                dve.wait_ge(S["rank_step"], steps[0])

            def diag_add(batch, i):
                for j in range(2):
                    dve.wait_ge(S[f"stage_in{j}"], 16 * (4 * batch + i + 1))
                    d = stage[:, j, ds(i * P, P)]
                    dve.tensor_tensor(d, d, ident[:], ALU.add).then_inc(S["diag_added"], 1)

            def convert(batch, i):
                for j in range(2):
                    dve.wait_ge(S["w_hi"], 8 * batch + 2 * i + j + 1)
                    slot = 8 * (batch % 2) + 4 * j
                    at = lambda part: wslot[:, ds(slot + i, 1), part, :].rearrange("p a d -> p (a d)")
                    dve.scalar_tensor_tensor(at(1), stage[:, j, :], SW, at(0), ALU.mult, ALU.subtract)\
                        .then_inc(S["w_lo"], 1)

            then(dve.memset(mask[:], 0.0))
            dve.memset(mask[0:HD, :, 0:HD], SS)
            then(dve.memset(mask[HD:P, :, HD:P], SS))
            dve.wait_ge(S["edge_in"], 32)
            src_f, dst_f, rowf, tmp, loc = (es[:, n, :] for n in range(5))
            then(dve.tensor_copy(es[:, 0:2, :], e_i[:]))
            for b in range(T + 1):
                m = dve.tensor_scalar(ge[:, b, :], src_f, float(P * b), None, ALU.is_ge)
            then(m)
            dve.memset(tmp, 1.0)
            then(dve.tensor_tensor(member[:], ge[:, 0:T, :], ge[:, 1:T + 1, :], ALU.subtract))
            for b in range(T):
                m = dve.tensor_tensor_scan(cum[:, b, :], tmp, member[:, b, :], 0.0, ALU.mult, ALU.add)
            then(m)
            dve.tensor_copy(e_small[:, 0, 0:T], cum[:, :, EJ - 1]).then_inc(S["edge_tot"], 1)

            before, size, ends, offs = (e_small[:, n, 0:T] for n in (1, 2, 3, 4))
            dve.wait_ge(S["totals_made"], 1)
            then(dve.tensor_copy(before, ps[:, 7, 0:T]))
            then(dve.tensor_scalar(size, ps[:, 7, 16:16 + T], float(TG * P - 1), None, ALU.add))

            dve.wait_ge(S["prep_step"], 4)
            dve.scalar_tensor_tensor(rw16[:, :, 1, :], rw32[:], SW, rw16[:, :, 0, :], ALU.mult, ALU.subtract)\
                .then_inc(S["rw_lo"], 1)

            def norm_tile(src, dst, count, stat, var, rstd_sem, eps, done, meanwhile=None):
                settle(dve)
                for hh in range(2):
                    m = dve.bn_stats(stats[:, 0, 6 * hh:6 * hh + 6], src[:, hh * 512:(hh + 1) * 512])
                m.then_inc(S[stat], 1)
                dve.wait_ge(S[stat], 2 * count + 1)
                settle(dve)
                dve.bn_aggr(mv[:, 0, :], stats[:, 0, :]).then_inc(S[stat], 1)
                dve.wait_ge(S[stat], 2 * count + 2)
                dve.tensor_scalar(mv[:, 0, 1:2], mv[:, 0, 1:2], eps, None, ALU.add).then_inc(S[var], 1)
                if meanwhile:
                    meanwhile()
                dve.wait_ge(S[rstd_sem], count + 1)
                return dve.tensor_scalar(dst, src, mv[:, 0, 0:1], rstd[:, 0:1], ALU.subtract, ALU.mult)\
                    .then_inc(S[done], 1)

            def ln0_lo(c, j):
                dve.wait_ge(S["ln0_hi"], c + 1)
                dve.scalar_tensor_tensor(act_lo[:, :, ds(c * P, P)], banks(4 + 2 * j, 2).rearrange("p (k n) -> p k n", n=P),
                                         SX, act_hi[:, :, ds(c * P, P)], ALU.mult, ALU.subtract)\
                    .then_inc(S["ln0_lo"], 1)

            def ln0(c, j, conv):
                i = c // 2 if isinstance(c, int) else conv + 1
                dve.wait_ge(S[f"x_in{j}"], 16 * (i + 1))
                if not (isinstance(c, int) and c < 2):
                    dve.wait_ge(S["ln0_T"], c - 1)
                norm_tile(xin0[:, j, :], xn0[:, j, :], c, "ln0_stat", "ln0_var", "ln0_rstd", 1e-5, "ln0_done",
                          (lambda: diag_add(0, conv)) if conv is not None and j == 1 else None)
                if not (isinstance(c, int) and c == 0):
                    ln0_lo(c - 1, 1 - j)
                if conv is not None and j == 1:
                    convert(0, conv)

            chunk_loop(dve, ln0)
            ln0_lo(T - 1, 1)

            def edge_positions():
                dve.wait_ge(S["const_made"], 10)
                dve.tensor_copy(iota_d[:], iota_i[:])
                dve.tensor_copy(giota[:], giota_i[:])
                then(dve.tensor_copy(ei_small[:, 0:T], size))
                then(dve.tensor_scalar(ei_small[:, 0:T], ei_small[:, 0:T], 9, 9, ALU.arith_shift_right,
                                       ALU.logical_shift_left))
                then(dve.tensor_copy(size, ei_small[:, 0:T]))
                then(dve.tensor_tensor_scan(ends, tmp[:, 0:T], size, 0.0, ALU.mult, ALU.add))
                then(dve.tensor_tensor(offs, ends, size, ALU.subtract))
                then(dve.scalar_tensor_tensor(offs, before, -1.0, offs, ALU.add, ALU.add))
                for b in range(T):
                    m = dve.scalar_tensor_tensor(posb[:, b, :], cum[:, b, :], offs[:, b:b + 1], member[:, b, :],
                                                 ALU.add, ALU.mult)
                then(m)
                then(dve.tensor_reduce(rowf, posb[:].rearrange("p b j -> p j b"), AX.X, ALU.add))

            def edge_rows():
                pi = e_i[:, 0, :]
                part = e_i[:, 1, :]
                then(dve.tensor_copy(pi, rowf))
                then(dve.tensor_scalar(part, pi, TG * P - 1, 2, ALU.bitwise_and, ALU.arith_shift_right))
                then(dve.tensor_copy(tmp, part))
                then(dve.tensor_scalar(part, pi, 9, 2, ALU.arith_shift_right, ALU.logical_shift_left))
                then(dve.tensor_copy(loc, part))
                then(dve.scalar_tensor_tensor(rowf, tmp, float(SPP), loc, ALU.mult, ALU.add))
                then(dve.tensor_scalar(part, pi, TG - 1, None, ALU.bitwise_and))
                then(dve.tensor_copy(tmp, part))
                then(dve.tensor_tensor(rowf, rowf, tmp, ALU.add))
                then(dve.tensor_copy(tmp, pid_i[:]))
                then(dve.tensor_tensor(rowf, rowf, tmp, ALU.subtract))
                then(dve.tensor_tensor(rowf, rowf, ge[:, 0, :], ALU.mult))
                then(dve.tensor_tensor(rowf, rowf, tmp, ALU.add))
                dve.tensor_copy(idx[:], rowf).then_inc(S["edge_placed"], 1)
                then(dve.tensor_reduce(loc, ge[:, 1:T, :].rearrange("p b j -> p j b"), AX.X, ALU.add))
                dve.tensor_copy(pay[:, :, 1], dst_f)
                dve.scalar_tensor_tensor(pay[:, :, 0], loc, -float(P), src_f, ALU.mult, ALU.add)\
                    .then_inc(S["edge_placed"], 1)

            dve.wait_ge(S["prep_step"], 5)

            def blocks_of_groups():
                then(dve.memset(block_f[:], 0.0))
                for b in range(T - 1):
                    then(dve.scalar_tensor_tensor(block_f[:], giota[:], ends[:, b:b + 1], block_f[:], ALU.is_ge, ALU.add))
                then(dve.tensor_copy(block_i[:], block_f[:]))

            def take_state(ph):
                kk, h = ph // 2, ph % 2
                dve.wait_ge(S["state_mm"], T * (ph + 1))
                sb = ps[:, 4 + ph % 2, :]
                sc = 1.0 / (SX * SX * N)
                if kk == 0:
                    dve.tensor_scalar(st0[:, h, :], sb, sc, None, ALU.mult).then_inc(S["state_first"], 1)
                else:
                    dve.scalar_tensor_tensor(stp[:], sb, sc, st0[:, h, :], ALU.mult, ALU.mult)\
                        .then_inc(S["state_step"], 1)
                    dve.wait_ge(S["state_step"], 3 * h + 1)
                    dve.tensor_tensor(stp[:], stp[:], mask[:].rearrange("p a b -> p (a b)"), ALU.mult)\
                        .then_inc(S["state_step"], 1)
                    dve.wait_ge(S["state_step"], 3 * h + 2)
                    dve.tensor_copy(st_hi[:, h, :], stp[:]).then_inc(S["state_step"], 1)
                    dve.wait_ge(S["state_step"], 3 * h + 3)
                    dve.tensor_tensor(st_lo[:, h, :], stp[:], st_hi[:, h, :], ALU.subtract)\
                        .then_inc(S["state_lo"], 1)

            for ph in range(4):
                kk, h = ph // 2, ph % 2

                def kv(c, j, conv, ph=ph, kk=kk, h=h):
                    g = T * ph + c
                    dve.wait_ge(S["kv_ready"], g + 1)
                    dve.scalar_tensor_tensor(kb[:, j, :], ps[:, 2 * j, :], 1.0 / (SW * SX),
                                             bk_bc[:, kk, h * 512:(h + 1) * 512], ALU.mult, ALU.add)\
                        .then_inc(S["k_biased"], 1)
                    dve.scalar_tensor_tensor(v16[:, j, :], ps[:, 2 * j + 1, :], 1.0 / SW,
                                             bv_bc[:, kk, h * 512:(h + 1) * 512], ALU.mult, ALU.add)\
                        .then_inc(S["v_scaled"], 1)
                    if isinstance(c, int) and c == 1 and ph > 0:
                        take_state(ph - 1)
                    if isinstance(c, int) and c == 0 and ph == 1:
                        blocks_of_groups()
                    if isinstance(c, int) and c == 0 and ph == 2:
                        dve.wait_ge(S["bsum_in"], 32)
                        then(dve.tensor_tensor(bsum[:], bsum[:], bo_bc[:], ALU.add))
                    if conv is not None and j == 0:
                        diag_add(ph + 1, conv)
                    dve.wait_ge(S["k_sq"], g + 1)
                    dve.tensor_reduce(ssq[:, 0, 0:8], ksq[:, j, :].rearrange("p (a b) -> p a b", b=HD), AX.X, ALU.add)\
                        .then_inc(S["k_ssq"], 1)
                    dve.wait_ge(S["v_hi"], g + 1)
                    dve.tensor_tensor(v_lo_t[:, j, :], v16[:, j, :], v_hi_t[:, j, :], ALU.subtract)\
                        .then_inc(S["v_lo"], 1)
                    dve.wait_ge(S["k_nrm"], g + 1)
                    dve.tensor_scalar(nrm[:, 0, 0:8], nrm[:, 0, 0:8], 1e-6, None, ALU.add).then_inc(S["k_inv"], 1)
                    dve.wait_ge(S["k_inv"], 2 * (g) + 1)
                    dve.reciprocal(nrm[:, 0, 0:8], nrm[:, 0, 0:8]).then_inc(S["k_inv"], 1)
                    dve.wait_ge(S["k_inv"], 2 * g + 2)
                    dve.scalar_tensor_tensor(kb[:, j, :].rearrange("p (a b) -> p a b", b=HD),
                                             ks[:, j, :].rearrange("p (a b) -> p a b", b=HD), 0.5,
                                             nrm[:, 0, 0:8].unsqueeze(2).broadcast_to([P, 8, HD]),
                                             ALU.add, ALU.mult).then_inc(S["k_normed"], 1)
                    dve.wait_ge(S["k_hi"], g + 1)
                    dve.scalar_tensor_tensor(k_lo_t[:, j, :], kb[:, j, :], SX, k_hi_t[:, j, :], ALU.mult,
                                             ALU.subtract).then_inc(S["k_lo"], 1)
                    if ph == 0 and isinstance(c, int) and c < 2:
                        (edge_positions if c == 0 else edge_rows)()
                    if conv is not None and j == 0:
                        convert(ph + 1, conv)

                chunk_loop(dve, kv)
            def q_body(c, j, conv):
                at = lambda lo, hi: stage_runs(c, lo, hi)

                def evac(hh):
                    dve.wait_ge(S[f"q_ready{hh}"], c + 1)
                    dve.scalar_tensor_tensor(qb[:, hh * 512:(hh + 1) * 512], ps[:, hh, :], 1.0 / (SW * SX),
                                             bq_bc[:, hh * 512:(hh + 1) * 512], ALU.mult, ALU.add)\
                        .then_inc(S[f"q_biased{hh}"], 1)
                if at(1, T + 1):
                    dve.wait_ge(S["q_sq"], c)
                    dve.tensor_reduce(ssq[:, 1, :], qb[:].rearrange("p (a b) -> p a b", b=HD), AX.X, ALU.add)\
                        .then_inc(S["q_ssq"], 1)
                if at(2, T + 2):
                    dve.wait_ge(S["qT_hi"], c - 1)
                    dve.scalar_tensor_tensor(qT_lo_t[:, j, :], banks(2, 2), SX, qT_hi_t[:, j, :], ALU.mult,
                                             ALU.subtract).then_inc(S["qT_lo"], 1)
                if conv is not None and j == 0:
                    convert(5, conv)
                if at(0, T):
                    if at(1, T):
                        dve.wait_ge(S["q_ssq"], c)
                    evac(0)
                if at(1, T + 1):
                    dve.wait_ge(S["q_nrm"], c)
                    dve.tensor_scalar(nrm[:, 1, :], nrm[:, 1, :], 1e-6, None, ALU.add).then_inc(S["q_inv"], 1)
                    dve.wait_ge(S["q_inv"], 2 * c - 1)
                    dve.reciprocal(nrm[:, 1, :], nrm[:, 1, :]).then_inc(S["q_inv"], 1)
                    dve.wait_ge(S["q_inv"], 2 * c)
                    dve.scalar_tensor_tensor(qn[:, 1 - j, :].rearrange("p (a b) -> p a b", b=HD),
                                             qs[:].rearrange("p (a b) -> p a b", b=HD), 0.5,
                                             nrm[:, 1, :].unsqueeze(2).broadcast_to([P, HEADS, HD]),
                                             ALU.add, ALU.mult).then_inc(S["q_normed"], 1)
                if at(2, T + 2):
                    dve.wait_ge(S["o_ready"], c - 1)
                    if at(3, T + 2):
                        dve.wait_ge(S["lnT_ready"], c - 2)
                    norm_tile(banks(4, 2), lnx[:], c - 2, "o_stat", "o_var", "o_rstd", 1e-5 * (SX * SS) ** 2, "o_normed")
                if at(3, T + 3):
                    dve.wait_ge(S["lnT_hi"], c - 2)
                    dve.tensor_tensor(ln_lo[:, :, ds(c * P - 3 * P, P)], lnf[:].rearrange("p (k n) -> p k n", n=P),
                                      ln_hi[:, :, ds(c * P - 3 * P, P)], ALU.subtract).then_inc(S["lnT_lo"], 1)
                if at(0, T):
                    evac(1)
                if at(0, 1):
                    take_state(3)

            q_loop(dve, q_body)


            def wo_body(c, j, conv):
                i = c // 2 if isinstance(c, int) else conv + 1
                dve.wait_ge(S["wo_ready"], c + 1)
                if not (isinstance(c, int) and c < 2):
                    dve.wait_ge(S[f"res_out{j}"], 16 * i)
                dve.scalar_tensor_tensor(mo[:, j, :], banks(2 * c if isinstance(c, int) else 2 * j, 2),
                                         1.0 / (SW * SX), bsum[:], ALU.mult,
                                         ALU.add).then_inc(S["wo_biased"], 1)
                dve.wait_ge(S["wo_biased"], c + 1)
                dve.wait_ge(S[f"xin_in{j}"], 16 * (i + 1))
                dve.tensor_tensor(mo[:, j, :], mo[:, j, :], xin[:, j, :], ALU.add).then_inc(S["wo_x"], 1)
                if conv is not None and j == 0:
                    convert(6, conv)

            for c in range(4):
                wo_body(c, c % 2, None if c < 2 else 0)
            with dve.Fori(2, T // 2) as i:
                wo_body(2 * i, 0, i - 1)
                wo_body(2 * i + 1, 1, i - 1)

            dve.wait_ge(S["table_in"], 16)
            dve.wait_ge(S["zeros_made"], 5)
            for j in range(2):
                dve.wait_ge(S[f"res_out{j}"], 16 * T // 2)

            def one_hots(g, par, first):
                if not first:
                    dve.wait_ge(S["grp_ready"], g - 1)
                for t in range(TG):
                    col = TG * g + t
                    dve.tensor_scalar(src_1h[:, par, t, :], iota_d[:, 0:P],
                                      edges[:, ds(col, 1), 0], None, ALU.is_equal)
                    m = dve.tensor_scalar(dst_1h[:, par, t, :], iota_d[:],
                                          edges[:, ds(col, 1), 1], None, ALU.is_equal)
                m.then_inc(S["onehot"], 1)

            def add_group(g):
                dve.wait_ge(S["grp_copied"], g + 1)
                if not (isinstance(g, int) and g == 0):
                    dve.wait_ge(S["grp_added"], g)
                blk = dve.value_load(block_i[0:1, ds(g, 1)], min_val=0, max_val=T - 1)
                row = adj[:, ds(blk, 1), 0:N].rearrange("p a n -> p (a n)")
                dve.tensor_tensor(row, counts[:], row, ALU.add).then_inc(S["grp_added"], 1)

            def z_low(c):
                dve.wait_ge(S["z_hi"], c + 1)
                at = lambda t: t[:, ds(c, 1), :].rearrange("p a d -> p (a d)")
                dve.scalar_tensor_tensor(at(z_lo), banks(6, 2), 1.0 / SW, at(z_hi), ALU.mult, ALU.subtract)\
                    .then_inc(S["z_lo"], 1)

            def z_body(c, j, conv):
                for q in range(5):
                    g = 5 * c + q
                    par = (5 * j + q) % 2
                    one_hots(g, par, isinstance(c, int) and g < 2)
                    if q == 4:
                        z_low(c)
                    if not (isinstance(c, int) and g < 2):
                        add_group(g - 2)
                if conv is not None and j == 0:
                    convert(7, conv)

            chunk_loop(dve, z_body)
            add_group(GROUPS - 2)
            add_group(GROUPS - 1)
            dve.wait_ge(S["deg_ready"], 1)
            dve.tensor_scalar(dinv[:], banks(5, 3, NP), 1.0, None, ALU.max).then_inc(S["dinv_made"], 1)
            dve.wait_ge(S["dinv_made"], 1)
            dve.reciprocal(dinv[:], dinv[:]).then_inc(S["dinv_made"], 1)
            dve.wait_ge(S["dcol_ready"], 1)
            dve.tensor_scalar(dinv_col[:], ps[:, 7, 0:T], 1.0 / SX, None, ALU.mult).then_inc(S["dcol_made"], 1)

            with dve.Fori(0, 4) as i:
                convert(8, i)
            dve.wait_ge(S["dinv_made"], 2)

            def h_chunk(o, i, j):
                dve.wait_ge(S["a_ready"], o + 1)
                dve.tensor_tensor(tg[:], banks(3 * j, 3, N), dinv[:, 0:N], ALU.mult).then_inc(S["a_scaled"], 1)
                dve.wait_ge(S["a_scaled"], o + 1)
                dve.wait_ge(S[f"s_in{j}"], 16 * (i + 1))
                dve.scalar_tensor_tensor(s0[:, j, :], s0[:, j, :], SX, tg[:], ALU.mult, ALU.add)\
                    .then_inc(S["a_sum"], 1)
                dve.wait_ge(S["h_hi"], o + 1)
                at = lambda t: t[:, ds(o, 1), 0:N].rearrange("p a n -> p (a n)")
                dve.scalar_tensor_tensor(at(act_lo), s0[:, j, :], 0.0, at(act_hi), ALU.max, ALU.subtract)\
                    .then_inc(S["h_lo"], 1)

            with dve.Fori(0, KC // 2) as i:
                h_chunk(2 * i, i, 0)
                h_chunk(2 * i + 1, i, 1)

            def z1_body(c, j, conv):
                dve.wait_ge(S["z_hi"], T + c + 1)
                at = lambda t: t[:, ds(c, 1), :].rearrange("p a d -> p (a d)")
                dve.scalar_tensor_tensor(at(z_lo), banks(2 * j, 2), 1.0 / SW, at(z_hi), ALU.mult, ALU.subtract)\
                    .then_inc(S["z_lo"], 1)
                if conv is not None and j == 0:
                    convert(9, conv)

            chunk_loop(dve, z1_body)

            def f_body(c, j, conv):
                i = c // 2 if isinstance(c, int) else conv + 1
                done = isinstance(c, int) and c >= T
                if not done:
                    dve.wait_ge(S["f_s"], c + 1)
                    dve.wait_ge(S[f"res_in{j}"], 16 * (i + 1))
                    if not (isinstance(c, int) and c < 2):
                        dve.wait_ge(S[f"res_out{j}"], 16 * (T // 2 + i))
                    dve.scalar_tensor_tensor(x1[:, j, :], banks(0, 2), 1.0 / (SW * SX), xm[:, j, :], ALU.mult,
                                             ALU.add).then_inc(S["f_x1a"], 1)
                if not (isinstance(c, int) and c == 0):
                    dve.wait_ge(S["f_yhi"], c)
                    dve.scalar_tensor_tensor(act_lo[:, :, ds(c * P - P, P)],
                                             banks(4, 2).rearrange("p (k n) -> p k n", n=P), SX,
                                             act_hi[:, :, ds(c * P - P, P)], ALU.mult, ALU.subtract)\
                        .then_inc(S["f_ylo"], 1)
                if not done:
                    dve.wait_ge(S["f_g"], c + 1)
                    dve.wait_ge(S["f_x1a"], c + 1)
                    dve.scalar_tensor_tensor(x1[:, j, :], banks(2, 2), dinv_col[:, ds(c, 1)], x1[:, j, :], ALU.mult,
                                             ALU.add).then_inc(S["f_x1"], 1)
                    dve.wait_ge(S["f_x1"], c + 1)
                    if not (isinstance(c, int) and c < 2):
                        dve.wait_ge(S[f"rows_out{j}"], 16 * i)
                    norm_tile(x1[:, j, :], yb[:, j, :], c, "f_stat", "f_var", "f_rstd", 1e-5, "f_y")
                if conv is not None and j == 0:
                    convert(10, conv)

            chunk_loop(dve, f_body)
            f_body(T, 0, None)

            dve.wait_ge(S["r_const"], 6)
            dve.tensor_copy(iota_m[:], iota_m[:].bitcast(I32))
            dve.tensor_copy(node_f[:], node_f[:].bitcast(I32))
            dve.tensor_copy(count_down[:], count_down[:].bitcast(I32))
            dve.tensor_copy(mgroup[:, 0, :], mgroup[:, 0, :].bitcast(I32))
            dve.memset(reset[:], 1.0)
            then(dve.memset(mgroup[:, 1, :], 0.0))
            then(dve.memset(reset[:, :, 0], 0.0))
            then(dve.tensor_scalar(mpos[:, 2, 0, :], node_f[:], float(N), None, ALU.is_lt))
            then(dve.tensor_tensor(node_f[:], node_f[:], mpos[:, 2, 0, :], ALU.mult))
            dve.wait_ge(S["f_lg"], T)
            L, one1, one2, rest, tmp8 = (lg[:, n] for n in range(5))
            v1, dv, ex, v2, w1v, w2v = (sel[:, n, :] for n in range(6))
            bc = lambda a: a.unsqueeze(2).broadcast_to([P, T, EXPERTS])

            def first_largest(src, best, onehot):
                then(dve.tensor_reduce(best, src, AX.X, ALU.max))
                then(dve.tensor_tensor(tmp8, src, bc(best), ALU.is_equal))
                then(dve.tensor_tensor(tmp8, tmp8, count_down[:].unsqueeze(1).broadcast_to([P, T, EXPERTS]), ALU.mult))
                then(dve.tensor_reduce(w1v, tmp8, AX.X, ALU.max))
                then(dve.tensor_tensor(onehot, tmp8, bc(w1v), ALU.is_equal))

            then(dve.scalar_tensor_tensor(L, ps[:, 6, 0:T * EXPERTS].rearrange("p (t e) -> p t e", e=EXPERTS),
                                          1.0 / (SW * SX), rb[:].unsqueeze(1).broadcast_to([P, T, EXPERTS]),
                                          ALU.mult, ALU.add))
            first_largest(L, v1, one1)
            then(dve.scalar_tensor_tensor(rest, one1, -1e30, L, ALU.mult, ALU.add))
            first_largest(rest, v2, one2)
            dve.tensor_tensor(dv, v2, v1, ALU.subtract).then_inc(S["r_step"], 1)

            member_e, cum_e, at_e, picked = (mrank[:, n] for n in range(4))
            te = lambda a: a.rearrange("p t e -> p e t")
            then(dve.tensor_tensor(member_e, te(one1), te(one2), ALU.add))
            then(dve.tensor_tensor(member_e, member_e, mpos[:, 2, 0, :].unsqueeze(1).broadcast_to([P, EXPERTS, T]),
                                   ALU.mult))
            flat = lambda a: a.rearrange("p e t -> p (e t)")
            then(dve.tensor_tensor_scan(flat(cum_e), flat(reset[:]), flat(member_e), 0.0, ALU.mult, ALU.add))
            dve.tensor_copy(msmall[:, 0, :], cum_e[:, :, T - 1]).then_inc(S["r_tot"], 1)
            dve.wait_ge(S["r_before"], 1)
            size, ends, offs = (msmall[:, n, :] for n in (1, 2, 3))
            then(dve.tensor_scalar(size, ps[:, 7, 16:16 + EXPERTS], 1.0, float(2 * P - 1), ALU.max, ALU.add))
            then(dve.tensor_copy(msmall_i[:], size))
            then(dve.tensor_scalar(msmall_i[:], msmall_i[:], 8, 8, ALU.arith_shift_right, ALU.logical_shift_left))
            then(dve.tensor_copy(size, msmall_i[:]))
            then(dve.tensor_tensor_scan(ends, ones2[:, 0:EXPERTS], size, 0.0, ALU.mult, ALU.add))
            then(dve.tensor_tensor(offs, ends, size, ALU.subtract))
            then(dve.scalar_tensor_tensor(offs, ps[:, 7, 0:EXPERTS], -1.0, offs, ALU.add, ALU.add))
            then(dve.tensor_tensor(at_e, cum_e, offs.unsqueeze(2).broadcast_to([P, EXPERTS, T]), ALU.add))
            for k, one in enumerate((one1, one2)):
                then(dve.tensor_tensor(te(picked), one, te(at_e), ALU.mult))
                then(dve.tensor_reduce(mpos[:, 0, k, :], te(picked), AX.X, ALU.add))
                then(dve.tensor_tensor(mpos[:, 0, k, :], mpos[:, 0, k, :], mpos[:, 2, 0, :], ALU.mult))
            then(dve.tensor_copy(slot_i[:], mpos[:, 0]))
            dve.tensor_scalar(mpos_i[:, 0], slot_i[:], P - 1, None, ALU.bitwise_and)
            then(dve.tensor_scalar(mpos_i[:, 1], slot_i[:], 7, None, ALU.arith_shift_right))
            then(dve.tensor_copy(mpos[:, 0:2], mpos_i[:]))
            same = lambda out, at, n: dve.tensor_tensor(
                out.rearrange("p k t n -> p (k t) n"), iota_m[:, 0:n].unsqueeze(1).broadcast_to([P, TOP * T, n]),
                at.rearrange("p k t -> p (k t)").unsqueeze(2).broadcast_to([P, TOP * T, n]), ALU.is_equal)
            then(same(tile_1h[:], mpos[:, 1], MOE_TILES))
            for k in range(TOP):
                dve.tensor_tensor(tile_1h[:, k], tile_1h[:, k], node_f[:].unsqueeze(2).broadcast_to([P, T, MOE_TILES]),
                                  ALU.mult)
            same(row_1h[:], mpos[:, 0], P).then_inc(S["r_1h"], 1)
            dve.wait_ge(S["nodes_ready"], 1)
            dve.tensor_copy(node_i[:], ps[:, 6, 0:MOE_TILES]).then_inc(S["nodes_made"], 1)
            for e in range(EXPERTS - 1):
                then(dve.scalar_tensor_tensor(mgroup[:, 1, :], mgroup[:, 0, :], ends[:, e:e + 1], mgroup[:, 1, :],
                                              ALU.is_ge, ALU.add))
            dve.tensor_copy(expert_i[:], mgroup[:, 1, :]).then_inc(S["experts_made"], 1)
            dve.wait_ge(S["r_exp"], 1)
            then(dve.tensor_scalar(w2v, ex, 1.0, None, ALU.add))
            then(dve.reciprocal(cw[:, 0, :], w2v))
            then(dve.tensor_tensor(cw[:, 1, :], ex, cw[:, 0, :], ALU.mult))

            def turned(g, par, h, bank=0):
                dve.wait_ge(S["xT_hi"], 2 * g + h + 1)
                dve.scalar_tensor_tensor(xT_lo_t[:, par, :, h * P:(h + 1) * P],
                                         banks(bank, 2).rearrange("p (k n) -> p k n", n=P), SX,
                                         xT_hi_t[:, par, :, h * P:(h + 1) * P], ALU.mult, ALU.subtract)\
                    .then_inc(S["xT_lo"], 1)

            def expert_group(g, par, last):
                if not last:
                    turned(g + 1, 1 - par, 0)
                for f in range(4):
                    dve.wait_ge(S["g_hi"], 4 * g + f + 1)
                    dve.scalar_tensor_tensor(gelu_lo[:, f, :], g32[:, f % 2, :], SX, gelu_hi[:, f, :], ALU.mult,
                                             ALU.subtract).then_inc(S["g_lo"], 1)
                    if not last:
                        for j in range(2):
                            buf = (2 * f + j) % 4
                            t = stage[:, buf, :] if buf < 2 else stage2[:, buf - 2, :]
                            dve.wait_ge(S["w_hi"], 8 * g + 8 * (DENSE + 1) + 2 * f + j + 1)
                            at = lambda part: wslot[:, 8 * (1 - par) + 4 * j + f, part, :]
                            dve.scalar_tensor_tensor(at(1), t, SW, at(0), ALU.mult, ALU.subtract)\
                                .then_inc(S["w_lo"], 1)
                if not last:
                    turned(g + 1, 1 - par, 1)
                dve.wait_ge(S[f"b2_in{par}"], 16 * trips(g) + 16)
                if not (isinstance(g, int) and g < 2):
                    dve.wait_ge(S[f"yo_out{par}"], 32 * trips(g))
                for b in range(4):
                    h, hh = b // 2, b % 2
                    dve.wait_ge(S["y_ready"], 4 * g + b + 1)
                    dve.scalar_tensor_tensor(yo[:, par, h, hh * 512:(hh + 1) * 512], ps[:, 4 + b, :], 1.0 / (SW * SX),
                                             b2_bc[:, par, hh * 512:(hh + 1) * 512], ALU.mult, ALU.add)\
                        .then_inc(S["y_evac"], 1)

            turned(0, 0, 0)
            turned(0, 0, 1, bank=6)
            group_loop(dve, expert_group)

            dve.wait_ge(S["acc_in"], 16)
            dve.wait_ge(S["x1_in"], 16)

            def finish(c, j):
                dve.wait_ge(S["e_w"], c + 1)
                dve.tensor_tensor(fin[:, j, :], fin[:, j, :], x1in[:, ds(c, 1), :].rearrange("p a d -> p (a d)"),
                                  ALU.add).then_inc(S["e_x"], 1)

            def end_body(c, j, conv):
                i = c // 2 if isinstance(c, int) else conv + 1
                a = acc[:, ds(c, 1), :].rearrange("p a d -> p (a d)")
                for k in range(TOP):
                    dve.wait_ge(S[f"xg_in{j}{k}"], 16 * i + 16 * (MOE_GROUPS // 2 + 2 - j))
                for k in range(TOP):
                    if k == 1:
                        dve.wait_ge(S["e_sum"], 2 * c + 1)
                    dve.scalar_tensor_tensor(a, yg[:, j, k, :], cw[:, k, ds(c, 1)], a, ALU.mult, ALU.add)\
                        .then_inc(S["e_sum"], 1)
                dve.wait_ge(S["e_sum"], 2 * c + 2)
                settle(dve)
                for hh in range(2):
                    m = dve.bn_stats(stats[:, j, 6 * hh:6 * hh + 6], a[:, hh * 512:(hh + 1) * 512])
                m.then_inc(S["f_stat"], 1)
                dve.wait_ge(S["f_stat"], 2 * T + 2 * c + 1)
                settle(dve)
                dve.bn_aggr(mv[:, j, :], stats[:, j, :]).then_inc(S["f_stat"], 1)
                dve.wait_ge(S["f_stat"], 2 * T + 2 * c + 2)
                dve.tensor_scalar(mv[:, j, 1:2], mv[:, j, 1:2], 1e-12, None, ALU.add).then_inc(S["f_var"], 1)
                if not (isinstance(c, int) and c == 0):
                    finish(c - 1, 1 - j)
                dve.wait_ge(S["f_rstd"], T + c + 1)
                dve.tensor_scalar(nmr[:, j:j + 1], mv[:, j, 0:1], rstd[:, j:j + 1], -1.0, ALU.mult, ALU.mult)\
                    .then_inc(S["e_nmr"], 1)

            chunk_loop(dve, end_body)
            finish(T - 1, 1)


def trips(g):
    return g // 2


def unit(w, order):
    import numpy as np
    v = w.reshape(KC, P, 512)[order].reshape(4, 2, P, 512)
    return np.ascontiguousarray(v.transpose(0, 2, 1, 3)).reshape(4, P, D)


def kernel(**inputs):
    import numpy as np
    import concourse.bacc as bacc
    from concourse import mybir as mb
    from concourse.bass_utils import run_bass_kernel_spmd

    g = {k.replace("L0_", ""): np.asarray(v) for k, v in inputs.items()}
    x = np.zeros((NP, D), np.float32)
    x[:N] = g["x"]

    def edge_grid(e):
        v = np.full(EJ * P, -1, np.int32)
        v[:E] = e
        return np.ascontiguousarray(v.reshape(EJ, P).T)

    units = []
    for kk in range(2):
        for h in range(2):
            for name in ("mix_Wk", "mix_Wv"):
                units.append(unit(g[name][kk].T[:, h * 512:(h + 1) * 512], DIAG[h]))
    for w, orders in ((g["mix_Wq"].T, DIAG), (g["mix_Wo"].T, (PLAIN, PLAIN)), (g["gnn_W_neigh0"], (PLAIN, PLAIN)),
                      (g["gnn_W_self0"], (PLAIN, PLAIN)), (g["gnn_W_neigh1"], (PLAIN, PLAIN)),
                      (g["gnn_W_self1"], (PLAIN, PLAIN))):
        for h in range(2):
            units.append(unit(w[:, h * 512:(h + 1) * 512], orders[h]))
    for e in range(EXPERTS):
        units.append(unit(g["ffn_w1"][e].T, PLAIN))
        units.append(np.ascontiguousarray(g["ffn_w2"][e].T).reshape(4, P, D))

    def columns(v):
        return v.reshape(-1, P).T

    arrays = {
        "x": x, "edge_src": edge_grid(g["src"]), "edge_dst": edge_grid(g["dst"]),
        "weights": np.concatenate(units),
        "rows": np.stack([g["mix_bq"], g["mix_bk"][0], g["mix_bk"][1], g["mix_bv"][0], g["mix_bv"][1], g["gnn_b1"],
                          g["mix_bo"], g["ffn_ln_w"], g["ffn_ln_b"]]),
        "cols": np.stack([columns(g["gnn_b0"]), columns(g["mix_ln_g"]), columns(g["mix_ln_b"])], axis=1),
        "b1col": columns(g["ffn_b1"]),
        "router": g["ffn_router_w"].T.reshape(KC, P, EXPERTS).transpose(1, 0, 2),
        "router_b": g["ffn_router_b"], "b2": g["ffn_b2"],
    }
    arrays = {k: np.ascontiguousarray(v) for k, v in arrays.items()}
    nc = bacc.Bacc("TRN2", target_bir_lowering=False, num_devices=1)
    aps = [nc.dram_tensor("in_" + k, v.shape, mb.dt.from_np(v.dtype), kind="ExternalInput").ap()
           for k, v in arrays.items()]
    aps.append(nc.dram_tensor("out_y", (NP, D), mb.dt.float32, kind="ExternalOutput").ap())
    program(nc, *aps)
    r = run_bass_kernel_spmd(nc, [{"in_" + k: v for k, v in arrays.items()}], core_ids=[0])
    return r.results[0]["out_y"][:N]
```
